# Optimizing a Trainium2 kernel written in Bass

```python
import numpy as np
import jax
import jax.numpy as jnp

def _softmax(x, axis=-1):
    return jax.nn.softmax(x, axis=axis)

def _gelu(x):
    return jax.nn.gelu(x, approximate=True)

def _silu(x):
    return jax.nn.silu(x)

def _sigmoid(x):
    return jax.nn.sigmoid(x)

def _layernorm(x, axis=-1, eps=1e-05):
    m = jnp.mean(x, axis=axis, keepdims=True)
    v = jnp.var(x, axis=axis, keepdims=True)
    return (x - m) / jnp.sqrt(v + eps)

def _scatter_add(tgt, idx, src, axis=0):
    return tgt.at[idx].add(src)

def _segment_sum(src, seg, n):
    return jax.ops.segment_sum(src, seg, n)
kernel_name = 'mk_conv_preact_d4_conv_nchw32_r4_824ed0'

def setup_inputs(seed: int=0):
    np.random.seed(seed)
    _w = jnp.asarray

    def _rec_inputs():
        import jax
        import jax.numpy as jnp
        _gk = jax.random.key(seed)
        x = -0.000125 + 0.9999 * jax.random.normal(jax.random.fold_in(_gk, 1), (16, 32, 64, 64), jnp.float32)
        return x
    x = _rec_inputs()

    def _L0_conv_setup():
        import jax, jax.numpy as jnp
        import numpy as np
        IN_C, OUT_C = (32, 32)
        MODES_X, MODES_T = (16, 16)
        K2 = MODES_X // 2
        BAND_START = 50
        SCALE = 1.0 / (IN_C * OUT_C)
        key = jax.random.key(seed)
        k1, k2_, k3 = jax.random.split(key, 3)
        x = jax.random.normal(k1, (16, IN_C, 64, 64), dtype=jnp.float32)
        weights_r = SCALE * jax.random.uniform(k2_, (4, IN_C, OUT_C, K2, MODES_T), dtype=jnp.float32)
        weights_i = SCALE * jax.random.uniform(k3, (4, IN_C, OUT_C, K2, MODES_T), dtype=jnp.float32)
        return {'x': x, 'weights_r': weights_r, 'weights_i': weights_i}
    _L0_conv_all = _L0_conv_setup()
    _L0_conv_in = {k: v for k, v in _L0_conv_all.items() if k in ('weights_r', 'weights_i')}
    del _L0_conv_all

    def _L1_conv_setup():
        import jax, jax.numpy as jnp
        import numpy as np
        from jax import lax
        P = 8
        NB = 6
        EDGE_BOOST = 0.5
        HF_THR = 0.6
        DELTA = 1.0 / (NB - 1)

        def _radial_grid():
            ky = jnp.arange(P, dtype=jnp.float32)
            ky = jnp.minimum(ky, P - ky)
            kx = jnp.arange(P // 2 + 1, dtype=jnp.float32)
            r = jnp.sqrt(ky[:, None] ** 2 + kx[None, :] ** 2)
            r_max = np.sqrt(2.0 * (P // 2) ** 2) + 1e-08
            return jnp.clip(r / r_max, 0.0, 1.0)
        key = jax.random.key(seed)
        k1, k2 = jax.random.split(key)
        x = jax.random.normal(k1, (4, 32, 128, 128), dtype=jnp.float32)
        gain = jax.random.uniform(k2, (1, NB), dtype=jnp.float32)
        return {'x': x, 'gain': gain}
    _L1_conv_all = _L1_conv_setup()
    _L1_conv_in = {k: v for k, v in _L1_conv_all.items() if k in ('gain',)}
    del _L1_conv_all

    def _L2_conv_setup():
        import jax, jax.numpy as jnp
        import numpy as np
        key = jax.random.key(seed)
        k1, k2 = jax.random.split(key)
        x = jax.random.normal(k1, (8, 32, 63, 63), dtype=jnp.float32)
        weight = jax.random.normal(k2, (32, 32, 5, 5), dtype=jnp.float32)
        return {'x': x, 'weight': weight}
    _L2_conv_all = _L2_conv_setup()
    _L2_conv_in = {k: v for k, v in _L2_conv_all.items() if k in ('weight',)}
    del _L2_conv_all

    def _L3_conv_setup():
        import jax, jax.numpy as jnp
        import numpy as np
        key = jax.random.key(seed)
        kx, kw = jax.random.split(key)
        B, C, O, H, W = (16, 32, 32, 64, 64)
        x = jax.random.normal(kx, (B, C, H, W), dtype=jnp.float32)
        fan_in = C * H * W
        fan_out = O * H * W
        limit = float(np.sqrt(6.0 / (fan_in + fan_out)))
        weights = jax.random.uniform(kw, (O, C, H, W), dtype=jnp.float32, minval=-limit, maxval=limit)
        return {'x': x, 'weights': weights}
    _L3_conv_all = _L3_conv_setup()
    _L3_conv_in = {k: v for k, v in _L3_conv_all.items() if k in ('weights',)}
    del _L3_conv_all
    return {'x': x, 'L0_conv_weights_r': _L0_conv_in['weights_r'], 'L0_conv_weights_i': _L0_conv_in['weights_i'], 'L1_conv_gain': _L1_conv_in['gain'], 'L2_conv_weight': _L2_conv_in['weight'], 'L3_conv_weights': _L3_conv_in['weights']}

def reference(x, L0_conv_weights_r, L0_conv_weights_i, L1_conv_gain, L2_conv_weight, L3_conv_weights):
    import jax
    import jax.numpy as jnp

    def _L0_conv_ref(x, weights_r, weights_i):
        import jax, jax.numpy as jnp
        import numpy as np
        IN_C, OUT_C = (32, 32)
        MODES_X, MODES_T = (16, 16)
        K2 = MODES_X // 2
        BAND_START = 50
        SCALE = 1.0 / (IN_C * OUT_C)
        w = (weights_r + 1j * weights_i).astype(jnp.complex64)
        B, _, Nx, Nt = x.shape
        x_ft = jnp.fft.rfft2(x)
        out_ft = jnp.zeros((B, OUT_C, Nx, x_ft.shape[-1]), dtype=jnp.complex64)
        mix = lambda xs, ws: jnp.einsum('bixy,ioxy->boxy', xs, ws)
        out_ft = out_ft.at[:, :, :K2, :MODES_T].set(mix(x_ft[:, :, :K2, :MODES_T], w[0]))
        out_ft = out_ft.at[:, :, BAND_START:BAND_START + K2, :MODES_T].set(mix(x_ft[:, :, BAND_START:BAND_START + K2, :MODES_T], w[1]))
        out_ft = out_ft.at[:, :, Nx - K2:, :MODES_T].set(mix(x_ft[:, :, Nx - K2:, :MODES_T], w[2]))
        ns, ne = (Nx - BAND_START - K2, Nx - BAND_START)
        out_ft = out_ft.at[:, :, ns:ne, :MODES_T].set(mix(x_ft[:, :, ns:ne, :MODES_T], w[3]))
        return jnp.fft.irfft2(out_ft, s=(Nx, Nt))

    def _L1_conv_ref(x, gain):
        import jax, jax.numpy as jnp
        import numpy as np
        from jax import lax
        P = 8
        NB = 6
        EDGE_BOOST = 0.5
        HF_THR = 0.6
        DELTA = 1.0 / (NB - 1)

        def _radial_grid():
            ky = jnp.arange(P, dtype=jnp.float32)
            ky = jnp.minimum(ky, P - ky)
            kx = jnp.arange(P // 2 + 1, dtype=jnp.float32)
            r = jnp.sqrt(ky[:, None] ** 2 + kx[None, :] ** 2)
            r_max = np.sqrt(2.0 * (P // 2) ** 2) + 1e-08
            return jnp.clip(r / r_max, 0.0, 1.0)
        B, C, H, W = x.shape
        ht, wt = (H // P, W // P)
        r = _radial_grid()
        centers = jnp.linspace(0.0, 1.0, NB).astype(jnp.float32)
        w = jax.nn.relu(1.0 - jnp.abs(r[None] - centers[:, None, None]) / DELTA)
        w = w / (w.sum(axis=0, keepdims=True) + 1e-08)
        mask = jnp.maximum((w * gain.reshape(-1)[:, None, None]).sum(axis=0), 0.0)
        x_mean = x.mean(axis=1, keepdims=True)
        sobel_x = jnp.array([[-1.0, 0.0, 1.0], [-2.0, 0.0, 2.0], [-1.0, 0.0, 1.0]], dtype=x.dtype).reshape(1, 1, 3, 3)
        sobel_y = jnp.array([[-1.0, -2.0, -1.0], [0.0, 0.0, 0.0], [1.0, 2.0, 1.0]], dtype=x.dtype).reshape(1, 1, 3, 3)
        gx = lax.conv_general_dilated(x_mean, sobel_x, (1, 1), ((1, 1), (1, 1)))
        gy = lax.conv_general_dilated(x_mean, sobel_y, (1, 1), ((1, 1), (1, 1)))
        edge = jnp.sqrt(gx * gx + gy * gy + 1e-06)
        edge_strength = edge.reshape(B, 1, ht, P, wt, P).mean(axis=(3, 5))
        edge_strength = edge_strength - edge_strength.min(axis=(2, 3), keepdims=True)
        edge_norm = edge_strength / (edge_strength.max(axis=(2, 3), keepdims=True) + 1e-06)
        edge_coeff = 1.0 + EDGE_BOOST * edge_norm
        hf_mask = (r >= HF_THR).astype(x.dtype)
        scaling = 1.0 + (edge_coeff[..., None, None] - 1.0) * hf_mask
        x_patch = x.reshape(B, C, ht, P, wt, P).transpose(0, 1, 2, 4, 3, 5)
        xf = jnp.fft.rfft2(x_patch)
        xf = xf * mask * scaling
        out = jnp.fft.irfft2(xf, s=(P, P))
        return out.transpose(0, 1, 2, 4, 3, 5).reshape(B, C, H, W)

    def _L2_conv_ref(x, weight):
        import jax, jax.numpy as jnp
        import numpy as np
        k = weight.shape[-1]
        p = k // 2
        xp = jnp.pad(x, ((0, 0), (0, 0), (p, p), (p, p)), mode='reflect')
        H, W = (xp.shape[-2], xp.shape[-1])
        wp = jnp.zeros((weight.shape[0], weight.shape[1], H, W), dtype=x.dtype)
        wp = wp.at[:, :, :k, :k].set(weight)
        shift = -k // 2
        wp = jnp.roll(wp, shift=(shift, shift), axis=(-2, -1))
        x_fft = jnp.fft.fft2(xp)
        w_fft = jnp.fft.fft2(wp)
        out_fft = jnp.einsum('bihw,oihw->bohw', x_fft, w_fft)
        out = jnp.fft.ifft2(out_fft).real
        return out[:, :, p:-p, p:-p]

    def _L3_conv_ref(x, weights):
        import jax, jax.numpy as jnp
        import numpy as np
        B, C, H, W = x.shape
        x_f = jnp.fft.rfft2(x)
        k_f = jnp.fft.rfft2(weights)
        out_f = jnp.einsum('bchw,ochw->bohw', x_f, k_f)
        out = jnp.fft.irfft2(out_f, s=(H, W))
        return out

    def _gn(v, G=16, eps=1e-05):
        B_, C_, H_, W_ = v.shape
        g = v.reshape(B_, G, C_ // G, H_, W_)
        m = jnp.mean(g, axis=(2, 3, 4), keepdims=True)
        s = jnp.var(g, axis=(2, 3, 4), keepdims=True)
        return ((g - m) / jnp.sqrt(s + eps)).reshape(v.shape)

    def _ln_c(v, eps=1e-06):
        m = jnp.mean(v, axis=1, keepdims=True)
        s = jnp.var(v, axis=1, keepdims=True)
        return (v - m) / jnp.sqrt(s + eps)

    def _ln_t(v, eps=1e-05):
        m = jnp.mean(v, axis=-1, keepdims=True)
        s = jnp.var(v, axis=-1, keepdims=True)
        return (v - m) / jnp.sqrt(s + eps)

    def _to_tokens(v):
        B_, C_, H_, W_ = v.shape
        return v.reshape(B_, C_, H_ * W_).transpose(0, 2, 1)

    def _from_tokens(t, like):
        B_, C_, H_, W_ = like.shape
        return t.transpose(0, 2, 1).reshape(B_, C_, H_, W_)
    x = x + _L0_conv_ref(_gn(x), L0_conv_weights_r, L0_conv_weights_i)
    x = x + _L1_conv_ref(_gn(x), L1_conv_gain)
    x = x + _L2_conv_ref(_gn(x), L2_conv_weight)
    x = x + _L3_conv_ref(_gn(x), L3_conv_weights)
    return x

_drawn_inputs = setup_inputs


def setup_inputs(seed=0):
    import zlib

    import numpy as np

    out = dict(_drawn_inputs(seed))
    spreads = {}
    factors = {'L0_conv_weights_r': 64.0, 'L0_conv_weights_i': 64.0}
    for name, (base, spread) in spreads.items():
        noise = np.random.default_rng([zlib.crc32(name.encode()), seed]).standard_normal(out[name].shape)
        drawn = base * np.exp(spread * noise) if base else spread * noise
        out[name] = jnp.asarray(drawn.astype(out[name].dtype))
    for name, factor in factors.items():
        out[name] = (out[name] * factor).astype(out[name].dtype)
    return out
```

```python
from contextlib import ExitStack

import numpy as np

import concourse.bass as bass
from concourse import mybir

F32 = mybir.dt.float32
ALU = mybir.AluOpType
ACT = mybir.ActivationFunctionType
AX = mybir.AxisListType

B, C, N = 16, 32, 64
P = 128
Q = B * C // P
IB = P // C
PIX = N * N
CH = 512
NCH = PIX // CH
ROWS = CH // N
SLOT = N // 2
KT = 16
K2 = 8
BAND = 50
L0_BLOCKS = [list(range(0, N - BAND - K2)), list(range(BAND, N - K2)), list(range(N - K2, N)),
             list(range(N - BAND - K2, N - BAND))]
L0_OFF = [0, 6, 12, 20]
KX = sum(len(b) for b in L0_BLOCKS)
PS = 8
NB = 6
KS = 5
RB = N // 4 + 1
PW = N + KS - 1
GN_EPS = 1e-5


def constants():
    f = np.float64
    ang = 2 * np.pi / N
    n = np.arange(N)
    out = {}
    out["ident"] = np.eye(P)
    out["pair"] = np.kron(np.eye(P // 2), np.full((2, 2), 0.5))

    def two(m, k=2):
        return np.kron(np.eye(k), m)

    kt = np.arange(KT)
    fw = np.stack([np.cos(ang * np.outer(n, kt)), -np.sin(ang * np.outer(n, kt))], 1)
    out["l0_fw"] = two(fw.reshape(N, 2 * KT))
    kx = np.array(sum(L0_BLOCKS, []))
    out["l0_fh"] = complex_matrix(n, kx, -1.0)
    out["l0_ih"] = complex_matrix(kx, n, 1.0) / N
    iw = np.stack([np.cos(ang * np.outer(kt, n)), -np.sin(ang * np.outer(kt, n))], 1) * 2 / N
    iw[0] /= 2
    iw[0, 1] = 0
    out["l0_iw"] = two(iw.reshape(2 * KT, N), 4)

    s = np.arange(SLOT)
    fw = np.stack([np.cos(ang * np.outer(n, s)), -np.sin(ang * np.outer(n, s))], 1)
    fw[:, 1, 0] = (-1.0) ** n
    out["l3_fw"] = two(fw.reshape(N, 2 * SLOT))
    out["l3_fh"] = complex_matrix(n, n, -1.0)
    out["l3_ih"] = complex_matrix(n, n, 1.0) / N
    iw = np.stack([np.cos(ang * np.outer(s, n)), -np.sin(ang * np.outer(s, n))], 1) * 2 / N
    iw[0, 0] = 1.0 / N
    iw[0, 1] = (-1.0) ** n / N
    out["l3_iw"] = two(iw.reshape(2 * SLOT, N))
    f0 = np.zeros((N, 2, N, 2))
    i0 = np.zeros((N, 2, N, 2))
    for half in range(2):
        for m in range(SLOT):
            at = half * SLOT + m
            if m:
                f0[:, half, at, 0], f0[:, half, at, 1] = np.cos(ang * n * m), -np.sin(ang * n * m)
                i0[at, 0, :, half], i0[at, 1, :, half] = 2 * np.cos(ang * n * m) / N, -2 * np.sin(ang * n * m) / N
            else:
                f0[:, half, at, 0], f0[:, half, at, 1] = 1.0, (-1.0) ** n
                i0[at, 0, :, half], i0[at, 1, :, half] = 1.0 / N, (-1.0) ** n / N
    out["l3_fh0"] = f0.reshape(P, P)
    out["l3_ih0"] = i0.reshape(P, P)

    k = np.arange(PS)
    y = np.repeat(k, PS)
    x = np.tile(k, PS)
    th = 2 * np.pi / PS * (np.outer(y, y) + np.outer(x, x))
    d = np.concatenate([np.cos(th), np.sin(th)], 0) / PS
    out["l1_dft"] = np.concatenate([d, d], 1)
    out["l1_same"] = np.kron(np.eye(2), np.ones((PS * PS, PS * PS)))
    ky = np.minimum(y, PS - y).astype(np.float32)
    kx8 = np.minimum(x, PS - x).astype(np.float32)
    r = np.sqrt(ky ** 2 + kx8 ** 2).astype(np.float32)
    r = np.clip(r / np.float32(np.sqrt(2.0 * (PS // 2) ** 2) + 1e-08), 0, 1).astype(f)
    centers = np.linspace(0.0, 1.0, NB)
    w = np.maximum(1.0 - np.abs(r[None] - centers[:, None]) / (1.0 / (NB - 1)), 0)
    w = w / (w.sum(0, keepdims=True) + 1e-08)
    out["l1_band"] = np.concatenate([w, w], 1)
    out["l1_high"] = np.concatenate([(r >= 0.6), (r >= 0.6)]).astype(f)[:, None]
    wide = np.zeros((P, 12 + 124 + IB + 124))
    for b in range(IB):
        wide[b * C:(b + 1) * C, 12 + 124 + b] = 1.0 / C
    out["l1_mean"] = wide
    out["l1_pick"] = np.stack([np.eye(P)[:, 16 * s:16 * s + 16] for s in range(PS)], 1).reshape(P, P)
    out["l1_spread"] = np.concatenate([np.kron(np.eye(B)[:, IB * q:IB * q + IB], np.ones((1, C)))
                                       for q in range(Q)], 1)
    return {k: np.ascontiguousarray(v, np.float32) for k, v in out.items()}


def complex_matrix(a, b, sign):
    th = 2 * np.pi / N * np.outer(a, b)
    c, s = np.cos(th), sign * np.sin(th)
    m = np.stack([np.stack([c, s], -1), np.stack([-s, c], -1)], 1)
    return m.reshape(2 * len(a), 2 * len(b))


class Program:

    def __init__(self, nc, ctx, ins, out):
        self.nc, self.ins, self.out, self.names = nc, ins, out, set()
        self.ctx = ctx
        self.X = self.sb(ctx, "X", [P, Q, PIX])
        self.ident = self.sb(ctx, "ident", [P, P])
        self.pair = self.sb(ctx, "pair", [P, P])
        self.bn = self.sb(ctx, "bn", [P, NCH, 6])
        self.mv = self.sb(ctx, "mv", [P, 2])
        self.st = self.sb(ctx, "st", [P, Q, 2])
        self.gm = self.sb(ctx, "gm", [P, Q, 2])
        self.var = self.sb(ctx, "var", [P, Q])
        self.sd = self.sb(ctx, "sd", [P, Q])
        self.rstd = self.sb(ctx, "rstd", [P, Q])
        self.shift = self.sb(ctx, "shift", [P, Q])
        self.eps = self.sb(ctx, "eps", [P, 2])
        self.psum = [ctx.enter_context(nc.psum_tensor(f"bank{i}", [P, CH], F32)) for i in range(8)]
        self.zero = self.sb(ctx, "zero", [P, 1])
        self.pace = self.sem("pace")
        self.kf = nc.dram_tensor("kf", (SLOT // 4, P, 8, P * 4), F32, kind="Internal").ap()

    def sb(self, ctx, name, shape, dt=F32):
        return ctx.enter_context(self.nc.sbuf_tensor(name, shape, dt))

    def sem(self, name):
        assert name not in self.names
        self.names.add(name)
        return self.ctx.enter_context(self.nc.semaphore(name))


    def image_stats(self, dve, q, step, at):
        dve.sem_inc(self.pace, 1)
        for c in range(NCH):
            s = dve.bn_stats(self.bn[:, c, :], self.X[:, q, c * CH:(c + 1) * CH])
        s.then_inc(step, 1)
        dve.wait_ge(step, at + 1)
        dve.sem_inc(self.pace, 1)
        dve.bn_aggr(self.mv[:], self.bn[:].rearrange("p a b -> p (a b)")).then_inc(step, 1)
        dve.wait_ge(step, at + 2)
        dve.tensor_copy(self.st[:, q, 0:1], self.mv[:, 0:1])
        dve.scalar_tensor_tensor(self.st[:, q, 1:2], self.mv[:, 0:1], self.mv[:, 0:1], self.mv[:, 1:2],
                                 ALU.mult, ALU.add).then_inc(step, 1)
        dve.wait_ge(step, at + 3)

    def stats_stage(self, name):
        summed, read, deviation, done = (self.sem(f"{name}_{x}") for x in ("sum", "var", "dev", "norm"))
        gm, sm = self.gm, self.psum[0]
        with self.nc.Block() as block:
            @block.tensor
            def _(pe):
                pe.matmul(sm[:, 0:2 * Q], self.pair[:], self.st[:].rearrange("p q t -> p (q t)"),
                          start=True, stop=True).then_inc(summed, 1)

            @block.scalar
            def _(act):
                act.wait_ge(read, 4)
                act.activation(self.sd[:], self.var[:], ACT.Sqrt, bias=self.eps[:, 0:1]).then_inc(deviation, 1)

            @block.vector
            def _(dve):
                dve.wait_ge(summed, 1)
                dve.tensor_copy(gm[:].rearrange("p q t -> p (q t)"), sm[:, 0:2 * Q]).then_inc(read, 1)
                dve.wait_ge(read, 1)
                dve.tensor_tensor(self.var[:], gm[:, :, 0], gm[:, :, 0], ALU.mult).then_inc(read, 1)
                dve.wait_ge(read, 2)
                dve.tensor_tensor(self.var[:], gm[:, :, 1], self.var[:], ALU.subtract).then_inc(read, 1)
                dve.wait_ge(read, 3)
                dve.tensor_scalar(self.var[:], self.var[:], 0.0, None, ALU.max).then_inc(read, 1)
                dve.wait_ge(deviation, 1)
                dve.reciprocal(self.rstd[:], self.sd[:]).then_inc(done, 1)
                dve.wait_ge(done, 1)
                dve.scalar_tensor_tensor(self.shift[:], gm[:, :, 0], -1.0, self.rstd[:], ALU.mult, ALU.mult)

    def normalise(self, act, dst, q, c, ready, patches=False):
        to, of = dst[:, c * CH:(c + 1) * CH], self.X[:, q, c * CH:(c + 1) * CH]
        if patches:
            to = to.rearrange("p (a y x) -> p a y x", a=PS, x=PS)
            of = of.rearrange("p (y a x) -> p a y x", y=PS, x=PS)
        act.activation(to, of, ACT.Identity,
                       scale=self.rstd[:, bass.ds(q, 1)], bias=self.shift[:, bass.ds(q, 1)]).then_inc(ready, 1)


def load_constant(pr, ctx, eng, sem, name, shape):
    t = pr.sb(ctx, name, shape)
    eng.append((t, pr.ins[name]))
    return t


def kernel_spectra_stage(pr):
    nc, ps = pr.nc, pr.psum
    tiles = C // IB
    const, loaded = pr.sem("ks_const"), [pr.sem(f"ks_load{p}") for p in range(2)]
    x_loaded = pr.sem("ks_x")
    turned, turned_read = pr.sem("ks_turned"), pr.sem("ks_turned_read")
    made, made_read = pr.sem("ks_made"), pr.sem("ks_made_read")
    stored, step, eps = pr.sem("ks_stored"), pr.sem("ks_step"), pr.sem("ks_eps")
    w_tiles = pr.ins["L3_conv_weights"].rearrange("(t o) c h w -> t (o c) (h w)", o=IB)
    x_groups = pr.ins["x"].rearrange("(q b) c h w -> q (b c) (h w)", b=IB)
    with ExitStack() as ctx:
        src = [pr.sb(ctx, f"ks_src{p}", [P, PIX]) for p in range(2)]
        tt = [pr.sb(ctx, f"ks_tt{p}", [P, CH]) for p in range(2)]
        cols = pr.sb(ctx, "ks_cols", [P, IB, SLOT, C])
        spec = pr.sb(ctx, "ks_spec", [P, SLOT // 4, IB, N, 2])
        fw, fh, fh0 = (pr.sb(ctx, f"ks_{n}", [P, P]) for n in ("fw", "fh", "fh0"))
        with nc.Block() as block:
            @block.sync
            def _(sp):
                for t, n in ((pr.ident, "ident"), (pr.pair, "pair"), (fw, "l3_fw"), (fh, "l3_fh"), (fh0, "l3_fh0")):
                    sp.dma_start(t[:], pr.ins[n]).then_inc(const, 16)
                with sp.Fori(0, tiles // 2) as i:
                    for p in range(2):
                        sp.wait_ge(turned, 32 * i)
                        sp.dma_start(src[p][:], w_tiles[2 * i + p]).then_inc(loaded[p], 16)
                    sp.wait_ge(x_loaded, 16 * i)
                    sp.dma_start(pr.X[:, i, :], x_groups[i]).then_inc(x_loaded, 16)

            @block.gpsimd
            def _(pool):
                with pool.Fori(0, tiles // 2) as i:
                    for p in range(2):
                        pool.wait_ge(made_read, 32 * i + 16 * p + 16)
                        pool.dma_start(pr.kf[:, :, 2 * i + p, :].rearrange("s p n -> p s n"),
                                       spec[:].rearrange("p s o k r -> p s (o k r)")).then_inc(stored, 16)
                pool.wait_ge(stored, 16 * tiles)

            @block.tensor
            def _(pe):
                pe.wait_ge(const, 16 * 5)
                with pe.Fori(0, tiles // 2) as i:
                    for p in range(2):
                        pe.wait_ge(loaded[p], 16 * i + 16)
                        forward_products(pe, pr, src[p], tt, cols, fw, fh, fh0, 32 * i + 16 * p,
                                         turned, turned_read, made, made_read)

            @block.vector
            def _(dve):
                dve.memset(pr.eps[:], GN_EPS).then_inc(eps, 1)
                dve.memset(pr.zero[:], 0.0).then_inc(eps, 1)
                with dve.Fori(0, tiles // 2) as i:
                    for p in range(2):
                        copy_turned(dve, ps, tt, cols, 32 * i + 16 * p, turned, turned_read, made)
                    dve.wait_ge(x_loaded, 16 * i + 16)
                    pr.image_stats(dve, i, step, 3 * i)

            @block.scalar
            def _(act):
                with act.Fori(0, tiles // 2) as i:
                    for p in range(2):
                        base = 32 * i + 16 * p
                        copy_rows(act, ps, src[p], base, made, made_read)
                        for s in range(SLOT // 4):
                            act.wait_ge(made, base + NCH + s + 1)
                            if s == 0:
                                act.wait_ge(stored, 32 * i + 16 * p)
                            act.copy(spec[:, s].rearrange("p o k r -> p (o k r)"), ps[2 + s % 2][:]
                                     ).then_inc(made_read, 1)


def forward_products(pe, pr, src, tt, cols, fw, fh, fh0, base, turned, turned_read, made, made_read,
                     src_ready=None, src_base=None):
    ps = pr.psum

    def turn(j):
        if src_ready is not None:
            pe.wait_ge(src_ready, src_base + j + 1)
        if j >= 2:
            pe.wait_ge(turned_read, base + j - 1)
        for k in range(4):
            m = pe.transpose(ps[j % 2][:, k * P:(k + 1) * P], src[:, (4 * j + k) * P:(4 * j + k + 1) * P], pr.ident[:])
        m.then_inc(turned, 1)

    def rows(j):
        pe.wait_ge(turned_read, base + j + 1)
        if j == 0:
            pe.wait_ge(made_read, base)
        if j >= 2:
            pe.wait_ge(made_read, base + j - 1)
        for k in range(4):
            m = pe.matmul(ps[2 + j % 2][:, k * P:(k + 1) * P], tt[j % 2][:, k * P:(k + 1) * P], fw[:],
                          start=True, stop=True)
        m.then_inc(made, 1)

    turn(0)
    for j in range(NCH):
        if j + 1 < NCH:
            turn(j + 1)
        rows(j)
    spectra = src[:].rearrange("p (k s) -> p k s", s=SLOT)

    def turn_columns(s):
        if s == 0:
            pe.wait_ge(made_read, base + NCH)
        if s >= 2:
            pe.wait_ge(turned_read, base + NCH + s - 1)
        for k in range(4):
            m = pe.transpose(ps[s % 2][:, k * P:(k + 1) * P], spectra[:, :, 4 * s + k], pr.ident[:])
        m.then_inc(turned, 1)

    def columns(s):
        pe.wait_ge(turned_read, base + NCH + s + 1)
        if s >= 2:
            pe.wait_ge(made_read, base + NCH + s - 1)
        for b in range(IB):
            m = pe.matmul(ps[2 + s % 2][:, b * P:(b + 1) * P], cols[:, b, 4 * s:4 * s + 4].rearrange("p s c -> p (s c)"),
                          fh[:], start=True, stop=True)
        if s == 0:
            for b in range(IB):
                m = pe.matmul(ps[2][0:C, b * P:(b + 1) * P], cols[:, b, 0], fh0[:],
                              start=True, stop=True)
        m.then_inc(made, 1)

    turn_columns(0)
    for s in range(SLOT // 4):
        if s + 1 < SLOT // 4:
            turn_columns(s + 1)
        columns(s)


def copy_turned(dve, ps, tt, cols, base, turned, turned_read, made):
    for j in range(NCH):
        dve.wait_ge(turned, base + j + 1)
        if j >= 2:
            dve.wait_ge(made, base + j - 1)
        dve.tensor_copy(tt[j % 2][:], ps[j % 2][:]).then_inc(turned_read, 1)
    for s in range(SLOT // 4):
        dve.wait_ge(turned, base + NCH + s + 1)
        dve.tensor_copy(cols[:, :, 4 * s:4 * s + 4].rearrange("p b s c -> p s b c"),
                        ps[s % 2][:].rearrange("p (s b c) -> p s b c", s=4, b=IB)).then_inc(turned_read, 1)


def copy_rows(act, ps, src, base, made, made_read, after=lambda j: None):
    for j in range(NCH):
        act.wait_ge(made, base + j + 1)
        act.copy(src[:, j * CH:(j + 1) * CH], ps[2 + j % 2][:]).then_inc(made_read, 1)
        after(j)


def l0_forward_stage(pr, xm0):
    nc, ps = pr.nc, pr.psum
    const, ready, turned, turned_read = (pr.sem(f"f0_{n}") for n in ("const", "ready", "turned", "turned_read"))
    made, made_read, negated = (pr.sem(f"f0_{n}") for n in ("made", "made_read", "negated"))
    TG, MG = NCH + KT // 4, NCH + KT // 4
    RW = 2 * 2 * KT
    with ExitStack() as ctx:
        src = pr.sb(ctx, "f0_src", [P, PIX])
        tt = [pr.sb(ctx, f"f0_tt{p}", [P, CH]) for p in range(2)]
        rows = pr.sb(ctx, "f0_rows", [P, N, 2, KT])
        cols = pr.sb(ctx, "f0_cols", [P, IB, KT, C])
        fw, fh = pr.sb(ctx, "f0_fw", [P, RW]), pr.sb(ctx, "f0_fh", [P, 2 * KX])
        with nc.Block() as block:
            @block.sync
            def _(sp):
                sp.dma_start(fw[:], pr.ins["l0_fw"]).then_inc(const, 16)
                sp.dma_start(fh[:], pr.ins["l0_fh"]).then_inc(const, 16)

            @block.tensor
            def _(pe):
                pe.wait_ge(const, 32)
                with pe.Fori(0, Q) as q:
                    def turn(j):
                        pe.wait_ge(ready, NCH * q + j + 1)
                        if j >= 2:
                            pe.wait_ge(turned_read, TG * q + j - 1)
                        for k in range(4):
                            at = (4 * j + k) * P
                            m = pe.transpose(ps[j % 2][:, k * P:(k + 1) * P], src[:, at:at + P], pr.ident[:])
                        m.then_inc(turned, 1)

                    turn(0)
                    for j in range(NCH):
                        if j + 1 < NCH:
                            turn(j + 1)
                        pe.wait_ge(turned_read, TG * q + j + 1)
                        if j == 0:
                            pe.wait_ge(made_read, MG * q)
                        if j >= 2:
                            pe.wait_ge(made_read, MG * q + j - 1)
                        for k in range(4):
                            m = pe.matmul(ps[2 + j % 2][:, k * RW:(k + 1) * RW], tt[j % 2][:, k * P:(k + 1) * P],
                                          fw[:], start=True, stop=True)
                        m.then_inc(made, 1)
                    pe.wait_ge(made_read, MG * q + NCH)

                    def turn_columns(s):
                        if s >= 2:
                            pe.wait_ge(turned_read, TG * q + NCH + s - 1)
                        for k in range(4):
                            m = pe.transpose(ps[s % 2][:, k * P:(k + 1) * P], rows[:, :, :, 4 * s + k].rearrange("p h r -> p (h r)"),
                                             pr.ident[:])
                        m.then_inc(turned, 1)

                    turn_columns(0)
                    for s in range(KT // 4):
                        if s + 1 < KT // 4:
                            turn_columns(s + 1)
                        pe.wait_ge(turned_read, TG * q + NCH + s + 1)
                        if s >= 2:
                            pe.wait_ge(made_read, MG * q + NCH + s - 1)
                        for b in range(IB):
                            m = pe.matmul(ps[2 + s % 2][:, b * 2 * KX:(b + 1) * 2 * KX],
                                          cols[:, b, 4 * s:4 * s + 4].rearrange("p s c -> p (s c)"), fh[:],
                                          start=True, stop=True)
                        m.then_inc(made, 1)

            @block.vector
            def _(dve):
                with dve.Fori(0, Q) as q:
                    for j in range(NCH):
                        dve.wait_ge(turned, TG * q + j + 1)
                        if j >= 2:
                            dve.wait_ge(made, MG * q + j - 1)
                        dve.tensor_copy(tt[j % 2][:], ps[j % 2][:]).then_inc(turned_read, 1)
                    for s in range(KT // 4):
                        dve.wait_ge(turned, TG * q + NCH + s + 1)
                        dve.tensor_copy(cols[:, :, 4 * s:4 * s + 4].rearrange("p b s c -> p s b c"),
                                        ps[s % 2][:].rearrange("p (s b c) -> p s b c", s=4, b=IB)
                                        ).then_inc(turned_read, 1)

            @block.scalar
            def _(act):
                with act.Fori(0, Q) as q:
                    act.wait_ge(turned, TG * q)
                    for j in range(2):
                        pr.normalise(act, src, q, j, ready)
                    for j in range(NCH):
                        act.wait_ge(made, MG * q + j + 1)
                        act.copy(rows[:, ROWS * j:ROWS * j + ROWS].rearrange("p h r k -> p (h r k)"),
                                 ps[2 + j % 2][:, 0:4 * RW]).then_inc(made_read, 1)
                        if j + 2 < NCH:
                            pr.normalise(act, src, q, j + 2, ready)
                    for s in range(KT // 4):
                        act.wait_ge(made, MG * q + NCH + s + 1)
                        for r in range(2):
                            m = act.copy(xm0[:, s, :, 1 + r, bass.ds(IB * q, IB)],
                                         ps[2 + s % 2][:, 0:IB * 2 * KX].rearrange(
                                             "p (b k r) -> p k r b", b=IB, r=2)[:, :, r, :])
                        m.then_inc(made_read, 1)

            @block.gpsimd
            def _(pool):
                with pool.Fori(0, Q) as q:
                    pool.wait_ge(made_read, MG * q + MG)
                    for s in range(KT // 4):
                        pool.tensor_tensor(xm0[:, s, :, 0, bass.ds(IB * q, IB)],
                                           pr.zero[:].unsqueeze(2).broadcast_to([P, KX, IB]),
                                           xm0[:, s, :, 2, bass.ds(IB * q, IB)], ALU.subtract).then_inc(negated, 1)


def l0_mix_stage(pr, xm0, y0):
    nc, ps = pr.nc, pr.psum
    moved, mixed, mixed_read = (pr.sem(f"m0_{n}") for n in ("moved", "mixed", "mixed_read"))
    w_loaded, back = pr.sem("m0_weights"), pr.sem("m0_back")
    with ExitStack() as ctx:
        wr, wi = (pr.sb(ctx, f"m0_{n}", [P, C, K2, KT]) for n in ("wr", "wi"))
        xb = pr.sb(ctx, "m0_xb", [P, KT, K2, 3, B])
        yb = pr.sb(ctx, "m0_yb", [P, KT, K2, 2, B])
        used = [len(b) for b in L0_BLOCKS]
        with nc.Block() as block:
            @block.sync
            def _(sp):
                for t, n in ((wr, "L0_conv_weights_r"), (wi, "L0_conv_weights_i")):
                    sp.dma_start(t[:].rearrange("p o x y -> p (o x y)"),
                                 pr.ins[n].rearrange("n i o x y -> (n i) (o x y)")).then_inc(w_loaded, 16)
                for w in range(4):
                    for s in range(4):
                        sp.dma_start(xb[w * C:(w + 1) * C, s:KT:4, 0:used[w]].rearrange("c s x r b -> c s (x r b)"),
                                     xm0[s * C:(s + 1) * C, :, L0_OFF[w]:L0_OFF[w] + used[w]].rearrange(
                                         "c s x r b -> c s (x r b)")).then_inc(moved, 16)
                sp.wait_ge(mixed_read, 16)
                for w in range(4):
                    for s in range(4):
                        sp.dma_start(y0[s * C:(s + 1) * C, :, L0_OFF[w]:L0_OFF[w] + used[w]].rearrange(
                            "c s x r b -> c s (x r b)"),
                            yb[w * C:(w + 1) * C, s:KT:4, 0:used[w]].rearrange("c s x r b -> c s (x r b)")
                        ).then_inc(back, 16)
                sp.wait_ge(back, 16 * 16)

            @block.tensor
            def _(pe):
                pe.wait_ge(w_loaded, 32)
                pe.wait_ge(moved, 16 * 16)
                for n in range(KT * K2):
                    for w in range(4):
                        m = (n + 32 * w) % (KT * K2)
                        kt, x = m // K2, m % K2
                        if x >= used[w]:
                            continue
                        at = slice(w * C, (w + 1) * C)
                        to = ps[m // 16][at, m % 16 * 2 * B:(m % 16 + 1) * 2 * B]
                        pe.matmul(to, wr[at, :, x, kt], xb[at, kt, x, 1:3, :], start=True, stop=False)
                        last = pe.matmul(to, wi[at, :, x, kt], xb[at, kt, x, 0:2, :], start=False, stop=True)
                last.then_inc(mixed, 1)

            def copy_out(eng, copy, k):
                for at, n in ((slice(0, 64), used[0]), (slice(64, 128), used[2])):
                    copy(yb[at, 2 * k:2 * k + 2, 0:n].rearrange("p k x r b -> p k (x r b)"),
                         ps[k][at, :].rearrange("p (k m) -> p k m", k=2)[:, :, 0:n * 2 * B]).then_inc(mixed_read, 1)

            @block.vector
            def _(dve):
                dve.wait_ge(mixed, 1)
                for k in range(0, 8, 2):
                    copy_out(dve, dve.tensor_copy, k)

            @block.scalar
            def _(act):
                act.wait_ge(mixed, 1)
                for k in range(1, 8, 2):
                    copy_out(act, act.copy, k)


def inverse_stage(pr, name, y, slots, modes, ih, ih0, iw, rows4, last):
    nc, ps = pr.nc, pr.psum
    K = 2 * modes
    SG = slots // 4
    HG = N // rows4 // 4
    per = CH // (rows4 * N)
    const, staged, turned, turned_read = (pr.sem(f"{name}_{n}") for n in ("const", "staged", "turned", "turned_read"))
    made, made_read, turned2, turned2_read = (pr.sem(f"{name}_{n}") for n in ("made", "made_read", "turned2", "turned2_read"))
    pixels, added, step, stored = (pr.sem(f"{name}_{n}") for n in ("pixels", "added", "step", "stored"))
    out_groups = pr.out.rearrange("(q b) c h w -> q (b c) (h w)", b=IB)
    with ExitStack() as ctx:
        yq = pr.sb(ctx, f"{name}_yq", [P, SG, modes, 2, IB])
        cols = pr.sb(ctx, f"{name}_cols", [P, slots, IB, C])
        rows = pr.sb(ctx, f"{name}_rows", [P, N, slots, 2])
        tt = [pr.sb(ctx, f"{name}_tt{p}", [P, CH]) for p in range(2)]
        mh = pr.sb(ctx, f"{name}_mh", [K, P])
        mh0 = pr.sb(ctx, f"{name}_mh0", [K, P])
        mw = pr.sb(ctx, f"{name}_mw", [P, rows4 * N])
        with nc.Block() as block:
            @block.sync
            def _(sp):
                for t, n in ((mh, ih), (mh0, ih0), (mw, iw)):
                    sp.dma_start(t[:], pr.ins[n]).then_inc(const, 16)
                if last:
                    with sp.Fori(0, Q) as q:
                        sp.wait_ge(added, NCH * q + NCH)
                        sp.dma_start(out_groups[q], pr.X[:, q, :]).then_inc(stored, 16)
                    sp.wait_ge(stored, 16 * Q)

            @block.gpsimd
            def _(pool):
                with pool.Fori(0, Q) as q:
                    pool.wait_ge(turned, SG * q)
                    for s in range(SG):
                        pool.tensor_copy(yq[:, s].rearrange("p k r b -> p (k r) b"),
                                         y[:, s, :, :, bass.ds(IB * q, IB)].rearrange("p k r b -> p (k r) b")
                                         ).then_inc(staged, 1)

            @block.tensor
            def _(pe):
                pe.wait_ge(const, 48)
                with pe.Fori(0, Q) as q:
                    def turn(s):
                        pe.wait_ge(staged, SG * q + s + 1)
                        if s >= 2:
                            pe.wait_ge(turned_read, SG * q + s - 1)
                        pe.sem_inc(pr.pace, 1)
                        for b in range(IB):
                            m = pe.transpose(ps[s % 2][0:K, b * P:(b + 1) * P],
                                             yq[:, s].rearrange("p k r b -> p (k r) b")[:, :, b], pr.ident[:])
                        m.then_inc(turned, 1)

                    turn(0)
                    for s in range(SG):
                        if s + 1 < SG:
                            turn(s + 1)
                        pe.wait_ge(turned_read, SG * q + s + 1)
                        if s >= 2:
                            pe.wait_ge(made_read, SG * q + s - 1)
                        for k in range(4):
                            m = pe.matmul(ps[2 + s % 2][:, k * P:(k + 1) * P],
                                          cols[0:K, 4 * s + k].rearrange("p b o -> p (b o)"),
                                          (mh0 if s == 0 and k == 0 else mh)[:], start=True, stop=True)
                        m.then_inc(made, 1)
                    pe.wait_ge(made_read, SG * q + SG)

                    def turn_rows(g):
                        if g >= 2:
                            pe.wait_ge(turned2_read, HG * q + g - 1)
                        for k in range(4):
                            h = (4 * g + k) * rows4
                            m = pe.transpose(ps[4 + g % 2][:, k * P:(k + 1) * P],
                                             rows[:, h:h + rows4].rearrange("p h s r -> p (h s r)"), pr.ident[:])
                        m.then_inc(turned2, 1)

                    turn_rows(0)
                    for c in range(NCH):
                        g, first = c * per // 4, c * per % 4
                        if first == 0 and g + 1 < HG:
                            turn_rows(g + 1)
                        if first == 0:
                            pe.wait_ge(turned2_read, HG * q + g + 1)
                        if c == 0:
                            pe.wait_ge(added, NCH * q)
                        if c >= 2:
                            pe.wait_ge(added, NCH * q + c - 1)
                        for k in range(per):
                            n = rows4 * N
                            m = pe.matmul(ps[6 + c % 2][:, k * n:(k + 1) * n],
                                          tt[g % 2][:, (first + k) * P:(first + k + 1) * P], mw[:],
                                          start=True, stop=True)
                        m.then_inc(pixels, 1)

            @block.vector
            def _(dve):
                with dve.Fori(0, Q) as q:
                    for s in range(SG):
                        dve.wait_ge(turned, SG * q + s + 1)
                        dve.tensor_copy(cols[0:K, 4 * s:4 * s + 4].rearrange("p s b o -> p b s o"),
                                        ps[s % 2][0:K, :].rearrange("p (b s o) -> p b s o", b=IB, s=4)
                                        ).then_inc(turned_read, 1)
                    for c in range(NCH):
                        dve.wait_ge(pixels, NCH * q + c + 1)
                        x = pr.X[:, q, c * CH:(c + 1) * CH]
                        dve.tensor_tensor(x, x, ps[6 + c % 2][:], ALU.add).then_inc(added, 1)
                    if not last:
                        dve.wait_ge(added, NCH * q + NCH)
                        pr.image_stats(dve, q, step, 3 * q)

            @block.scalar
            def _(act):
                with act.Fori(0, Q) as q:
                    for s in range(SG):
                        act.wait_ge(made, SG * q + s + 1)
                        for r in range(2):
                            m = act.copy(rows[:, :, 4 * s:4 * s + 4, r].rearrange("p h s -> p s h"),
                                         ps[2 + s % 2][:].rearrange("p (s h r) -> p s h r", s=4, r=2)[:, :, :, r])
                        m.then_inc(made_read, 1)
                    for g in range(HG):
                        act.wait_ge(turned2, HG * q + g + 1)
                        if g >= 2:
                            act.wait_ge(pixels, NCH * q + (g - 1) * 4 // per)
                        act.copy(tt[g % 2][:], ps[4 + g % 2][:]).then_inc(turned2_read, 1)


def l1_edge_stage(pr, edge):
    nc, ps = pr.nc, pr.psum
    const, ready, window, meant = (pr.sem(f"e1_{n}") for n in ("const", "ready", "window", "meant"))
    seq, root, picked, spread = (pr.sem(f"e1_{n}") for n in ("seq", "root", "picked", "spread"))
    zeroed = pr.sem("e1_zeroed")
    HALO = ROWS + 2
    with ExitStack() as ctx:
        src = pr.sb(ctx, "e1_src", [P, PIX])
        wide = pr.sb(ctx, "e1_wide", [P, 264])
        wq = pr.sb(ctx, "e1_wq", [P, 252])
        pick = pr.sb(ctx, "e1_pick", [P, P])
        spread_m = pr.sb(ctx, "e1_spread_m", [B, Q * P])
        m = pr.sb(ctx, "e1_m", [P, HALO, N + 2])
        d = pr.sb(ctx, "e1_d", [P, HALO, N])
        v = pr.sb(ctx, "e1_v", [P, HALO, N])
        g1, g2 = pr.sb(ctx, "e1_g1", [P, ROWS, N]), pr.sb(ctx, "e1_g2", [P, ROWS, N])
        es = pr.sb(ctx, "e1_es", [P, PS])
        eb = pr.sb(ctx, "e1_eb", [B, N])
        lo = pr.sb(ctx, "e1_lo", [B, 4])
        sq_eps = pr.sb(ctx, "e1_eps", [P, 1])
        rows_src = src[:].rearrange("p (h w) -> p h w", w=N)
        with nc.Block() as block:
            @block.sync
            def _(sp):
                for t, n in ((wide, "l1_mean"), (pick, "l1_pick"), (spread_m, "l1_spread")):
                    sp.dma_start(t[:], pr.ins[n]).then_inc(const, 16)

            @block.scalar
            def _(act):
                with act.Fori(0, Q) as q:
                    act.wait_ge(meant, q)
                    for j in range(NCH):
                        pr.normalise(act, src, q, j, ready)
                act.wait_ge(seq, 10)
                act.activation(g1[:], g2[:], ACT.Sqrt, bias=sq_eps[:, 0:1]).then_inc(root, 1)

            @block.tensor
            def _(pe):
                pe.wait_ge(const, 48)
                pe.wait_ge(window, 1)
                pe.wait_ge(ready, NCH)
                pe.matmul(ps[0][:], wide[:, 0:P], src[:, 0:CH], start=True, stop=False, skip_group_check=True)
                pe.matmul(ps[1][:, 0:P], wide[:, 0:P], src[:, 0:P], start=True, stop=False, skip_group_check=True)
                with pe.Fori(0, Q) as q:
                    pe.wait_ge(window, q + 1)
                    pe.wait_ge(ready, NCH * q + NCH)
                    for s in range(NCH):
                        at = 124 - B * s
                        w = wq[:, at:at + P]
                        pe.matmul(ps[0][:], w, src[:, s * CH:(s + 1) * CH], start=False, stop=False,
                                  skip_group_check=True)
                        if s > 0:
                            pe.matmul(ps[1][:, 0:N], w, rows_src[:, ROWS * s - 1, :], start=False, stop=False,
                                      skip_group_check=True)
                        if s < NCH - 1:
                            last = pe.matmul(ps[1][:, N:2 * N], w, rows_src[:, ROWS * s + ROWS, :], start=False,
                                             stop=False, skip_group_check=True)
                        else:
                            last = pe.matmul(ps[1][:, N:2 * N], wide[:, 0:P], src[:, 0:N], start=False,
                                             stop=False, skip_group_check=True)
                    last.then_inc(meant, 1)
                pe.wait_ge(seq, 11)
                for s in range(PS):
                    last = pe.matmul(ps[2][0:B, s * PS:(s + 1) * PS], pick[:, B * s:B * s + B], es[:],
                                     start=True, stop=True)
                last.then_inc(picked, 1)
                pe.wait_ge(seq, 18)
                for q in range(Q):
                    last = pe.matmul(ps[3][:, q * N:(q + 1) * N], spread_m[:, q * P:(q + 1) * P], eb[:],
                                     start=True, stop=True)
                last.then_inc(spread, 1)

            @block.vector
            def _(dve):
                count = [0]

                def then(ins):
                    count[0] += 1
                    ins.then_inc(seq, 1)
                    dve.wait_ge(seq, count[0])

                dve.memset(m[:], 0.0).then_inc(zeroed, 1)
                dve.memset(sq_eps[:], 1e-6).then_inc(zeroed, 1)
                dve.wait_ge(const, 48)
                with dve.Fori(0, Q) as q:
                    dve.wait_ge(meant, q)
                    dve.tensor_copy(wq[:], wide[:, bass.ds(12 - IB * q, 252)]).then_inc(window, 1)
                dve.wait_ge(meant, Q)
                dve.wait_ge(zeroed, 2)
                dve.tensor_copy(m[:, 1:1 + ROWS, 1:1 + N], ps[0][:].rearrange("p (h w) -> p h w", w=N))
                then(dve.tensor_copy(m[:, 0:HALO:HALO - 1, 1:1 + N],
                                     ps[1][:, 0:2 * N].rearrange("p (h w) -> p h w", w=N)))
                dve.scalar_tensor_tensor(v[:], m[:, :, 1:1 + N], 2.0, m[:, :, 0:N], ALU.mult, ALU.add)
                then(dve.tensor_tensor(d[:], m[:, :, 2:2 + N], m[:, :, 0:N], ALU.subtract))
                then(dve.tensor_tensor(v[:], v[:], m[:, :, 2:2 + N], ALU.add))
                then(dve.scalar_tensor_tensor(g1[:], d[:, 1:1 + ROWS], 2.0, d[:, 0:ROWS], ALU.mult, ALU.add))
                then(dve.tensor_tensor(g1[:], g1[:], d[:, 2:2 + ROWS], ALU.add))
                then(dve.tensor_tensor(g2[:], v[:, 2:2 + ROWS], v[:, 0:ROWS], ALU.subtract))
                then(dve.tensor_tensor(g2[:], g2[:], g2[:], ALU.mult))
                then(dve.tensor_tensor(g1[:], g1[:], g1[:], ALU.mult))
                then(dve.tensor_tensor(g2[:], g2[:], g1[:], ALU.add))
                then(dve.memset(lo[:], 0.0))
                dve.wait_ge(root, 1)
                then(dve.tensor_reduce(es[:], g1[:].rearrange("p y (c x) -> p c y x", x=PS), AX.XY, ALU.add))
                dve.wait_ge(picked, 1)
                then(dve.tensor_scalar(eb[:], ps[2][0:B, 0:N], 1.0 / (PS * PS), None, ALU.mult))
                then(dve.tensor_reduce(lo[:, 0:1], eb[:], AX.X, ALU.min))
                then(dve.tensor_scalar(eb[:], eb[:], lo[:, 0:1], None, ALU.subtract))
                then(dve.tensor_reduce(lo[:, 1:2], eb[:], AX.X, ALU.max))
                then(dve.tensor_scalar(lo[:, 2:3], lo[:, 1:2], 1e-6, None, ALU.add))
                then(dve.reciprocal(lo[:, 3:4], lo[:, 2:3]))
                then(dve.tensor_scalar(eb[:], eb[:], lo[:, 3:4], 0.5, ALU.mult, ALU.mult))
                dve.wait_ge(spread, 1)
                dve.tensor_copy(edge[:].rearrange("p q n -> p (q n)"), ps[3][:, 0:Q * N])


def l1_filter_stage(pr, edge):
    nc, ps = pr.nc, pr.psum
    const, ready, mask, turned = (pr.sem(f"p1_{n}") for n in ("const", "ready", "mask", "turned"))
    turned_read, filtered, added, scaled = (pr.sem(f"p1_{n}") for n in ("turned_read", "filtered", "added", "scaled"))
    finished, step, mats = (pr.sem(f"p1_{n}") for n in ("finished", "step", "mats"))
    with ExitStack() as ctx:
        src = pr.sb(ctx, "p1_src", [P, PIX])
        tt = [pr.sb(ctx, f"p1_tt{p}", [P, CH]) for p in range(2)]
        tmp = [pr.sb(ctx, f"p1_tmp{p}", [P, PS, PS * PS]) for p in range(2)]
        dft, same = pr.sb(ctx, "p1_dft", [P, P]), pr.sb(ctx, "p1_same", [P, P])
        band, gain = pr.sb(ctx, "p1_band", [NB, P]), pr.sb(ctx, "p1_gain", [NB, 1])
        high, mk = pr.sb(ctx, "p1_high", [P, 1]), pr.sb(ctx, "p1_mk", [P, 2])
        md = pr.sb(ctx, "p1_md", [P, 2, P])
        mm = pr.sb(ctx, "p1_mm", [P, 2, P])
        with nc.Block() as block:
            @block.sync
            def _(sp):
                for t, n in ((dft, "l1_dft"), (same, "l1_same"), (band, "l1_band"), (high, "l1_high")):
                    sp.dma_start(t[:], pr.ins[n]).then_inc(const, 16)
                sp.dma_start(gain[:], pr.ins["L1_conv_gain"].rearrange("a n -> n a")).then_inc(const, 16)

            @block.tensor
            def _(pe):
                pe.wait_ge(const, 80)
                pe.matmul(ps[2][:, 0:1], band[:], gain[:], start=True, stop=True).then_inc(mask, 1)
                pe.wait_ge(mats, 4)
                pe.matmul(ps[3][:, 0:2 * P], dft[:], md[:].rearrange("p t n -> p (t n)"), start=True,
                          stop=True).then_inc(mask, 1)
                pe.wait_ge(mats, 6)
                with pe.Fori(0, Q) as q:
                    def turn(j):
                        pe.wait_ge(ready, NCH * q + j + 1)
                        if j >= 2:
                            pe.wait_ge(turned_read, NCH * q + j - 1)
                        for k in range(4):
                            m = pe.transpose(ps[j % 2][:, k * P:(k + 1) * P],
                                             src[:, (4 * j + k) * P:(4 * j + k + 1) * P], pr.ident[:])
                        m.then_inc(turned, 1)

                    turn(0)
                    for j in range(NCH):
                        if j + 1 < NCH:
                            turn(j + 1)
                        pe.wait_ge(turned_read, NCH * q + j + 1)
                        if j == 0:
                            pe.wait_ge(added, NCH * q)
                        if j >= 2:
                            pe.wait_ge(added, NCH * q + j - 1)
                        for t in range(2):
                            for k in range(4):
                                m = pe.matmul(ps[2 + 2 * (j % 2) + t][:, k * P:(k + 1) * P],
                                              tt[j % 2][:, k * P:(k + 1) * P], mm[:, t, :], start=True, stop=True)
                        m.then_inc(filtered, 1)

            @block.scalar
            def _(act):
                with act.Fori(0, Q) as q:
                    act.wait_ge(turned, NCH * q)
                    for j in range(2):
                        pr.normalise(act, src, q, j, ready, True)
                    for j in range(NCH):
                        act.wait_ge(turned, NCH * q + j + 1)
                        if j >= 2:
                            act.wait_ge(filtered, NCH * q + j - 1)
                        act.copy(tt[j % 2][:], ps[j % 2][:]).then_inc(turned_read, 1)
                        if j + 2 < NCH:
                            pr.normalise(act, src, q, j + 2, ready, True)

            @block.vector
            def _(dve):
                dve.wait_ge(mask, 1)
                dve.tensor_scalar(mk[:, 0:1], ps[2][:, 0:1], 0.0, None, ALU.max).then_inc(mats, 1)
                dve.wait_ge(mats, 1)
                dve.wait_ge(const, 80)
                dve.tensor_tensor(mk[:, 1:2], mk[:, 0:1], high[:], ALU.mult).then_inc(mats, 1)
                dve.wait_ge(mats, 2)
                for t in range(2):
                    dve.tensor_scalar(md[:, t, :], dft[:], mk[:, t:t + 1], None, ALU.mult).then_inc(mats, 1)
                dve.wait_ge(mask, 2)
                for t in range(2):
                    dve.tensor_tensor(mm[:, t, :], ps[3][:, t * P:(t + 1) * P], same[:], ALU.mult).then_inc(mats, 1)
                with dve.Fori(0, Q) as q:
                    for j in range(NCH):
                        dve.wait_ge(filtered, NCH * q + j + 1)
                        if j >= 2:
                            dve.wait_ge(finished, NCH * q + j - 1)
                        elif j == 0:
                            dve.wait_ge(finished, NCH * q)
                        dve.tensor_tensor(tmp[j % 2][:], ps[3 + 2 * (j % 2)][:].rearrange("p (a b) -> p a b", a=PS),
                                          edge[:, q, PS * j:PS * j + PS].unsqueeze(2).broadcast_to([P, PS, PS * PS]),
                                          ALU.mult).then_inc(scaled, 1)
                        x = pr.X[:, q, j * CH:(j + 1) * CH].rearrange("p (y a x) -> p a y x", y=PS, x=PS)
                        dve.tensor_tensor(x, x, ps[2 + 2 * (j % 2)][:].rearrange("p (a y x) -> p a y x", a=PS, x=PS),
                                          ALU.add).then_inc(added, 1)
                    dve.wait_ge(finished, NCH * q + NCH)
                    pr.image_stats(dve, q, step, 3 * q)

            @block.gpsimd
            def _(pool):
                with pool.Fori(0, Q) as q:
                    for j in range(NCH):
                        pool.wait_ge(scaled, NCH * q + j + 1)
                        pool.wait_ge(added, NCH * q + j + 1)
                        x = pr.X[:, q, j * CH:(j + 1) * CH].rearrange("p (y a x) -> p a y x", y=PS, x=PS)
                        pool.tensor_tensor(x, x, tmp[j % 2][:].rearrange("p a (y x) -> p a y x", x=PS),
                                           ALU.add).then_inc(finished, 1)


def l2_stage(pr):
    nc, ps = pr.nc, pr.psum
    wl, zero, placed, ready = (pr.sem(f"c2_{n}") for n in ("weights", "zero", "placed", "ready"))
    moved, padded, conv, added = (pr.sem(f"c2_{n}") for n in ("moved", "padded", "conv", "added"))
    step = pr.sem("c2_step")
    G = 8
    HG = N // 4 // G
    with ExitStack() as ctx:
        src = pr.sb(ctx, "c2_src", [P, N, N])
        R = pr.sb(ctx, "c2_r", [P, Q, IB, RB, PW])
        wn = pr.sb(ctx, "c2_wn", [P, C, KS * KS])
        wt = pr.sb(ctx, "c2_wt", [P, 2, KS, 4, C])
        edge_rows = [(0, 0, 1), (1, RB - 1, N - 2), (2, RB - 1, N - 3), (3, RB - 1, 2)]
        moves = IB * 8
        with nc.Block() as block:
            @block.sync
            def _(sp):
                w = pr.ins["L2_conv_weight"].rearrange("o c y x -> c o (y x)")
                for i in range(4):
                    sp.dma_start(wn[i * C:(i + 1) * C], w).then_inc(wl, 16)
                with sp.Fori(0, Q) as q:
                    sp.wait_ge(ready, NCH * q + NCH)
                    for b in range(IB):
                        at = slice(b * C, (b + 1) * C)
                        for r in range(4):
                            first = 1 if r == 0 else 0
                            n = RB - 1
                            h = 4 * first + r - 1
                            sp.dma_start(R[r * C:(r + 1) * C, q, b, first:first + n, 1:1 + N],
                                         src[at, h:h + 4 * n - 3:4, :]).then_inc(moved, 16)
                        for r, k, h in edge_rows:
                            sp.dma_start(R[r * C:(r + 1) * C, q, b, k, 1:1 + N], src[at, h, :]).then_inc(moved, 16)

            @block.scalar
            def _(act):
                flat = src[:].rearrange("p h w -> p (h w)")
                with act.Fori(0, Q) as q:
                    act.wait_ge(moved, 16 * moves * q)
                    for j in range(NCH):
                        pr.normalise(act, flat, q, j, ready)

            @block.gpsimd
            def _(pool):
                with pool.Fori(0, Q) as q:
                    pool.wait_ge(moved, 16 * moves * q + 16 * moves)
                    r = R[:, q].rearrange("p b k w -> p (b k) w")
                    for to, of in ((0, 2), (N + 1, N - 1), (N + 2, N - 2), (N + 3, 3)):
                        pool.tensor_copy(r[:, :, to:to + 1], r[:, :, of:of + 1]).then_inc(padded, 1)

            @block.tensor
            def _(pe):
                pe.wait_ge(placed, 20)
                with pe.Fori(0, Q) as q:
                    pe.wait_ge(padded, 4 * q + 4)
                    for n in range(IB * HG):
                        b, half = n // HG, n % HG
                        if n >= 4:
                            pe.wait_ge(added, 32 * q + 4 * (n - 3))
                        elif n == 0:
                            pe.wait_ge(added, 32 * q)
                        for k in range(2):
                            for x in range(KS):
                                m = pe.matmul(ps[n % 4][:], wt[:, k, x].rearrange("p o c -> p (o c)"),
                                              R[:, q, b, G * half + k:G * half + k + G, 4 - x:4 - x + N],
                                              start=(k == 0 and x == 0), stop=(k == 1 and x == KS - 1))
                        m.then_inc(conv, 1)

            @block.vector
            def _(dve):
                dve.memset(wt[:], 0.0).then_inc(zero, 1)
                dve.wait_ge(zero, 1)
                dve.wait_ge(wl, 64)
                for i in range(4):
                    for k in range(2):
                        for o in range(4):
                            jy = o + 4 - 4 * k - i
                            if 0 <= jy < KS:
                                at = slice(i * C, (i + 1) * C)
                                dve.tensor_copy(wt[at, k, :, o, :],
                                                 wn[at, :, jy * KS:(jy + 1) * KS].rearrange("c o x -> c x o")
                                                 ).then_inc(placed, 1)
                with dve.Fori(0, Q) as q:
                    for n in range(IB * HG):
                        b, half = n // HG, n % HG
                        dve.wait_ge(conv, 8 * q + n + 1)
                        for o in range(4):
                            x = pr.X[b * C:(b + 1) * C, q, :].rearrange("p (g o w) -> p g o w", o=4, w=N)[
                                :, G * half:G * half + G, o, :]
                            dve.tensor_tensor(x, ps[n % 4][o * C:(o + 1) * C, :].rearrange("p (g w) -> p g w", w=N), x,
                                              ALU.add).then_inc(added, 1)
                    dve.wait_ge(added, 32 * q + 32)
                    pr.image_stats(dve, q, step, 3 * q)


def l3_forward_stage(pr, xm):
    nc, ps = pr.nc, pr.psum
    const, ready, turned, turned_read = (pr.sem(f"f3_{n}") for n in ("const", "ready", "turned", "turned_read"))
    made, made_read = pr.sem("f3_made"), pr.sem("f3_made_read")
    with ExitStack() as ctx:
        src = pr.sb(ctx, "f3_src", [P, PIX])
        tt = [pr.sb(ctx, f"f3_tt{p}", [P, CH]) for p in range(2)]
        cols = pr.sb(ctx, "f3_cols", [P, IB, SLOT, C])
        fw, fh, fh0 = (pr.sb(ctx, f"f3_{n}", [P, P]) for n in ("fw", "fh", "fh0"))
        with nc.Block() as block:
            @block.sync
            def _(sp):
                for t, n in ((fw, "l3_fw"), (fh, "l3_fh"), (fh0, "l3_fh0")):
                    sp.dma_start(t[:], pr.ins[n]).then_inc(const, 16)

            @block.tensor
            def _(pe):
                pe.wait_ge(const, 48)
                with pe.Fori(0, Q) as q:
                    forward_products(pe, pr, src, tt, cols, fw, fh, fh0, 16 * q, turned, turned_read, made,
                                     made_read, ready, NCH * q)

            @block.vector
            def _(dve):
                with dve.Fori(0, Q) as q:
                    copy_turned(dve, ps, tt, cols, 16 * q, turned, turned_read, made)

            @block.scalar
            def _(act):
                with act.Fori(0, Q) as q:
                    act.wait_ge(turned, 16 * q)
                    for j in range(2):
                        pr.normalise(act, src, q, j, ready)

                    def ahead(j):
                        if j + 2 < NCH:
                            pr.normalise(act, src, q, j + 2, ready)

                    copy_rows(act, ps, src, 16 * q, made, made_read, ahead)
                    for s in range(SLOT // 4):
                        act.wait_ge(made, 16 * q + NCH + s + 1)
                        act.copy(xm[:, s, :, :, bass.ds(IB * q, IB)].rearrange("p k r b -> p b (k r)"),
                                 ps[2 + s % 2][:].rearrange("p (b k) -> p b k", b=IB)).then_inc(made_read, 1)


def l3_mix_stage(pr, xm):
    nc, ps = pr.nc, pr.psum
    SG = SLOT // 4
    loaded = [pr.sem(f"m3_load{p}") for p in range(2)]
    staged, mixed, mixed_read, fix = (pr.sem(f"m3_{n}") for n in ("staged", "mixed", "mixed_read", "fix"))
    H = N // 2
    with ExitStack() as ctx:
        kf = [pr.sb(ctx, f"m3_kf{p}", [P, C, N, 2]) for p in range(2)]
        xp = [pr.sb(ctx, f"m3_xp{p}", [P, N, 4, B]) for p in range(2)]
        with nc.Block() as block:
            @block.sync
            def _(sp):
                with sp.Fori(0, SG // 2) as i:
                    for p in range(2):
                        sp.wait_ge(mixed, 4 * i)
                        sp.dma_start(kf[p][:].rearrange("p o k r -> p (o k r)"), pr.kf[2 * i + p].rearrange("p t n -> p (t n)")
                                     ).then_inc(loaded[p], 16)

            def stage(eng, s, p):
                eng.tensor_copy(xp[p][:, :, 0:2, :], xm[:, s, :, :, :]).then_inc(staged, 1)
                eng.tensor_copy(xp[p][:, :, 3, :], xm[:, s, :, 0, :]).then_inc(staged, 1)
                eng.tensor_tensor(xp[p][:, :, 2, :], pr.zero[:].unsqueeze(2).broadcast_to([P, N, B]),
                                  xm[:, s, :, 1, :], ALU.subtract).then_inc(staged, 1)

            @block.gpsimd
            def _(pool):
                for p in range(2):
                    stage(pool, p, p)
                pool.wait_ge(staged, 6)
                pool.memset(xp[0][0:C, 0:N:H, 1:3, :], 0.0).then_inc(fix, 1)
                pool.tensor_copy(xp[0][0:C, 0:N:H, 3, :], xm[0:C, 0, 0:N:H, 1, :]).then_inc(fix, 1)
                with pool.Fori(1, SG // 2) as i:
                    for p in range(2):
                        pool.wait_ge(mixed, 4 * i + 2 * p - 2)
                        stage(pool, 2 * i + p, p)

            @block.tensor
            def _(pe):
                pe.wait_ge(fix, 2)
                with pe.Fori(0, SG // 2) as i:
                    for p in range(2):
                        pe.wait_ge(loaded[p], 16 * i + 16)
                        pe.wait_ge(staged, 6 * i + 3 * p + 3)
                        for half in range(2):
                            bank = 4 * half
                            pe.wait_ge(mixed_read, 16 * i + 8 * p)
                            pe.sem_inc(pr.pace, 1)
                            for n in range(H):
                                for w in range(4):
                                    m = (n + 8 * w) % H
                                    k = H * half + m
                                    at = slice(w * C, (w + 1) * C)
                                    to = ps[bank + m // 8][at, m % 8 * 2 * B:(m % 8 + 1) * 2 * B]
                                    pe.matmul(to, kf[p][at, :, k, 0], xp[p][at, k, 0:2, :], start=True, stop=False)
                                    last = pe.matmul(to, kf[p][at, :, k, 1], xp[p][at, k, 2:4, :], start=False,
                                                     stop=True)
                            last.then_inc(mixed, 1)

            def copy_out(eng, copy, banks):
                with eng.Fori(0, SG // 2) as i:
                    for p in range(2):
                        for half in range(2):
                            eng.wait_ge(mixed, 4 * i + 2 * p + half + 1)
                            eng.wait_ge(staged, 6 * i + 3 * p + 3)
                            for m in banks:
                                copy(xm[:, 2 * i + p, H * half + 8 * m:H * half + 8 * m + 8].rearrange(
                                    "p k r b -> p (k r b)"), ps[4 * half + m][:, 0:256]).then_inc(mixed_read, 1)

            @block.vector
            def _(dve):
                copy_out(dve, dve.tensor_copy, (0, 1))

            @block.scalar
            def _(act):
                copy_out(act, act.copy, (2, 3))


def four_layers(nc, ins, out, stop=None):
    with ExitStack() as ctx:
        pr = Program(nc, ctx, ins, out)
        kernel_spectra_stage(pr)
        pr.stats_stage("n0")
        with ExitStack() as layer:
            xm0 = pr.sb(layer, "xm0", [P, KT // 4, KX, 3, B])
            l0_forward_stage(pr, xm0)
            with ExitStack() as inner:
                y0 = pr.sb(inner, "y0", [P, KT // 4, KX, 2, B])
                l0_mix_stage(pr, xm0, y0)
                inverse_stage(pr, "i0", y0, KT, KX, "l0_ih", "l0_ih", "l0_iw", 4, False)
        if stop == 0: return dump(pr)
        pr.stats_stage("n1")
        with ExitStack() as layer:
            edge = pr.sb(layer, "edge", [P, Q, N])
            l1_edge_stage(pr, edge)
            l1_filter_stage(pr, edge)
        if stop == 1: return dump(pr)
        pr.stats_stage("n2")
        l2_stage(pr)
        if stop == 2: return dump(pr)
        pr.stats_stage("n3")
        with ExitStack() as layer:
            xm = pr.sb(layer, "xm", [P, SLOT // 4, N, 2, B])
            l3_forward_stage(pr, xm)
            l3_mix_stage(pr, xm)
            inverse_stage(pr, "i3", xm, SLOT, N, "l3_ih", "l3_ih0", "l3_iw", 2, True)


def dump(pr):
    s = pr.sem("dump")
    with pr.nc.Block() as block:
        @block.sync
        def _(sp):
            og = pr.out.rearrange("(q b) c h w -> q (b c) (h w)", b=IB)
            for q in range(Q):
                sp.dma_start(og[q], pr.X[:, q, :]).then_inc(s, 16)
            sp.wait_ge(s, 64)


_INS = ["x", "L0_conv_weights_r", "L0_conv_weights_i", "L1_conv_gain", "L2_conv_weight", "L3_conv_weights"]


def kernel(**inputs):
    import concourse.bacc as bacc
    from concourse.bass_utils import run_bass_kernel_spmd

    nc = bacc.Bacc("TRN2", target_bir_lowering=False, num_devices=1)
    arrays = {n: np.ascontiguousarray(inputs[n]) for n in _INS} | constants()
    ins = {n: nc.dram_tensor(f"in_{n}", a.shape, F32, kind="ExternalInput").ap() for n, a in arrays.items()}
    out = nc.dram_tensor("out_y", (B, C, N, N), F32, kind="ExternalOutput").ap()
    four_layers(nc, ins, out)
    r = run_bass_kernel_spmd(nc, [{f"in_{n}": a for n, a in arrays.items()}], core_ids=[0])
    return r.results[0]["out_y"]
```

```python
from contextlib import ExitStack

import numpy as np

import concourse.bass as bass
from concourse import mybir

F32 = mybir.dt.float32
F16 = mybir.dt.float16
I32 = mybir.dt.int32
ALU = mybir.AluOpType
ACT = mybir.ActivationFunctionType
AX = mybir.AxisListType

B, C, N = 16, 32, 64
P = 128
Q = B * C // P
IB = P // C
PIX = N * N
CH = 512
NCH = PIX // CH
ROWS = CH // N
SLOT = N // 2
KT = 16
K2 = 8
BAND = 50
L0_BLOCKS = [list(range(0, N - BAND - K2)), list(range(BAND, N - K2)), list(range(N - K2, N)),
             list(range(N - BAND - K2, N - BAND))]
L0_OFF = [0, 6, 12, 20]
KX = sum(len(b) for b in L0_BLOCKS)
PS = 8
NB = 6
KS = 5
RB = N // 4 + 1
PW = N + KS - 1
GN_EPS = 1e-5
START = 32


def constants():
    f = np.float64
    ang = 2 * np.pi / N
    n = np.arange(N)
    out = {}
    out["ident"] = np.eye(P)
    out["pair"] = np.kron(np.eye(P // 2), np.full((2, 2), 0.5))

    def two(m, k=2):
        return np.kron(np.eye(k), m)

    kt = np.arange(KT)
    fw = np.stack([np.cos(ang * np.outer(n, kt)), -np.sin(ang * np.outer(n, kt))], 1)
    out["l0_fw"] = two(fw.reshape(N, 2 * KT))
    kx = np.array(sum(L0_BLOCKS, []))
    out["l0_fh"] = complex_matrix(n, kx, -1.0)
    out["l0_ih"] = np.concatenate([complex_matrix(kx, n, 1.0) / N, np.zeros((P - 2 * KX, P))])
    iw = np.stack([np.cos(ang * np.outer(kt, n)), -np.sin(ang * np.outer(kt, n))], 1) * 2 / N
    iw[0] /= 2
    iw[0, 1] = 0
    out["l0_iw"] = two(iw.reshape(2 * KT, N), 4)

    s = np.arange(SLOT)
    fw = np.stack([np.cos(ang * np.outer(n, s)), -np.sin(ang * np.outer(n, s))], 1)
    fw[:, 1, 0] = (-1.0) ** n
    out["l3_fw"] = two(fw.reshape(N, 2 * SLOT))
    out["l3_fh"] = complex_matrix(n, n, -1.0).reshape(P, N, 2).transpose(0, 2, 1).reshape(P, P)
    out["l3_ih"] = complex_matrix(n, n, 1.0) / N
    iw = np.stack([np.cos(ang * np.outer(s, n)), -np.sin(ang * np.outer(s, n))], 1) * 2 / N
    iw[0, 0] = 1.0 / N
    iw[0, 1] = (-1.0) ** n / N
    out["l3_iw"] = two(iw.reshape(2 * SLOT, N))
    f0 = np.zeros((N, 2, N, 2))
    i0 = np.zeros((N, 2, N, 2))
    for half in range(2):
        for m in range(SLOT):
            at = half * SLOT + m
            if m:
                f0[:, half, at, 0], f0[:, half, at, 1] = np.cos(ang * n * m), -np.sin(ang * n * m)
                i0[at, 0, :, half], i0[at, 1, :, half] = 2 * np.cos(ang * n * m) / N, -2 * np.sin(ang * n * m) / N
            else:
                f0[:, half, at, 0], f0[:, half, at, 1] = 1.0, (-1.0) ** n
                i0[at, 0, :, half], i0[at, 1, :, half] = 1.0 / N, (-1.0) ** n / N
    out["l3_fh0"] = f0.transpose(0, 1, 3, 2).reshape(P, P)
    out["l3_ih0"] = i0.reshape(P, P)

    k = np.arange(PS)
    y = np.repeat(k, PS)
    x = np.tile(k, PS)
    th = 2 * np.pi / PS * (np.outer(y, y) + np.outer(x, x))
    d = np.concatenate([np.cos(th), np.sin(th)], 0) / PS
    out["l1_dft"] = np.concatenate([d, d], 1)
    out["l1_same"] = np.kron(np.eye(2), np.ones((PS * PS, PS * PS)))
    ky = np.minimum(y, PS - y).astype(np.float32)
    kx8 = np.minimum(x, PS - x).astype(np.float32)
    r = np.sqrt(ky ** 2 + kx8 ** 2).astype(np.float32)
    r = np.clip(r / np.float32(np.sqrt(2.0 * (PS // 2) ** 2) + 1e-08), 0, 1).astype(f)
    centers = np.linspace(0.0, 1.0, NB)
    w = np.maximum(1.0 - np.abs(r[None] - centers[:, None]) / (1.0 / (NB - 1)), 0)
    w = w / (w.sum(0, keepdims=True) + 1e-08)
    out["l1_band"] = np.concatenate([w, w], 1)
    out["l1_high"] = np.concatenate([(r >= 0.6), (r >= 0.6)]).astype(f)[:, None]
    wide = np.zeros((P, 12 + 124 + IB + 124))
    for b in range(IB):
        wide[b * C:(b + 1) * C, 12 + 124 + b] = 1.0 / C
    out["l1_mean"] = wide
    out["l1_pick"] = np.stack([np.eye(P)[:, 16 * s:16 * s + 16] for s in range(PS)], 1).reshape(P, P)
    out["l1_spread"] = np.concatenate([np.kron(np.eye(B)[:, IB * q:IB * q + IB], np.ones((1, C)))
                                       for q in range(Q)], 1)
    return {k: np.ascontiguousarray(v, np.float32) for k, v in out.items()}


def complex_matrix(a, b, sign):
    th = 2 * np.pi / N * np.outer(a, b)
    c, s = np.cos(th), sign * np.sin(th)
    m = np.stack([np.stack([c, s], -1), np.stack([-s, c], -1)], 1)
    return m.reshape(2 * len(a), 2 * len(b))


class Program:

    def __init__(self, nc, ctx, ins, out):
        self.nc, self.ins, self.out, self.names = nc, ins, out, set()
        self.ctx = ctx
        self.X = self.sb(ctx, "X", [P, Q, PIX])
        self.ident = self.sb(ctx, "ident", [P, P])
        self.pair = self.sb(ctx, "pair", [P, P])
        self.bn = self.sb(ctx, "bn", [P, NCH, 6])
        self.mv = self.sb(ctx, "mv", [P, 2])
        self.st = self.sb(ctx, "st", [P, Q, 2])
        self.gm = self.sb(ctx, "gm", [P, Q, 2])
        self.var = self.sb(ctx, "var", [P, Q])
        self.sd = self.sb(ctx, "sd", [P, Q])
        self.rstd = self.sb(ctx, "rstd", [P, Q])
        self.shift = self.sb(ctx, "shift", [P, Q])
        self.eps = self.sb(ctx, "eps", [P, 2])
        self.psum = [ctx.enter_context(nc.psum_tensor(f"bank{i}", [P, CH], F32)) for i in range(8)]
        self.zero = self.sb(ctx, "zero", [P, 1])
        self.pace = self.sem("pace")
        self.kf = nc.dram_tensor("kf", (SLOT // 4, P, 2, C // IB, IB * N), F32, kind="Internal").ap()
        self.xf = nc.dram_tensor("xf", (Q, 2, C, KT, KX * 2 * IB), F32, kind="Internal").ap()

    def sb(self, ctx, name, shape, dt=F32):
        return ctx.enter_context(self.nc.sbuf_tensor(name, shape, dt))

    def sem(self, name):
        assert name not in self.names
        self.names.add(name)
        return self.ctx.enter_context(self.nc.semaphore(name))


    def chunk_stats(self, dve, q, c, step):
        dve.sem_inc(self.pace, 1)
        dve.bn_stats(self.bn[:, c, :], self.X[:, q, c * CH:(c + 1) * CH]).then_inc(step, 1)

    def group_stats(self, dve, q, step):
        at = (NCH + 2) * q
        dve.wait_ge(step, at + NCH)
        dve.sem_inc(self.pace, 1)
        dve.bn_aggr(self.mv[:], self.bn[:].rearrange("p a b -> p (a b)")).then_inc(step, 1)
        dve.wait_ge(step, at + NCH + 1)
        dve.tensor_copy(self.st[:, q, 0:1], self.mv[:, 0:1])
        dve.scalar_tensor_tensor(self.st[:, q, 1:2], self.mv[:, 0:1], self.mv[:, 0:1], self.mv[:, 1:2],
                                 ALU.mult, ALU.add).then_inc(step, 1)
        dve.wait_ge(step, at + NCH + 2)

    def stats_stage(self, name):
        summed, read, deviation, done = (self.sem(f"{name}_{x}") for x in ("sum", "var", "dev", "norm"))
        gm, sm = self.gm, self.psum[0]
        with self.nc.Block() as block:
            @block.tensor
            def _(pe):
                pe.matmul(sm[:, 0:2 * Q], self.pair[:], self.st[:].rearrange("p q t -> p (q t)"),
                          start=True, stop=True).then_inc(summed, 1)

            @block.scalar
            def _(act):
                act.wait_ge(read, 4)
                act.activation(self.sd[:], self.var[:], ACT.Sqrt, bias=self.eps[:, 0:1]).then_inc(deviation, 1)

            @block.vector
            def _(dve):
                dve.wait_ge(summed, 1)
                dve.tensor_copy(gm[:].rearrange("p q t -> p (q t)"), sm[:, 0:2 * Q]).then_inc(read, 1)
                dve.wait_ge(read, 1)
                dve.tensor_tensor(self.var[:], gm[:, :, 0], gm[:, :, 0], ALU.mult).then_inc(read, 1)
                dve.wait_ge(read, 2)
                dve.tensor_tensor(self.var[:], gm[:, :, 1], self.var[:], ALU.subtract).then_inc(read, 1)
                dve.wait_ge(read, 3)
                dve.tensor_scalar(self.var[:], self.var[:], 0.0, None, ALU.max).then_inc(read, 1)
                dve.wait_ge(deviation, 1)
                dve.reciprocal(self.rstd[:], self.sd[:]).then_inc(done, 1)
                dve.wait_ge(done, 1)
                dve.scalar_tensor_tensor(self.shift[:], gm[:, :, 0], -1.0, self.rstd[:], ALU.mult, ALU.mult)

    def normalise(self, act, dst, q, c, ready, patches=False):
        to, of = dst[:, c * CH:(c + 1) * CH], self.X[:, q, c * CH:(c + 1) * CH]
        if patches:
            to = to.rearrange("p (a y x) -> p a y x", a=PS, x=PS)
            of = of.rearrange("p (y a x) -> p a y x", y=PS, x=PS)
        act.activation(to, of, ACT.Identity,
                       scale=self.rstd[:, bass.ds(q, 1)], bias=self.shift[:, bass.ds(q, 1)]).then_inc(ready, 1)


def load_constant(pr, ctx, eng, sem, name, shape):
    t = pr.sb(ctx, name, shape)
    eng.append((t, pr.ins[name]))
    return t


def kernel_spectra_stage(pr):
    nc, ps = pr.nc, pr.psum
    tiles = C // IB
    const, loaded = pr.sem("ks_const"), [[pr.sem(f"ks_load{p}{k}") for k in range(4)] for p in range(2)]
    x_loaded = pr.sem("ks_x")
    turned, turned_read = pr.sem("ks_turned"), pr.sem("ks_turned_read")
    made, made_read = pr.sem("ks_made"), pr.sem("ks_made_read")
    stored, step, eps = pr.sem("ks_stored"), pr.sem("ks_step"), pr.sem("ks_eps")
    w_tiles = pr.ins["L3_conv_weights"].rearrange("(t o) c h w -> t (o c) (h w)", o=IB)
    x_groups = pr.ins["x"].rearrange("(q b) c h w -> q (b c) (h w)", b=IB)
    with ExitStack() as ctx:
        src = [pr.sb(ctx, f"ks_src{p}", [P, PIX]) for p in range(2)]
        tt = [pr.sb(ctx, f"ks_tt{p}", [P, CH]) for p in range(4)]
        cols = pr.sb(ctx, "ks_cols", [P, IB, SLOT, C])
        spec = pr.sb(ctx, "ks_spec", [P, SLOT // 4, 2, IB, N])
        fw, fh, fh0 = (pr.sb(ctx, f"ks_{n}", [P, P]) for n in ("fw", "fh", "fh0"))
        with nc.Block() as block:
            @block.sync
            def _(sp):
                for t, n in ((pr.ident, "ident"), (pr.pair, "pair"), (fw, "l3_fw"), (fh, "l3_fh"), (fh0, "l3_fh0")):
                    sp.dma_start(t[:], pr.ins[n]).then_inc(const, 16)
                sp.sem_inc(x_loaded, START)
                with sp.Fori(0, tiles // 2) as i:
                    for p in range(2):
                        sp.wait_ge(turned, START + 32 * i + 16 * p - 16)
                        for k in range(4):
                            at = slice(k * PIX // 4, (k + 1) * PIX // 4)
                            sp.dma_start(src[p][:, at], w_tiles[2 * i + p][:, at]).then_inc(loaded[p][k], 16)
                    sp.wait_ge(x_loaded, 16 * i + START)
                    sp.dma_start(pr.X[:, i, :], x_groups[i]).then_inc(x_loaded, 16)

            @block.tensor
            def _(pe):
                pe.sem_inc(turned, START)
                pe.wait_ge(const, 16 * 5)
                with pe.Fori(0, tiles // 2) as i:
                    for p in range(2):
                        forward_products(pe, pr, src[p], tt, cols, fw, fh, fh0, 32 * i + 16 * p,
                                         turned, turned_read, made, made_read,
                                         lambda j: pe.wait_ge(loaded[p][j // 2], 16 * i + 16))

            @block.vector
            def _(dve):
                dve.memset(pr.eps[:], GN_EPS).then_inc(eps, 1)
                dve.memset(pr.zero[:], 0.0).then_inc(eps, 1)
                with dve.Fori(0, tiles // 2) as i:
                    for p in range(2):
                        def stats(s):
                            if p == 1:
                                if s == 0:
                                    dve.wait_ge(x_loaded, START + 16 * i + 16)
                                pr.chunk_stats(dve, i, s, step)

                        copy_turned(dve, ps, tt, cols, 32 * i + 16 * p, turned, turned_read, made, stats)
                    pr.group_stats(dve, i, step)

            @block.scalar
            def _(act):
                act.sem_inc(made_read, START)
                act.sem_inc(stored, START)
                with act.Fori(0, tiles // 2) as i:
                    for p in range(2):
                        base = 32 * i + 16 * p
                        copy_rows(act, ps, src[p], base, made, made_read)
                        for s in range(SLOT // 4):
                            act.wait_ge(made, base + NCH + s + 1)
                            if s == 0:
                                act.wait_ge(stored, START + 64 * i + 32 * p)
                            act.copy(spec[:, s].rearrange("p r o k -> p o r k"),
                                     ps[4 + s % 4][:].rearrange("p (o r k) -> p o r k", o=IB, r=2)
                                     ).then_inc(made_read, 1)
                        act.wait_ge(made_read, START + base + 16)
                        for part in range(2):
                            act.dma_start(pr.kf[:, :, part, 2 * i + p, :].rearrange("s p n -> p s n"),
                                          spec[:, :, part].rearrange("p s o k -> p s (o k)")).then_inc(stored, 16)
                act.wait_ge(stored, START + 32 * tiles)


def forward_products(pe, pr, src, tt, cols, fw, fh, fh0, base, turned, turned_read, made, made_read,
                     src_ready):
    ps = pr.psum

    def turn(j):
        src_ready(j)
        if j >= 4:
            pe.wait_ge(turned_read, base + j - 3)
        for k in range(4):
            m = pe.transpose(ps[j % 4][:, k * P:(k + 1) * P], src[:, (4 * j + k) * P:(4 * j + k + 1) * P], pr.ident[:])
        m.then_inc(turned, 1)

    def rows(j):
        pe.wait_ge(turned_read, base + j + 1)
        pe.wait_ge(made_read, START + base + j - 3)
        for k in range(4):
            m = pe.matmul(ps[4 + j % 4][:, k * P:(k + 1) * P], tt[j % 4][:, k * P:(k + 1) * P], fw[:],
                          start=True, stop=True)
        m.then_inc(made, 1)

    turn(0)
    turn(1)
    for j in range(NCH):
        if j + 2 < NCH:
            turn(j + 2)
        rows(j)
    spectra = src[:].rearrange("p (k s) -> p k s", s=SLOT)

    def turn_columns(s):
        if s == 0:
            pe.wait_ge(made_read, START + base + NCH)
        if s >= 4:
            pe.wait_ge(turned_read, base + NCH + s - 3)
        for k in range(4):
            m = pe.transpose(ps[s % 4][:, k * P:(k + 1) * P], spectra[:, :, 4 * s + k], pr.ident[:])
        m.then_inc(turned, 1)

    def columns(s):
        pe.wait_ge(turned_read, base + NCH + s + 1)
        if s >= 4:
            pe.wait_ge(made_read, START + base + NCH + s - 3)
        for b in range(IB):
            m = pe.matmul(ps[4 + s % 4][:, b * P:(b + 1) * P], cols[:, b, 4 * s:4 * s + 4].rearrange("p s c -> p (s c)"),
                          fh[:], start=True, stop=True)
        if s == 0:
            for b in range(IB):
                m = pe.matmul(ps[4][0:C, b * P:(b + 1) * P], cols[:, b, 0], fh0[:],
                              start=True, stop=True)
        m.then_inc(made, 1)

    turn_columns(0)
    turn_columns(1)
    for s in range(SLOT // 4):
        if s + 2 < SLOT // 4:
            turn_columns(s + 2)
        columns(s)


def copy_turned(dve, ps, tt, cols, base, turned, turned_read, made, after=lambda s: None):
    for j in range(NCH):
        dve.wait_ge(turned, START + base + j + 1)
        if j >= 4:
            dve.wait_ge(made, base + j - 3)
        dve.tensor_copy(tt[j % 4][:], ps[j % 4][:]).then_inc(turned_read, 1)
    for s in range(SLOT // 4):
        dve.wait_ge(turned, START + base + NCH + s + 1)
        dve.tensor_copy(cols[:, :, 4 * s:4 * s + 4].rearrange("p b s c -> p s b c"),
                        ps[s % 4][:].rearrange("p (s b c) -> p s b c", s=4, b=IB)).then_inc(turned_read, 1)
        after(s)


def copy_rows(act, ps, src, base, made, made_read, after=lambda j: None):
    for j in range(NCH):
        act.wait_ge(made, base + j + 1)
        act.copy(src[:, j * CH:(j + 1) * CH], ps[4 + j % 4][:]).then_inc(made_read, 1)
        after(j)


def l0_forward_stage(pr, xb, wb, w_loaded, xb_loaded):
    nc, ps = pr.nc, pr.psum
    const, ready, turned, turned_read = (pr.sem(f"f0_{n}") for n in ("const", "ready", "turned", "turned_read"))
    made, made_read, negated, moved = (pr.sem(f"f0_{n}") for n in ("made", "made_read", "negated", "moved"))
    G = NCH + KT // 4
    RW = 2 * 2 * KT
    with ExitStack() as ctx:
        src = pr.sb(ctx, "f0_src", [P, PIX])
        tt = [pr.sb(ctx, f"f0_tt{p}", [P, CH]) for p in range(4)]
        rows = pr.sb(ctx, "f0_rows", [P, N, 2, KT])
        cols = pr.sb(ctx, "f0_cols", [P, IB, KT, C])
        xm = pr.sb(ctx, "f0_xm", [P, 2, KT // 4, KX, 2, IB])
        fw, fh = pr.sb(ctx, "f0_fw", [P, RW]), pr.sb(ctx, "f0_fh", [P, 2 * KX])
        with nc.Block() as block:
            @block.sync
            def _(sp):
                sp.sem_inc(moved, START)
                sp.dma_start(fw[:], pr.ins["l0_fw"]).then_inc(const, 16)
                sp.dma_start(fh[:], pr.ins["l0_fh"]).then_inc(const, 16)
                for w in range(4):
                    for part, n in enumerate(("L0_conv_weights_r", "L0_conv_weights_i")):
                        to = (w % 2 * 2 + part) * C
                        sp.dma_start(wb[to:to + C, w // 2].rearrange("p o x y -> p (o x y)"),
                                     pr.ins[n][w].rearrange("i o x y -> i (o x y)")).then_inc(w_loaded, 16)
                with sp.Fori(0, Q) as q:
                    sp.wait_ge(negated, 4 * q + 4)
                    for part in range(2):
                        sp.dma_start(pr.xf[q, part].rearrange("c (s k) n -> s c (k n)", s=4),
                                     xm[:, part].rearrange("p s k r b -> p (s k r b)")).then_inc(moved, 16)
                    sp.wait_ge(moved, START + 32 * q + 32)
                    for w in range(4):
                        for part in range(2):
                            to = (w % 2 * 2 + part) * C
                            n = len(L0_BLOCKS[w])
                            sp.dma_start(xb[to:to + C, w // 2, q, :, 0:n].rearrange("c k x r b -> c k (x r b)"),
                                         pr.xf[q, part, :, :, L0_OFF[w] * 2 * IB:(L0_OFF[w] + n) * 2 * IB]
                                         ).then_inc(xb_loaded, 16)

            @block.tensor
            def _(pe):
                pe.sem_inc(turned, START)
                pe.wait_ge(const, 32)
                with pe.Fori(0, Q) as q:
                    def turn(j):
                        pe.wait_ge(ready, NCH * q + j + 1)
                        if j >= 4:
                            pe.wait_ge(turned_read, G * q + j - 3)
                        for k in range(4):
                            at = (4 * j + k) * P
                            m = pe.transpose(ps[j % 4][:, k * P:(k + 1) * P], src[:, at:at + P], pr.ident[:])
                        m.then_inc(turned, 1)

                    turn(0)
                    turn(1)
                    for j in range(NCH):
                        if j + 2 < NCH:
                            turn(j + 2)
                        pe.wait_ge(turned_read, G * q + j + 1)
                        pe.wait_ge(made_read, START + G * q + j - 3)
                        for k in range(4):
                            m = pe.matmul(ps[4 + j % 4][:, k * RW:(k + 1) * RW], tt[j % 4][:, k * P:(k + 1) * P],
                                          fw[:], start=True, stop=True)
                        m.then_inc(made, 1)
                    pe.wait_ge(made_read, START + G * q + NCH)
                    for s in range(KT // 4):
                        for k in range(4):
                            m = pe.transpose(ps[s % 4][:, k * P:(k + 1) * P],
                                             rows[:, :, :, 4 * k + s].rearrange("p h r -> p (h r)"), pr.ident[:])
                        m.then_inc(turned, 1)
                    for s in range(KT // 4):
                        pe.wait_ge(turned_read, G * q + NCH + s + 1)
                        for b in range(IB):
                            m = pe.matmul(ps[4 + s % 4][:, b * 2 * KX:(b + 1) * 2 * KX],
                                          cols[:, b, 4 * s:4 * s + 4].rearrange("p s c -> p (s c)"), fh[:],
                                          start=True, stop=True)
                        m.then_inc(made, 1)

            @block.vector
            def _(dve):
                with dve.Fori(0, Q) as q:
                    for j in range(NCH):
                        dve.wait_ge(turned, START + G * q + j + 1)
                        if j >= 4:
                            dve.wait_ge(made, G * q + j - 3)
                        dve.tensor_copy(tt[j % 4][:], ps[j % 4][:]).then_inc(turned_read, 1)
                    for s in range(KT // 4):
                        dve.wait_ge(turned, START + G * q + NCH + s + 1)
                        dve.tensor_copy(cols[:, :, 4 * s:4 * s + 4].rearrange("p b s c -> p s b c"),
                                        ps[s % 4][:].rearrange("p (s b c) -> p s b c", s=4, b=IB)
                                        ).then_inc(turned_read, 1)

            @block.scalar
            def _(act):
                act.sem_inc(made_read, START)
                with act.Fori(0, Q) as q:
                    for j in range(4):
                        act.wait_ge(turned, START + G * q)
                        pr.normalise(act, src, q, j, ready)
                    for j in range(NCH):
                        act.wait_ge(made, G * q + j + 1)
                        act.copy(rows[:, ROWS * j:ROWS * j + ROWS].rearrange("p h r k -> p (h r k)"),
                                 ps[4 + j % 4][:, 0:4 * RW]).then_inc(made_read, 1)
                        if j + 4 < NCH:
                            pr.normalise(act, src, q, j + 4, ready)
                    for s in range(KT // 4):
                        act.wait_ge(made, G * q + NCH + s + 1)
                        if s == 0:
                            act.wait_ge(moved, START + 32 * q)
                        made_s = ps[4 + s % 4][:, 0:IB * 2 * KX].rearrange("p (b k r) -> p k r b", b=IB, r=2)
                        act.copy(xm[:, 0, s], made_s)
                        act.copy(xm[:, 1, s, :, 1, :], made_s[:, :, 0, :]).then_inc(made_read, 1)

            @block.gpsimd
            def _(pool):
                with pool.Fori(0, Q) as q:
                    for s in range(KT // 4):
                        pool.wait_ge(made_read, START + G * q + NCH + s + 1)
                        pool.tensor_tensor(xm[:, 1, s, :, 0, :], pr.zero[:].unsqueeze(2).broadcast_to([P, KX, IB]),
                                           xm[:, 0, s, :, 1, :], ALU.subtract).then_inc(negated, 1)


def l0_mix_stage(pr, xb, wb, w_loaded, xb_loaded, yb):
    nc, ps = pr.nc, pr.psum
    mixed, mixed_read = pr.sem("m0_mixed"), pr.sem("m0_mixed_read")
    used = [len(b) for b in L0_BLOCKS]
    with nc.Block() as block:
        @block.tensor
        def _(pe):
            pe.wait_ge(w_loaded, 16 * 8)
            pe.wait_ge(xb_loaded, 16 * 8 * Q)
            for n in range(KT * K2):
                for w in range(4):
                    m = (n + 64 * (w % 2)) % (KT * K2)
                    kt, x = m // K2, m % K2
                    if x >= used[w]:
                        continue
                    at = slice(w % 2 * 2 * C, (w % 2 + 1) * 2 * C)
                    last = pe.matmul(ps[m // 16][w * C:(w + 1) * C, m % 16 * 2 * B:(m % 16 + 1) * 2 * B],
                                     wb[at, w // 2, :, x, kt],
                                     xb[at, w // 2, :, kt, x].rearrange("p q r b -> p q (r b)"),
                                     start=True, stop=True)
            last.then_inc(mixed, 1)

        def copy_out(copy, k):
            full = ps[k][64:128, :].rearrange("p (m q n) -> p q m n", q=Q, n=2 * IB)
            copy(yb[64:128, :, 2 * k:2 * k + 2].rearrange("p q k x r b -> p q (k x) (r b)"), full)
            for t in range(2):
                part = ps[k][0:64, t * CH // 2:t * CH // 2 + used[0] * 2 * B]
                m = copy(yb[0:64, :, 2 * k + t, 0:used[0]].rearrange("p q x r b -> p q x (r b)"),
                         part.rearrange("p (x q n) -> p q x n", q=Q, n=2 * IB))
            m.then_inc(mixed_read, 1)

        @block.vector
        def _(dve):
            dve.wait_ge(mixed, 1)
            for k in range(0, 8, 2):
                copy_out(dve.tensor_copy, k)

        @block.scalar
        def _(act):
            act.wait_ge(mixed, 1)
            for k in range(1, 8, 2):
                copy_out(act.copy, k)


def inverse_stage(pr, name, y, yb, slots, modes, ih, ih0, iw, rows4, last):
    nc, ps = pr.nc, pr.psum
    K = P // 2 if 2 * modes <= P // 2 else P
    modes = K // 2
    SG = slots // 4
    HG = N // rows4 // 4
    per = CH // (rows4 * N)
    const, staged, turned, turned_read = (pr.sem(f"{name}_{n}") for n in ("const", "staged", "turned", "turned_read"))
    made, made_read, turned2, turned2_read = (pr.sem(f"{name}_{n}") for n in ("made", "made_read", "turned2", "turned2_read"))
    pixels, added, step, stored = (pr.sem(f"{name}_{n}") for n in ("pixels", "added", "step", "stored"))
    padded = pr.sem(f"{name}_padded")
    out_groups = pr.out.rearrange("(q b) c h w -> q (b c) (h w)", b=IB)
    with ExitStack() as ctx:
        yq = pr.sb(ctx, f"{name}_yq", [P, SG, modes, 2, IB])
        cols = pr.sb(ctx, f"{name}_cols", [P, slots, IB, C])
        rows = pr.sb(ctx, f"{name}_rows", [P, N, slots, 2])
        tt = [pr.sb(ctx, f"{name}_tt{p}", [P, CH]) for p in range(4)]
        mh = pr.sb(ctx, f"{name}_mh", [P, P])
        mh0 = pr.sb(ctx, f"{name}_mh0", [P, P])
        mw = pr.sb(ctx, f"{name}_mw", [P, rows4 * N])
        with nc.Block() as block:
            @block.sync
            def _(sp):
                for t, n in ((mh, ih), (mh0, ih0), (mw, iw)):
                    sp.dma_start(t[:], pr.ins[n]).then_inc(const, 16)
                if yb is not None:
                    with sp.Fori(0, Q) as q:
                        sp.wait_ge(turned, START + SG * q)
                        for w in range(4):
                            for s in range(4):
                                n = len(L0_BLOCKS[w])
                                sp.dma_start(yq[s * C:(s + 1) * C, :, L0_OFF[w]:L0_OFF[w] + n].rearrange(
                                    "c s x r b -> c s (x r b)"),
                                    yb[w * C:(w + 1) * C, q, s:KT:4, 0:n].rearrange("c s x r b -> c s (x r b)")
                                ).then_inc(staged, 16)
                if last:
                    with sp.Fori(0, Q) as q:
                        sp.wait_ge(added, START + NCH * q + NCH)
                        sp.dma_start(out_groups[q], pr.X[:, q, :]).then_inc(stored, 16)
                    sp.wait_ge(stored, 16 * Q)

            @block.gpsimd
            def _(pool):
                if y is None:
                    return
                with pool.Fori(0, Q) as q:
                    pool.wait_ge(turned, START + SG * q)
                    for s in range(SG):
                        pool.tensor_copy(yq[:, s].rearrange("p k r b -> p (k r) b"),
                                         y[:, s, :, :, bass.ds(IB * q, IB)].rearrange("p k r b -> p (k r) b")
                                         ).then_inc(staged, 1)

            @block.tensor
            def _(pe):
                pe.sem_inc(turned, START)
                pe.wait_ge(const, 48)
                pe.wait_ge(padded, 2)
                with pe.Fori(0, Q) as q:
                    def turn(s):
                        pe.wait_ge(staged, 256 * q + 256 if y is None else SG * q + s + 1)
                        if s >= 4:
                            pe.wait_ge(turned_read, SG * q + s - 3)
                        pe.sem_inc(pr.pace, 1)
                        for b in range(IB):
                            m = pe.transpose(ps[s % 4][0:K, b * P:(b + 1) * P],
                                             yq[:, s].rearrange("p k r b -> p (k r) b")[:, :, b], pr.ident[:])
                        m.then_inc(turned, 1)

                    turn(0)
                    turn(1)
                    for s in range(SG):
                        if s + 2 < SG:
                            turn(s + 2)
                        pe.wait_ge(turned_read, SG * q + s + 1)
                        if s < 4:
                            pe.wait_ge(added, START + NCH * q + s - 3)
                        else:
                            pe.wait_ge(made_read, SG * q + s - 3)
                        for k in range(4):
                            m = pe.matmul(ps[4 + s % 4][:, k * P:(k + 1) * P],
                                          cols[:, 4 * s + k].rearrange("p b o -> p (b o)"),
                                          (mh0 if s == 0 and k == 0 else mh)[:], start=True, stop=True)
                        m.then_inc(made, 1)
                    pe.wait_ge(made_read, SG * q + SG)

                    def turn_rows(g):
                        if g >= 4:
                            pe.wait_ge(turned2_read, HG * q + g - 3)
                        for k in range(4):
                            h = (4 * g + k) * rows4
                            m = pe.transpose(ps[g % 4][:, k * P:(k + 1) * P],
                                             rows[:, h:h + rows4].rearrange("p h s r -> p (h s r)"), pr.ident[:])
                        m.then_inc(turned2, 1)

                    turn_rows(0)
                    turn_rows(1)
                    for c in range(NCH):
                        g, first = c * per // 4, c * per % 4
                        if first == 0 and g + 2 < HG:
                            turn_rows(g + 2)
                        if first == 0:
                            pe.wait_ge(turned2_read, HG * q + g + 1)
                        if c >= 4:
                            pe.wait_ge(added, START + NCH * q + c - 3)
                        for k in range(per):
                            n = rows4 * N
                            m = pe.matmul(ps[4 + c % 4][:, k * n:(k + 1) * n],
                                          tt[g % 4][:, (first + k) * P:(first + k + 1) * P], mw[:],
                                          start=True, stop=True)
                        m.then_inc(pixels, 1)

            @block.vector
            def _(dve):
                dve.sem_inc(added, START)
                if K < P:
                    dve.memset(cols[K:P], 0.0).then_inc(padded, 1)
                    dve.memset(yq[:, :, KX:modes], 0.0).then_inc(padded, 1)
                else:
                    dve.sem_inc(padded, 2)
                with dve.Fori(0, Q) as q:
                    for c in range(NCH):
                        dve.wait_ge(pixels, NCH * q + c + 1)
                        x = pr.X[:, q, c * CH:(c + 1) * CH]
                        dve.tensor_tensor(x, x, ps[4 + c % 4][:], ALU.add).then_inc(added, 1)
                        if not last and c:
                            dve.wait_ge(added, START + NCH * q + c)
                            pr.chunk_stats(dve, q, c - 1, step)
                    if not last:
                        dve.wait_ge(added, START + NCH * q + NCH)
                        pr.chunk_stats(dve, q, NCH - 1, step)
                        pr.group_stats(dve, q, step)

            @block.scalar
            def _(act):
                with act.Fori(0, Q) as q:
                    def copy_columns(s):
                        act.wait_ge(turned, START + SG * q + s + 1)
                        act.copy(cols[0:K, 4 * s:4 * s + 4].rearrange("p s b o -> p b s o"),
                                 ps[s % 4][0:K, :].rearrange("p (b s o) -> p b s o", b=IB, s=4)
                                 ).then_inc(turned_read, 1)

                    copy_columns(0)
                    copy_columns(1)
                    for s in range(SG):
                        if s + 2 < SG:
                            copy_columns(s + 2)
                        act.wait_ge(made, SG * q + s + 1)
                        act.copy(rows[:, :, 4 * s:4 * s + 4, :].rearrange("p h s r -> p s h r"),
                                 ps[4 + s % 4][:].rearrange("p (s h r) -> p s h r", s=4, r=2)).then_inc(made_read, 1)
                    for g in range(HG):
                        act.wait_ge(turned2, HG * q + g + 1)
                        if g >= 4:
                            act.wait_ge(pixels, NCH * q + (g - 3) * 4 // per)
                        act.copy(tt[g % 4][:], ps[g % 4][:]).then_inc(turned2_read, 1)


def l1_edge_stage(pr, edge):
    nc, ps = pr.nc, pr.psum
    const, ready, window, meant = (pr.sem(f"e1_{n}") for n in ("const", "ready", "window", "meant"))
    seq, root, picked, spread = (pr.sem(f"e1_{n}") for n in ("seq", "root", "picked", "spread"))
    zeroed, high, split = pr.sem("e1_zeroed"), pr.sem("e1_high"), pr.sem("e1_split")
    HALO = ROWS + 2
    with ExitStack() as ctx:
        src = pr.sb(ctx, "e1_src", [P, PIX])
        hi, lo16 = (pr.sb(ctx, f"e1_{n}", [P, Q, PIX], F16) for n in ("high_part", "low_part"))
        wide = pr.sb(ctx, "e1_wide", [P, 264])
        wq = pr.sb(ctx, "e1_wq", [P, 252], F16)
        pick = pr.sb(ctx, "e1_pick", [P, P])
        spread_m = pr.sb(ctx, "e1_spread_m", [B, Q * P])
        m = pr.sb(ctx, "e1_m", [P, HALO, N + 2])
        d = pr.sb(ctx, "e1_d", [P, HALO, N])
        v = pr.sb(ctx, "e1_v", [P, HALO, N])
        g1, g2 = pr.sb(ctx, "e1_g1", [P, ROWS, N]), pr.sb(ctx, "e1_g2", [P, ROWS, N])
        es = pr.sb(ctx, "e1_es", [P, PS])
        eb = pr.sb(ctx, "e1_eb", [B, N])
        lo = pr.sb(ctx, "e1_lo", [B, 4])
        sq_eps = pr.sb(ctx, "e1_eps", [P, 1])
        nought = pr.sb(ctx, "e1_nought", [P, CH], F16)
        with nc.Block() as block:
            @block.sync
            def _(sp):
                for t, n in ((wide, "l1_mean"), (pick, "l1_pick"), (spread_m, "l1_spread")):
                    sp.dma_start(t[:], pr.ins[n]).then_inc(const, 16)

            @block.scalar
            def _(act):
                with act.Fori(0, Q) as q:
                    for j in range(NCH):
                        act.wait_ge(split, NCH * q + j + 1)
                        pr.normalise(act, src, q, j, ready)
                act.wait_ge(seq, 10)
                act.activation(g1[:], g2[:], ACT.Sqrt, bias=sq_eps[:, 0:1]).then_inc(root, 1)

            @block.tensor
            def _(pe):
                pe.wait_ge(const, 48)
                pe.wait_ge(zeroed, 3)
                pe.matmul(ps[0][:], nought[:, 0:P], nought[:], start=True, stop=False, skip_group_check=True)
                pe.matmul(ps[1][:, 0:P], nought[:, 0:P], nought[:, 0:P], start=True, stop=False,
                          skip_group_check=True)
                with pe.Fori(0, Q) as q:
                    pe.wait_ge(window, q + 1)
                    for s in range(NCH):
                        w = wq[:, 124 - B * s:124 - B * s + P]
                        pe.wait_ge(split, NCH * (q + 1) + s + 1)
                        for part in (hi, lo16):
                            rows = part[:, q, :].rearrange("p (h w) -> p h w", w=N)
                            last = pe.matmul(ps[0][:], w, part[:, q, s * CH:(s + 1) * CH], start=False, stop=False,
                                             skip_group_check=True)
                            if s > 0:
                                pe.matmul(ps[1][:, 0:N], w, rows[:, ROWS * s - 1, :], start=False, stop=False,
                                          skip_group_check=True)
                                above = wq[:, 124 - B * (s - 1):124 - B * (s - 1) + P]
                                last = pe.matmul(ps[1][:, N:2 * N], above, rows[:, ROWS * s, :], start=False,
                                                 stop=False, skip_group_check=True)
                    last.then_inc(meant, 1)
                pe.wait_ge(seq, 11)
                for s in range(PS):
                    last = pe.matmul(ps[2][0:B, s * PS:(s + 1) * PS], pick[:, B * s:B * s + B], es[:],
                                     start=True, stop=True)
                last.then_inc(picked, 1)
                pe.wait_ge(seq, 18)
                for q in range(Q):
                    last = pe.matmul(ps[3][:, q * N:(q + 1) * N], spread_m[:, q * P:(q + 1) * P], eb[:],
                                     start=True, stop=True)
                last.then_inc(spread, 1)

            @block.vector
            def _(dve):
                count = [0]

                def then(ins):
                    count[0] += 1
                    ins.then_inc(seq, 1)
                    dve.wait_ge(seq, count[0])

                def low_part(q, j):
                    at = slice(j * CH, (j + 1) * CH)
                    dve.wait_ge(high, NCH * q + j + 1)
                    dve.tensor_tensor(lo16[:, q, at], src[:, at], hi[:, q, at], ALU.subtract).then_inc(split, 1)

                dve.memset(m[:], 0.0).then_inc(zeroed, 1)
                dve.memset(sq_eps[:], 1e-6).then_inc(zeroed, 1)
                dve.memset(nought[:], 0.0).then_inc(zeroed, 1)
                dve.sem_inc(split, NCH)
                dve.sem_inc(meant, START)
                dve.wait_ge(const, 48)
                with dve.Fori(0, Q) as q:
                    dve.wait_ge(meant, START + q)
                    dve.tensor_copy(wq[:], wide[:, bass.ds(12 - IB * q, 252)]).then_inc(window, 1)
                    for j in range(NCH):
                        at = slice(j * CH, (j + 1) * CH)
                        dve.wait_ge(ready, NCH * q + j + 1)
                        dve.tensor_copy(hi[:, q, at], src[:, at]).then_inc(high, 1)
                        if j:
                            low_part(q, j - 1)
                    low_part(q, NCH - 1)
                dve.wait_ge(meant, START + Q)
                dve.wait_ge(zeroed, 3)
                dve.tensor_copy(m[:, 1:1 + ROWS, 1:1 + N], ps[0][:].rearrange("p (h w) -> p h w", w=N))
                then(dve.tensor_copy(m[:, 0:HALO:HALO - 1, 1:1 + N],
                                     ps[1][:, 0:2 * N].rearrange("p (h w) -> p h w", w=N)))
                dve.scalar_tensor_tensor(v[:], m[:, :, 1:1 + N], 2.0, m[:, :, 0:N], ALU.mult, ALU.add)
                then(dve.tensor_tensor(d[:], m[:, :, 2:2 + N], m[:, :, 0:N], ALU.subtract))
                then(dve.tensor_tensor(v[:], v[:], m[:, :, 2:2 + N], ALU.add))
                then(dve.scalar_tensor_tensor(g1[:], d[:, 1:1 + ROWS], 2.0, d[:, 0:ROWS], ALU.mult, ALU.add))
                then(dve.tensor_tensor(g1[:], g1[:], d[:, 2:2 + ROWS], ALU.add))
                then(dve.tensor_tensor(g2[:], v[:, 2:2 + ROWS], v[:, 0:ROWS], ALU.subtract))
                then(dve.tensor_tensor(g2[:], g2[:], g2[:], ALU.mult))
                then(dve.tensor_tensor(g1[:], g1[:], g1[:], ALU.mult))
                then(dve.tensor_tensor(g2[:], g2[:], g1[:], ALU.add))
                then(dve.memset(lo[:], 0.0))
                dve.wait_ge(root, 1)
                then(dve.tensor_reduce(es[:], g1[:].rearrange("p y (c x) -> p c y x", x=PS), AX.XY, ALU.add))
                dve.wait_ge(picked, 1)
                then(dve.tensor_scalar(eb[:], ps[2][0:B, 0:N], 1.0 / (PS * PS), None, ALU.mult))
                then(dve.tensor_reduce(lo[:, 0:1], eb[:], AX.X, ALU.min))
                then(dve.tensor_scalar(eb[:], eb[:], lo[:, 0:1], None, ALU.subtract))
                then(dve.tensor_reduce(lo[:, 1:2], eb[:], AX.X, ALU.max))
                then(dve.tensor_scalar(lo[:, 2:3], lo[:, 1:2], 1e-6, None, ALU.add))
                then(dve.reciprocal(lo[:, 3:4], lo[:, 2:3]))
                then(dve.tensor_scalar(eb[:], eb[:], lo[:, 3:4], 0.5, ALU.mult, ALU.mult))
                dve.wait_ge(spread, 1)
                dve.tensor_copy(edge[:].rearrange("p q n -> p (q n)"), ps[3][:, 0:Q * N])


def l1_filter_stage(pr, edge):
    nc, ps = pr.nc, pr.psum
    const, ready, mask, turned = (pr.sem(f"p1_{n}") for n in ("const", "ready", "mask", "turned"))
    turned_read, filtered, added, scaled = (pr.sem(f"p1_{n}") for n in ("turned_read", "filtered", "added", "scaled"))
    finished, step, mats = (pr.sem(f"p1_{n}") for n in ("finished", "step", "mats"))
    with ExitStack() as ctx:
        src = pr.sb(ctx, "p1_src", [P, PIX])
        tt = [pr.sb(ctx, f"p1_tt{p}", [P, CH]) for p in range(2)]
        tmp = [pr.sb(ctx, f"p1_tmp{p}", [P, PS, PS * PS]) for p in range(2)]
        dft, same = pr.sb(ctx, "p1_dft", [P, P]), pr.sb(ctx, "p1_same", [P, P])
        band, gain = pr.sb(ctx, "p1_band", [NB, P]), pr.sb(ctx, "p1_gain", [NB, 1])
        high, mk = pr.sb(ctx, "p1_high", [P, 1]), pr.sb(ctx, "p1_mk", [P, 2])
        md = pr.sb(ctx, "p1_md", [P, 2, P])
        mm = pr.sb(ctx, "p1_mm", [P, 2, P])
        with nc.Block() as block:
            @block.sync
            def _(sp):
                for t, n in ((dft, "l1_dft"), (same, "l1_same"), (band, "l1_band"), (high, "l1_high")):
                    sp.dma_start(t[:], pr.ins[n]).then_inc(const, 16)
                sp.dma_start(gain[:], pr.ins["L1_conv_gain"].rearrange("a n -> n a")).then_inc(const, 16)

            @block.tensor
            def _(pe):
                pe.sem_inc(turned, START)
                pe.wait_ge(const, 80)
                pe.matmul(ps[2][:, 0:1], band[:], gain[:], start=True, stop=True).then_inc(mask, 1)
                pe.wait_ge(mats, 4)
                pe.matmul(ps[3][:, 0:2 * P], dft[:], md[:].rearrange("p t n -> p (t n)"), start=True,
                          stop=True).then_inc(mask, 1)
                pe.wait_ge(mats, 6)
                with pe.Fori(0, Q) as q:
                    def turn(j):
                        pe.wait_ge(ready, NCH * q + j + 1)
                        if j >= 2:
                            pe.wait_ge(turned_read, NCH * q + j - 1)
                        for k in range(4):
                            m = pe.transpose(ps[j % 2][:, k * P:(k + 1) * P],
                                             src[:, (4 * j + k) * P:(4 * j + k + 1) * P], pr.ident[:])
                        m.then_inc(turned, 1)

                    turn(0)
                    for j in range(NCH):
                        if j + 1 < NCH:
                            turn(j + 1)
                        pe.wait_ge(turned_read, NCH * q + j + 1)
                        if j == 0:
                            pe.wait_ge(added, START + NCH * q)
                        if j >= 2:
                            pe.wait_ge(added, START + NCH * q + j - 1)
                        for t in range(2):
                            for k in range(4):
                                m = pe.matmul(ps[2 + 2 * (j % 2) + t][:, k * P:(k + 1) * P],
                                              tt[j % 2][:, k * P:(k + 1) * P], mm[:, t, :], start=True, stop=True)
                        m.then_inc(filtered, 1)

            @block.scalar
            def _(act):
                with act.Fori(0, Q) as q:
                    act.wait_ge(turned, START + NCH * q)
                    for j in range(3):
                        pr.normalise(act, src, q, j, ready, True)
                    for j in range(NCH):
                        act.wait_ge(turned, START + NCH * q + j + 1)
                        if j >= 2:
                            act.wait_ge(filtered, NCH * q + j - 1)
                        act.copy(tt[j % 2][:], ps[j % 2][:]).then_inc(turned_read, 1)
                        if j + 3 < NCH:
                            pr.normalise(act, src, q, j + 3, ready, True)

            @block.vector
            def _(dve):
                dve.sem_inc(added, START)
                dve.wait_ge(mask, 1)
                dve.tensor_scalar(mk[:, 0:1], ps[2][:, 0:1], 0.0, None, ALU.max).then_inc(mats, 1)
                dve.wait_ge(mats, 1)
                dve.wait_ge(const, 80)
                dve.tensor_tensor(mk[:, 1:2], mk[:, 0:1], high[:], ALU.mult).then_inc(mats, 1)
                dve.wait_ge(mats, 2)
                for t in range(2):
                    dve.tensor_scalar(md[:, t, :], dft[:], mk[:, t:t + 1], None, ALU.mult).then_inc(mats, 1)
                dve.wait_ge(mask, 2)
                for t in range(2):
                    dve.tensor_tensor(mm[:, t, :], ps[3][:, t * P:(t + 1) * P], same[:], ALU.mult).then_inc(mats, 1)
                with dve.Fori(0, Q) as q:
                    for j in range(NCH):
                        dve.wait_ge(filtered, NCH * q + j + 1)
                        if j >= 2:
                            dve.wait_ge(finished, NCH * q + j - 1)
                        dve.tensor_tensor(tmp[j % 2][:], ps[3 + 2 * (j % 2)][:].rearrange("p (a b) -> p a b", a=PS),
                                          edge[:, q, PS * j:PS * j + PS].unsqueeze(2).broadcast_to([P, PS, PS * PS]),
                                          ALU.mult).then_inc(scaled, 1)
                        x = pr.X[:, q, j * CH:(j + 1) * CH].rearrange("p (y a x) -> p a y x", y=PS, x=PS)
                        dve.tensor_tensor(x, x, ps[2 + 2 * (j % 2)][:].rearrange("p (a y x) -> p a y x", a=PS, x=PS),
                                          ALU.add).then_inc(added, 1)
                        if j >= 2:
                            pr.chunk_stats(dve, q, j - 2, step)
                    for j in (NCH - 2, NCH - 1):
                        dve.wait_ge(finished, NCH * q + j + 1)
                        pr.chunk_stats(dve, q, j, step)
                    pr.group_stats(dve, q, step)

            @block.gpsimd
            def _(pool):
                with pool.Fori(0, Q) as q:
                    for j in range(NCH):
                        pool.wait_ge(scaled, NCH * q + j + 1)
                        pool.wait_ge(added, START + NCH * q + j + 1)
                        x = pr.X[:, q, j * CH:(j + 1) * CH].rearrange("p (y a x) -> p a y x", y=PS, x=PS)
                        pool.tensor_tensor(x, x, tmp[j % 2][:].rearrange("p a (y x) -> p a y x", x=PS),
                                           ALU.add).then_inc(finished, 1)


def l2_stage(pr):
    nc, ps = pr.nc, pr.psum
    wl, zero, ready, padded = (pr.sem(f"c2_{n}") for n in ("weights", "zero", "ready", "padded"))
    moved, high, low = ([pr.sem(f"c2_{n}{b}") for b in range(IB)] for n in ("moved", "high", "low"))
    conv, added, step, seq, most, scales = (pr.sem(f"c2_{n}") for n in ("conv", "added", "step", "seq", "most", "scales"))
    G = 8
    HG = N // 4 // G
    TILES = IB * HG
    W_UP, X_UP = 128.0, 64.0
    with ExitStack() as ctx:
        src = pr.sb(ctx, "c2_src", [P, PW, PW])
        R = pr.sb(ctx, "c2_r", [P, IB, RB, PW])
        rh, rl = (pr.sb(ctx, f"c2_{n}", [P, Q, IB, RB, PW], F16) for n in ("rh", "rl"))
        wn = pr.sb(ctx, "c2_wn", [P, C, KS * KS])
        ws = pr.sb(ctx, "c2_ws", [P, C, KS * KS])
        nh, nl = (pr.sb(ctx, f"c2_{n}", [P, C, KS * KS], F16) for n in ("nh", "nl"))
        wh, wlo = (pr.sb(ctx, f"c2_{n}", [P, 2, KS, 4, C], F16) for n in ("wh", "wlo"))
        ones = pr.sb(ctx, "c2_ones", [1, P])
        mx = pr.sb(ctx, "c2_mx", [P, 1])
        top = pr.sb(ctx, "c2_top", [1, 2])
        pw = pr.sb(ctx, "c2_pw", [P, 4])
        nrm = pr.sb(ctx, "c2_nrm", [P, 2, Q])
        with nc.Block() as block:
            @block.sync
            def _(sp):
                w = pr.ins["L2_conv_weight"].rearrange("o c y x -> c o (y x)")
                for i in range(4):
                    sp.dma_start(wn[i * C:(i + 1) * C], w).then_inc(wl, 16)
                with sp.Fori(0, Q) as q:
                    for b in range(IB):
                        at = slice(b * C, (b + 1) * C)
                        sp.wait_ge(padded, 8 * q + 8)
                        for r in range(4):
                            sp.dma_start(R[r * C:(r + 1) * C, b].rearrange("c k w -> c k w"),
                                         src[at, r:PW:4, :]).then_inc(moved[b], 16)

            @block.scalar
            def _(act):
                for b in range(IB):
                    act.sem_inc(moved[b], START)
                act.wait_ge(scales, 1)
                with act.Fori(0, Q) as q:
                    for b in range(IB):
                        act.wait_ge(moved[b], START + 64 * q)
                    for j in range(NCH):
                        act.activation(src[:, 1 + ROWS * j:1 + ROWS * j + ROWS, 1:1 + N],
                                       pr.X[:, q, j * CH:(j + 1) * CH].rearrange("p (h w) -> p h w", w=N),
                                       ACT.Identity, scale=nrm[:, 0, bass.ds(q, 1)], bias=nrm[:, 1, bass.ds(q, 1)]
                                       ).then_inc(ready, 1)
                    for b in range(IB):
                        act.wait_ge(moved[b], START + 64 * q + 64)
                        act.copy(rh[:, q, b].rearrange("p k w -> p (k w)"), R[:, b].rearrange("p k w -> p (k w)")
                                 ).then_inc(high[b], 1)

            @block.gpsimd
            def _(pool):
                for b in range(IB):
                    pool.sem_inc(low[b], START)
                with pool.Fori(0, Q) as q:
                    for b in range(IB):
                        pool.wait_ge(low[b], START + q)
                    pool.wait_ge(ready, NCH * q + NCH)
                    pool.sem_inc(pr.pace, 1)
                    edges = ((0, 2), (N + 1, N - 1), (N + 2, N - 2), (N + 3, 3))
                    for to, of in edges:
                        pool.tensor_copy(src[:, 1:1 + N, to:to + 1], src[:, 1:1 + N, of:of + 1]).then_inc(padded, 1)
                    pool.wait_ge(padded, 8 * q + 4)
                    pool.sem_inc(pr.pace, 1)
                    for to, of in edges:
                        pool.tensor_copy(src[:, to, :], src[:, of, :]).then_inc(padded, 1)
                    for b in range(IB):
                        pool.wait_ge(high[b], q + 1)
                        pool.tensor_tensor(rl[:, q, b].rearrange("p k w -> p (k w)"),
                                           R[:, b].rearrange("p k w -> p (k w)"),
                                           rh[:, q, b].rearrange("p k w -> p (k w)"), ALU.subtract).then_inc(low[b], 1)

            @block.tensor
            def _(pe):
                pe.wait_ge(seq, 1)
                pe.transpose(ps[0][0:1, 0:P], mx[:], pr.ident[:]).then_inc(most, 1)
                pe.wait_ge(seq, 2)
                pe.matmul(ps[1][:, 0:1], ones[:], top[:, 0:1], start=True, stop=True).then_inc(most, 1)
                pe.wait_ge(zero, 43)
                with pe.Fori(0, Q) as q:
                    for n in range(TILES):
                        b, half = n // HG, n % HG
                        pe.wait_ge(low[b], START + q + 1)
                        pe.wait_ge(added, START + 32 * q + 4 * n - 28)
                        terms = [(k, x, w, d) for k in range(2) for x in range(KS)
                                 for w, d in ((wh, rh), (wh, rl), (wlo, rh))]
                        for i, (k, x, w, d) in enumerate(terms):
                            m = pe.matmul(ps[n][:], w[:, k, x].rearrange("p o c -> p (o c)"),
                                          d[:, q, b, G * half + k:G * half + k + G, 4 - x:4 - x + N],
                                          start=i == 0, stop=i == len(terms) - 1)
                        m.then_inc(conv, 1)

            @block.vector
            def _(dve):
                dve.sem_inc(added, START)
                dve.tensor_scalar(nrm[:, 0, :], pr.rstd[:], X_UP, None, ALU.mult)
                dve.tensor_scalar(nrm[:, 1, :], pr.shift[:], X_UP, None, ALU.mult).then_inc(scales, 1)
                dve.memset(ones[:], 1.0)
                dve.memset(wh[:], 0.0).then_inc(zero, 1)
                dve.memset(wlo[:], 0.0).then_inc(zero, 1)
                dve.wait_ge(wl, 64)
                flat = "p o y -> p (o y)"
                dve.tensor_reduce(mx[:], wn[:].rearrange(flat), AX.X, ALU.max, apply_absolute_value=True
                                  ).then_inc(seq, 1)
                dve.wait_ge(most, 1)
                dve.tensor_reduce(top[:, 0:1], ps[0][0:1, 0:P], AX.X, ALU.max).then_inc(seq, 1)
                dve.wait_ge(most, 2)
                dve.tensor_scalar(pw[:, 0:1], ps[1][:, 0:1], 2.0 ** -100, 2.0 ** 100, ALU.max, ALU.min).then_inc(seq, 1)
                dve.wait_ge(seq, 3)
                dve.tensor_scalar(pw[:, 1:2].bitcast(I32), pw[:, 0:1].bitcast(I32), 0x7F800000, None,
                                  ALU.bitwise_and).then_inc(seq, 1)
                dve.wait_ge(seq, 4)
                dve.tensor_scalar(pw[:, 2:3], pw[:, 1:2], 1.0 / (W_UP * X_UP), None, ALU.mult)
                dve.reciprocal(pw[:, 3:4], pw[:, 1:2]).then_inc(seq, 1)
                dve.wait_ge(seq, 5)
                dve.tensor_scalar(ws[:].rearrange(flat), wn[:].rearrange(flat), pw[:, 3:4], W_UP, ALU.mult, ALU.mult
                                  ).then_inc(seq, 1)
                dve.wait_ge(seq, 6)
                dve.tensor_copy(nh[:].rearrange(flat), ws[:].rearrange(flat)).then_inc(seq, 1)
                dve.wait_ge(seq, 7)
                dve.tensor_tensor(nl[:].rearrange(flat), ws[:].rearrange(flat), nh[:].rearrange(flat), ALU.subtract
                                  ).then_inc(zero, 1)
                dve.wait_ge(zero, 3)
                for t, n in ((wh, nh), (wlo, nl)):
                    for i in range(4):
                        for k in range(2):
                            for o in range(4):
                                jy = o + 4 - 4 * k - i
                                if 0 <= jy < KS:
                                    at = slice(i * C, (i + 1) * C)
                                    dve.tensor_copy(t[at, k, :, o, :],
                                                    n[at, :, jy * KS:(jy + 1) * KS].rearrange("c o x -> c x o")
                                                    ).then_inc(zero, 1)
                with dve.Fori(0, Q) as q:
                    for n in range(TILES):
                        b, half = n // HG, n % HG
                        dve.wait_ge(conv, TILES * q + n + 1)
                        for o in range(4):
                            at = slice(b * C, (b + 1) * C)
                            x = pr.X[at, q, :].rearrange("p (g o w) -> p g o w", o=4, w=N)[
                                :, G * half:G * half + G, o, :]
                            dve.scalar_tensor_tensor(x, ps[n][o * C:(o + 1) * C, :].rearrange("p (g w) -> p g w", w=N),
                                                     pw[at, 2:3], x, ALU.mult, ALU.add).then_inc(added, 1)
                    dve.wait_ge(added, START + 32 * q + 32)
                    for c in range(NCH):
                        pr.chunk_stats(dve, q, c, step)
                    pr.group_stats(dve, q, step)


def l3_forward_stage(pr, xm):
    nc, ps = pr.nc, pr.psum
    const, ready, turned, turned_read = (pr.sem(f"f3_{n}") for n in ("const", "ready", "turned", "turned_read"))
    made, made_read = pr.sem("f3_made"), pr.sem("f3_made_read")
    with ExitStack() as ctx:
        src = pr.sb(ctx, "f3_src", [P, PIX])
        tt = [pr.sb(ctx, f"f3_tt{p}", [P, CH]) for p in range(4)]
        cols = pr.sb(ctx, "f3_cols", [P, IB, SLOT, C])
        fw, fh, fh0 = (pr.sb(ctx, f"f3_{n}", [P, P]) for n in ("fw", "fh", "fh0"))
        with nc.Block() as block:
            @block.sync
            def _(sp):
                for t, n in ((fw, "l3_fw"), (fh, "l3_fh"), (fh0, "l3_fh0")):
                    sp.dma_start(t[:], pr.ins[n]).then_inc(const, 16)

            @block.tensor
            def _(pe):
                pe.sem_inc(turned, START)
                pe.wait_ge(const, 48)
                with pe.Fori(0, Q) as q:
                    forward_products(pe, pr, src, tt, cols, fw, fh, fh0, 16 * q, turned, turned_read, made,
                                     made_read, lambda j: pe.wait_ge(ready, NCH * q + j + 1))

            @block.vector
            def _(dve):
                with dve.Fori(0, Q) as q:
                    copy_turned(dve, ps, tt, cols, 16 * q, turned, turned_read, made)

            @block.scalar
            def _(act):
                act.sem_inc(made_read, START)
                with act.Fori(0, Q) as q:
                    act.wait_ge(turned, START + 16 * q)
                    for j in range(4):
                        pr.normalise(act, src, q, j, ready)

                    def ahead(j):
                        if j + 4 < NCH:
                            pr.normalise(act, src, q, j + 4, ready)

                    copy_rows(act, ps, src, 16 * q, made, made_read, ahead)
                    for s in range(SLOT // 4):
                        act.wait_ge(made, 16 * q + NCH + s + 1)
                        act.copy(xm[:, s, :, :, bass.ds(IB * q, IB)].rearrange("p k r b -> p b r k"),
                                 ps[4 + s % 4][:].rearrange("p (b r k) -> p b r k", b=IB, r=2)).then_inc(made_read, 1)


def l3_mix_stage(pr, xm):
    nc, ps = pr.nc, pr.psum
    SG = SLOT // 4
    loaded = [pr.sem(f"m3_load{p}") for p in range(2)]
    staged, mixed, mixed_read, fix = (pr.sem(f"m3_{n}") for n in ("staged", "mixed", "mixed_read", "fix"))
    H = N // 2
    with ExitStack() as ctx:
        kf = [pr.sb(ctx, f"m3_kf{p}", [P, 2, C, N]) for p in range(2)]
        xp = [pr.sb(ctx, f"m3_xp{p}", [P, 2, N, 2, B]) for p in range(2)]
        with nc.Block() as block:
            @block.sync
            def _(sp):
                with sp.Fori(0, SG // 2) as i:
                    for p in range(2):
                        sp.wait_ge(mixed, START + 4 * i + 2 * p - 2)
                        for s2 in range(2):
                            for part in range(2):
                                to = (2 * s2 + part) * C
                                of = pr.kf[2 * i + p, :, part].rearrange("(sp s c) t n -> s c sp (t n)", sp=2, s=2)
                                sp.dma_start(kf[p][to:to + C].rearrange("c sp o k -> c sp (o k)"), of[s2]
                                             ).then_inc(loaded[p], 16)

            def stage(dve, s, p):
                for slot in range(4):
                    of = xm[slot * C:(slot + 1) * C, s]
                    re = xp[p][slot % 2 * 2 * C:(slot % 2 * 2 + 1) * C, slot // 2]
                    im = xp[p][(slot % 2 * 2 + 1) * C:(slot % 2 * 2 + 2) * C, slot // 2]
                    dve.tensor_copy(re, of)
                    dve.tensor_copy(im[:, :, 1, :], of[:, :, 0, :])
                    m = dve.tensor_scalar(im[:, :, 0, :], of[:, :, 1, :], -1.0, None, ALU.mult)
                m.then_inc(staged, 1)

            @block.vector
            def _(dve):
                for p in range(2):
                    stage(dve, p, p)
                dve.wait_ge(staged, 2)
                dve.memset(xp[0][0:C, 0, 0:N:H, 1, :], 0.0).then_inc(fix, 1)
                dve.memset(xp[0][C:2 * C, 0, 0:N:H, 0, :], 0.0).then_inc(fix, 1)
                dve.tensor_copy(xp[0][C:2 * C, 0, 0:N:H, 1, :], xm[0:C, 0, 0:N:H, 1, :]).then_inc(fix, 1)
                with dve.Fori(1, SG // 2) as i:
                    for p in range(2):
                        dve.wait_ge(mixed, START + 4 * i + 2 * p - 2)
                        stage(dve, 2 * i + p, p)

            @block.tensor
            def _(pe):
                pe.sem_inc(mixed, START)
                pe.wait_ge(fix, 3)
                with pe.Fori(0, SG // 2) as i:
                    for p in range(2):
                        pe.wait_ge(loaded[p], 64 * i + 64)
                        pe.wait_ge(staged, 2 * i + p + 1)
                        for half in range(2):
                            pe.wait_ge(mixed_read, START + 4 * i + 2 * p + half - 1)
                            pe.sem_inc(pr.pace, 1)
                            for n in range(H):
                                for slot in range(4):
                                    m = (n + 16 * (slot % 2)) % H
                                    k = H * half + m
                                    at = slice(slot % 2 * 2 * C, (slot % 2 + 1) * 2 * C)
                                    to = ps[4 * half + m // 8][slot * C:(slot + 1) * C,
                                                               m % 8 * 2 * B:(m % 8 + 1) * 2 * B]
                                    last = pe.matmul(to, kf[p][at, slot // 2, :, k],
                                                     xp[p][at, slot // 2, k].rearrange("p r b -> p (r b)"),
                                                     start=True, stop=True)
                            last.then_inc(mixed, 1)

            @block.scalar
            def _(act):
                act.sem_inc(mixed_read, START)
                with act.Fori(0, SG // 2) as i:
                    for p in range(2):
                        for half in range(2):
                            act.wait_ge(mixed, START + 4 * i + 2 * p + half + 1)
                            act.wait_ge(staged, 2 * i + p + 1)
                            for m in range(4):
                                c = act.copy(xm[:, 2 * i + p, H * half + 8 * m:H * half + 8 * m + 8].rearrange(
                                    "p k r b -> p (k r b)"), ps[4 * half + m][:, 0:256])
                            c.then_inc(mixed_read, 1)


def four_layers(nc, ins, out, stop=None):
    with ExitStack() as ctx:
        pr = Program(nc, ctx, ins, out)
        kernel_spectra_stage(pr)
        pr.stats_stage("n0")
        with ExitStack() as layer:
            w_loaded = pr.sem("l0_weights")
            yb = pr.sb(layer, "l0_yb", [P, Q, KT, K2, 2, IB])
            with ExitStack() as inner:
                xb = pr.sb(inner, "l0_xb", [P, 2, Q, KT, K2, 2, IB])
                wb = pr.sb(inner, "l0_wb", [P, 2, C, K2, KT])
                xb_loaded = pr.sem("l0_xb_loaded")
                l0_forward_stage(pr, xb, wb, w_loaded, xb_loaded)
                l0_mix_stage(pr, xb, wb, w_loaded, xb_loaded, yb)
            inverse_stage(pr, "i0", None, yb, KT, KX, "l0_ih", "l0_ih", "l0_iw", 4, False)
        if stop == 0: return dump(pr)
        pr.stats_stage("n1")
        with ExitStack() as layer:
            edge = pr.sb(layer, "edge", [P, Q, N])
            l1_edge_stage(pr, edge)
            l1_filter_stage(pr, edge)
        if stop == 1: return dump(pr)
        pr.stats_stage("n2")
        l2_stage(pr)
        if stop == 2: return dump(pr)
        pr.stats_stage("n3")
        with ExitStack() as layer:
            xm = pr.sb(layer, "xm", [P, SLOT // 4, N, 2, B])
            l3_forward_stage(pr, xm)
            l3_mix_stage(pr, xm)
            inverse_stage(pr, "i3", xm, None, SLOT, N, "l3_ih", "l3_ih0", "l3_iw", 2, True)


def dump(pr):
    s = pr.sem("dump")
    with pr.nc.Block() as block:
        @block.sync
        def _(sp):
            og = pr.out.rearrange("(q b) c h w -> q (b c) (h w)", b=IB)
            for q in range(Q):
                sp.dma_start(og[q], pr.X[:, q, :]).then_inc(s, 16)
            sp.wait_ge(s, 64)


_INS = ["x", "L0_conv_weights_r", "L0_conv_weights_i", "L1_conv_gain", "L2_conv_weight", "L3_conv_weights"]


def kernel(**inputs):
    import concourse.bacc as bacc
    from concourse.bass_utils import run_bass_kernel_spmd

    nc = bacc.Bacc("TRN2", target_bir_lowering=False, num_devices=1)
    arrays = {n: np.ascontiguousarray(inputs[n]) for n in _INS} | constants()
    ins = {n: nc.dram_tensor(f"in_{n}", a.shape, F32, kind="ExternalInput").ap() for n, a in arrays.items()}
    out = nc.dram_tensor("out_y", (B, C, N, N), F32, kind="ExternalOutput").ap()
    four_layers(nc, ins, out)
    r = run_bass_kernel_spmd(nc, [{f"in_{n}": a for n, a in arrays.items()}], core_ids=[0])
    return r.results[0]["out_y"]
```

```python
from contextlib import ExitStack

import numpy as np

import concourse.bass as bass
from concourse import mybir

F32 = mybir.dt.float32
F16 = mybir.dt.float16
I32 = mybir.dt.int32
ALU = mybir.AluOpType
ACT = mybir.ActivationFunctionType
AX = mybir.AxisListType

B, C, N = 16, 32, 64
P = 128
Q = B * C // P
IB = P // C
PIX = N * N
CH = 512
NCH = PIX // CH
ROWS = CH // N
SLOT = N // 2
KT = 16
K2 = 8
BAND = 50
L0_BLOCKS = [list(range(0, N - BAND - K2)), list(range(BAND, N - K2)), list(range(N - K2, N)),
             list(range(N - BAND - K2, N - BAND))]
L0_OFF = [0, 6, 12, 20]
KX = sum(len(b) for b in L0_BLOCKS)
SLOT_AT = [[8 * (f // 2) + 2 * k + f % 2 for k in range(4)] for f in range(SLOT // 4)]
PS = 8
NB = 6
KS = 5
HN = N // 2
HP = (N + KS - 1) // 2
W_UP, X_UP = 128.0, 64.0
GN_EPS = 1e-5
START = 32


def constants():
    f = np.float64
    ang = 2 * np.pi / N
    n = np.arange(N)
    out = {}
    out["ident"] = np.eye(P)
    out["pair"] = np.kron(np.eye(P // 2), np.full((2, 2), 0.5))

    def two(m, k=2):
        return np.kron(np.eye(k), m)

    kt = np.arange(KT)
    fw = np.stack([np.cos(ang * np.outer(n, kt)), -np.sin(ang * np.outer(n, kt))], 1)
    out["l0_fw"] = two(fw.reshape(N, 2 * KT))
    kx = np.array(sum(L0_BLOCKS, []))
    out["l0_fh"] = complex_matrix(n, kx, -1.0)
    out["l0_ih"] = np.concatenate([complex_matrix(kx, n, 1.0) / N, np.zeros((P - 2 * KX, P))])
    iw = np.stack([np.cos(ang * np.outer(kt, n)), -np.sin(ang * np.outer(kt, n))], 1) * 2 / N
    iw[0] /= 2
    iw[0, 1] = 0
    out["l0_iw"] = two(iw.reshape(2 * KT, N), 4)

    s = np.arange(SLOT)
    fw = np.stack([np.cos(ang * np.outer(n, s)), -np.sin(ang * np.outer(n, s))], 1)
    fw[:, 1, 0] = (-1.0) ** n
    out["l3_fw"] = two(fw.reshape(N, 2 * SLOT))
    out["l3_fh"] = complex_matrix(n, n, -1.0).reshape(P, N, 2).transpose(0, 2, 1).reshape(P, P)
    out["l3_ih"] = complex_matrix(n, n, 1.0) / N
    iw = np.stack([np.cos(ang * np.outer(s, n)), -np.sin(ang * np.outer(s, n))], 1) * 2 / N
    iw[0, 0] = 1.0 / N
    iw[0, 1] = (-1.0) ** n / N
    out["l3_iw"] = two(iw[sum(SLOT_AT, [])].reshape(2 * SLOT, N))
    f0 = np.zeros((N, 2, N, 2))
    i0 = np.zeros((N, 2, N, 2))
    for half in range(2):
        for m in range(SLOT):
            at = half * SLOT + m
            if m:
                f0[:, half, at, 0], f0[:, half, at, 1] = np.cos(ang * n * m), -np.sin(ang * n * m)
                i0[at, 0, :, half], i0[at, 1, :, half] = 2 * np.cos(ang * n * m) / N, -2 * np.sin(ang * n * m) / N
            else:
                f0[:, half, at, 0], f0[:, half, at, 1] = 1.0, (-1.0) ** n
                i0[at, 0, :, half], i0[at, 1, :, half] = 1.0 / N, (-1.0) ** n / N
    out["l3_fh0"] = f0.transpose(0, 1, 3, 2).reshape(P, P)
    out["l3_ih0"] = i0.reshape(P, P)

    k = np.arange(PS)
    y = np.repeat(k, PS)
    x = np.tile(k, PS)
    th = 2 * np.pi / PS * (np.outer(y, y) + np.outer(x, x))
    d = np.concatenate([np.cos(th), np.sin(th)], 0) / PS
    out["l1_dft"] = np.concatenate([d, d], 1)
    out["l1_same"] = np.kron(np.eye(2), np.ones((PS * PS, PS * PS)))
    ky = np.minimum(y, PS - y).astype(np.float32)
    kx8 = np.minimum(x, PS - x).astype(np.float32)
    r = np.sqrt(ky ** 2 + kx8 ** 2).astype(np.float32)
    r = np.clip(r / np.float32(np.sqrt(2.0 * (PS // 2) ** 2) + 1e-08), 0, 1).astype(f)
    centers = np.linspace(0.0, 1.0, NB)
    w = np.maximum(1.0 - np.abs(r[None] - centers[:, None]) / (1.0 / (NB - 1)), 0)
    w = w / (w.sum(0, keepdims=True) + 1e-08)
    out["l1_band"] = np.concatenate([w, w], 1)
    out["l1_high"] = np.concatenate([(r >= 0.6), (r >= 0.6)]).astype(f)[:, None]
    wide = np.zeros((P, 12 + 124 + IB + 124))
    for b in range(IB):
        wide[b * C:(b + 1) * C, 12 + 124 + b] = 1.0 / C
    out["l1_mean"] = wide
    out["l1_pick"] = np.stack([np.eye(P)[:, 16 * s:16 * s + 16] for s in range(PS)], 1).reshape(P, P)
    out["l1_spread"] = np.concatenate([np.kron(np.eye(B)[:, IB * q:IB * q + IB], np.ones((1, C)))
                                       for q in range(Q)], 1)
    out = {k: np.ascontiguousarray(v, np.float32) for k, v in out.items()}
    out |= {f"{k}16": out[k] for k in ("l3_fw", "l3_fh", "l3_fh0")}
    for k in ("l0_fw", "l0_fh", "l3_fw16", "l3_fh16", "l3_fh016"):
        high = out[k].astype(np.float16)
        out[k] = np.stack([high, (out[k] - high).astype(np.float16)], 1)
    return out


def complex_matrix(a, b, sign):
    th = 2 * np.pi / N * np.outer(a, b)
    c, s = np.cos(th), sign * np.sin(th)
    m = np.stack([np.stack([c, s], -1), np.stack([-s, c], -1)], 1)
    return m.reshape(2 * len(a), 2 * len(b))


class Program:

    def __init__(self, nc, ctx, ins, out):
        self.nc, self.ins, self.out, self.names = nc, ins, out, set()
        self.ctx = ctx
        self.X = self.sb(ctx, "X", [P, Q, PIX])
        self.ident = self.sb(ctx, "ident", [P, P])
        self.pair = self.sb(ctx, "pair", [P, P])
        self.bn = self.sb(ctx, "bn", [P, NCH, 6])
        self.mv = self.sb(ctx, "mv", [P, 2])
        self.st = self.sb(ctx, "st", [P, Q, 2])
        self.gm = self.sb(ctx, "gm", [P, Q, 2])
        self.var = self.sb(ctx, "var", [P, Q])
        self.sd = self.sb(ctx, "sd", [P, Q])
        self.rstd = self.sb(ctx, "rstd", [P, Q])
        self.shift = self.sb(ctx, "shift", [P, Q])
        self.eps = self.sb(ctx, "eps", [P, 2])
        self.psum = [ctx.enter_context(nc.psum_tensor(f"bank{i}", [P, CH], F32)) for i in range(8)]
        self.zero = self.sb(ctx, "zero", [P, 1])
        self.pace = self.sem("pace")
        self.kf = nc.dram_tensor("kf", (SLOT // 4, P, 2, C // IB, IB * N), F32, kind="Internal").ap()
        self.kf_stored = self.sem("kf_stored")
        self.xf = nc.dram_tensor("xf", (Q, 2, C, KT, KX * 2 * IB), F32, kind="Internal").ap()

    def sb(self, ctx, name, shape, dt=F32):
        return ctx.enter_context(self.nc.sbuf_tensor(name, shape, dt))

    def sem(self, name):
        assert name not in self.names
        self.names.add(name)
        return self.ctx.enter_context(self.nc.semaphore(name))


    def keep_warm(self, pe, n):
        for _ in range(n):
            pe.transpose(self.psum[7][:, 0:P], self.ident[:], self.ident[:])

    def chunk_stats(self, dve, q, c, step):
        dve.sem_inc(self.pace, 1)
        dve.bn_stats(self.bn[:, c, :], self.X[:, q, c * CH:(c + 1) * CH]).then_inc(step, 1)

    def group_stats(self, dve, q, step):
        at = (NCH + 2) * q
        dve.wait_ge(step, at + NCH)
        dve.sem_inc(self.pace, 1)
        dve.bn_aggr(self.mv[:], self.bn[:].rearrange("p a b -> p (a b)")).then_inc(step, 1)
        dve.wait_ge(step, at + NCH + 1)
        dve.tensor_copy(self.st[:, q, 0:1], self.mv[:, 0:1])
        dve.scalar_tensor_tensor(self.st[:, q, 1:2], self.mv[:, 0:1], self.mv[:, 0:1], self.mv[:, 1:2],
                                 ALU.mult, ALU.add).then_inc(step, 1)
        dve.wait_ge(step, at + NCH + 2)

    def stats_stage(self, name, loads=()):
        summed, read, deviation, done = (self.sem(f"{name}_{x}") for x in ("sum", "var", "dev", "norm"))
        gm, sm = self.gm, self.psum[0]
        const = self.sem(f"{name}_const")
        with self.nc.Block() as block:
            @block.sync
            def _(sp):
                for t, n in loads:
                    sp.dma_start(t[:], self.ins[n]).then_inc(const, 16)
                if loads:
                    sp.wait_ge(const, 16 * len(loads))

            @block.tensor
            def _(pe):
                pe.matmul(sm[:, 0:2 * Q], self.pair[:], self.st[:].rearrange("p q t -> p (q t)"),
                          start=True, stop=True).then_inc(summed, 1)

            @block.scalar
            def _(act):
                act.wait_ge(read, 4)
                act.activation(self.sd[:], self.var[:], ACT.Sqrt, bias=self.eps[:, 0:1]).then_inc(deviation, 1)

            @block.vector
            def _(dve):
                dve.wait_ge(summed, 1)
                dve.tensor_copy(gm[:].rearrange("p q t -> p (q t)"), sm[:, 0:2 * Q]).then_inc(read, 1)
                dve.wait_ge(read, 1)
                dve.tensor_tensor(self.var[:], gm[:, :, 0], gm[:, :, 0], ALU.mult).then_inc(read, 1)
                dve.wait_ge(read, 2)
                dve.tensor_tensor(self.var[:], gm[:, :, 1], self.var[:], ALU.subtract).then_inc(read, 1)
                dve.wait_ge(read, 3)
                dve.tensor_scalar(self.var[:], self.var[:], 0.0, None, ALU.max).then_inc(read, 1)
                dve.wait_ge(deviation, 1)
                dve.reciprocal(self.rstd[:], self.sd[:]).then_inc(done, 1)
                dve.wait_ge(done, 1)
                dve.scalar_tensor_tensor(self.shift[:], gm[:, :, 0], -1.0, self.rstd[:], ALU.mult, ALU.mult)

    def normalise(self, act, dst, q, c, ready, patches=False):
        to, of = dst[:, c * CH:(c + 1) * CH], self.X[:, q, c * CH:(c + 1) * CH]
        if patches:
            to = to.rearrange("p (a y x) -> p a y x", a=PS, x=PS)
            of = of.rearrange("p (y a x) -> p a y x", y=PS, x=PS)
        act.activation(to, of, ACT.Identity,
                       scale=self.rstd[:, bass.ds(q, 1)], bias=self.shift[:, bass.ds(q, 1)]).then_inc(ready, 1)


def kernel_spectra_stage(pr, loads, filt):
    nc, ps = pr.nc, pr.psum
    tiles = C // IB
    const, loaded = pr.sem("ks_const"), [[pr.sem(f"ks_load{p}{k}") for k in range(4)] for p in range(2)]
    x_loaded, layer_const = pr.sem("ks_x"), pr.sem("ks_layer_const")
    turned, turned_read = pr.sem("ks_turned"), pr.sem("ks_turned_read")
    made, made_read = pr.sem("ks_made"), pr.sem("ks_made_read")
    stored, step, eps = pr.kf_stored, pr.sem("ks_step"), pr.sem("ks_eps")
    w_tiles = pr.ins["L3_conv_weights"].rearrange("(t o) c h w -> t (o c) (h w)", o=IB)
    x_groups = pr.ins["x"].rearrange("(q b) c h w -> q (b c) (h w)", b=IB)
    with ExitStack() as ctx:
        spec = pr.sb(ctx, "ks_spec", [P, SLOT // 4, 2, IB, N])
        src = [pr.sb(ctx, f"ks_src{p}", [P, PIX]) for p in range(2)]
        tt = [pr.sb(ctx, f"ks_tt{p}", [P, CH]) for p in range(4)]
        cols = pr.sb(ctx, "ks_cols", [P, IB, SLOT, C])
        fw, fh, fh0 = (pr.sb(ctx, f"ks_{n}", [P, P]) for n in ("fw", "fh", "fh0"))
        with nc.Block() as block:
            @block.sync
            def _(sp):
                for t, n in ((pr.ident, "ident"), (pr.pair, "pair"), (fw, "l3_fw"), (fh, "l3_fh"), (fh0, "l3_fh0")):
                    sp.dma_start(t[:], pr.ins[n]).then_inc(const, 16)
                sp.sem_inc(x_loaded, START)
                with sp.Fori(0, tiles // 2) as i:
                    for p in range(2):
                        sp.wait_ge(turned, START + 32 * i + 16 * p - 16)
                        for k in range(4):
                            at = slice(k * PIX // 4, (k + 1) * PIX // 4)
                            sp.dma_start(src[p][:, at], w_tiles[2 * i + p][:, at]).then_inc(loaded[p][k], 16)
                    sp.wait_ge(x_loaded, 16 * i + START)
                    sp.dma_start(pr.X[:, i, :], x_groups[i]).then_inc(x_loaded, 16)
                filt.load(sp)
                for t, n in loads:
                    sp.dma_start(t[:], pr.ins[n]).then_inc(layer_const, 16)
                sp.wait_ge(layer_const, 16 * len(loads))

            @block.tensor
            def _(pe):
                pe.sem_inc(turned, START)
                pe.wait_ge(const, 16 * 5)
                with pe.Fori(0, tiles // 2) as i:
                    for p in range(2):
                        forward_products(pe, pr, src[p], tt, cols, fw, fh, fh0, 32 * i + 16 * p,
                                         turned, turned_read, made, made_read,
                                         lambda j: pe.wait_ge(loaded[p][j // 2], 16 * i + 16))

            @block.vector
            def _(dve):
                dve.memset(pr.eps[:], GN_EPS).then_inc(eps, 1)
                dve.memset(pr.zero[:], 0.0).then_inc(eps, 1)
                filt.clear(dve)
                with dve.Fori(0, tiles // 2) as i:
                    for p in range(2):
                        def stats(s):
                            if p == 1:
                                if s == 0:
                                    dve.wait_ge(x_loaded, START + 16 * i + 16)
                                pr.chunk_stats(dve, i, s, step)

                        copy_turned(dve, ps, tt, cols, 32 * i + 16 * p, turned, turned_read, made, stats)
                    pr.group_stats(dve, i, step)
                filt.find_largest(dve)

            @block.scalar
            def _(act):
                act.sem_inc(made_read, START)
                act.sem_inc(stored, START)
                with act.Fori(0, tiles // 2) as i:
                    for p in range(2):
                        base = 32 * i + 16 * p
                        copy_rows(act, ps, src[p], base, made, made_read)
                        for s in range(SLOT // 4):
                            act.wait_ge(made, base + NCH + s + 1)
                            if s == 0:
                                act.wait_ge(stored, START + 64 * i + 32 * p)
                            act.copy(spec[:, s].rearrange("p r o k -> p o r k"),
                                     ps[4 + s % 4][:].rearrange("p (o r k) -> p o r k", o=IB, r=2)
                                     ).then_inc(made_read, 1)
                        act.wait_ge(made_read, START + base + 16)
                        for part in range(2):
                            act.dma_start(pr.kf[:, :, part, 2 * i + p, :].rearrange("s p n -> p s n"),
                                          spec[:, :, part].rearrange("p s o k -> p s (o k)")).then_inc(stored, 16)


def forward_products(pe, pr, src, tt, cols, fw, fh, fh0, base, turned, turned_read, made, made_read,
                     src_ready):
    ps = pr.psum

    def turn(j):
        src_ready(j)
        if j >= 4:
            pe.wait_ge(turned_read, base + j - 3)
        for k in range(4):
            m = pe.transpose(ps[j % 4][:, k * P:(k + 1) * P], src[:, (4 * j + k) * P:(4 * j + k + 1) * P], pr.ident[:])
        m.then_inc(turned, 1)

    def rows(j):
        pe.wait_ge(turned_read, base + j + 1)
        pe.wait_ge(made_read, START + base + j - 3)
        for k in range(4):
            m = pe.matmul(ps[4 + j % 4][:, k * P:(k + 1) * P], tt[j % 4][:, k * P:(k + 1) * P], fw[:],
                          start=True, stop=True)
        m.then_inc(made, 1)

    AHEAD = 3
    for j in range(AHEAD):
        turn(j)
    for j in range(NCH):
        if j + AHEAD < NCH:
            turn(j + AHEAD)
        rows(j)
    spectra = src[:].rearrange("p (k s) -> p k s", s=SLOT)

    def turn_columns(s):
        if s == 0:
            pe.wait_ge(made_read, START + base + NCH)
        if s >= 4:
            pe.wait_ge(turned_read, base + NCH + s - 3)
        for k in range(4):
            m = pe.transpose(ps[s % 4][:, k * P:(k + 1) * P], spectra[:, :, SLOT_AT[s][k]], pr.ident[:])
        m.then_inc(turned, 1)

    def columns(s):
        pe.wait_ge(turned_read, base + NCH + s + 1)
        if s >= 4:
            pe.wait_ge(made_read, START + base + NCH + s - 3)
        for b in range(IB):
            m = pe.matmul(ps[4 + s % 4][:, b * P:(b + 1) * P],
                          cols[:, b, 4 * s:4 * s + 4].rearrange("p s c -> p (s c)"),
                          fh[:], start=True, stop=True)
        if s == 0:
            for b in range(IB):
                m = pe.matmul(ps[4][0:C, b * P:(b + 1) * P], cols[:, b, 0], fh0[:],
                              start=True, stop=True)
        m.then_inc(made, 1)

    for s in range(AHEAD):
        turn_columns(s)
    for s in range(SLOT // 4):
        if s + AHEAD < SLOT // 4:
            turn_columns(s + AHEAD)
        columns(s)


def copy_turned(dve, ps, tt, cols, base, turned, turned_read, made, after=lambda s: None):
    for j in range(NCH):
        dve.wait_ge(turned, START + base + j + 1)
        if j >= 4:
            dve.wait_ge(made, base + j - 3)
        dve.tensor_copy(tt[j % 4][:], ps[j % 4][:]).then_inc(turned_read, 1)
    for s in range(SLOT // 4):
        dve.wait_ge(turned, START + base + NCH + s + 1)
        dve.tensor_copy(cols[:, :, 4 * s:4 * s + 4].rearrange("p b s c -> p s b c"),
                        ps[s % 4][:].rearrange("p (s b c) -> p s b c", s=4, b=IB)).then_inc(turned_read, 1)
        after(s)


def copy_rows(act, ps, src, base, made, made_read, after=lambda j: None):
    for j in range(NCH):
        act.wait_ge(made, base + j + 1)
        act.copy(src[:, j * CH:(j + 1) * CH], ps[4 + j % 4][:]).then_inc(made_read, 1)
        after(j)


class Forward:

    def __init__(self, pr, ctx, name, mats, slot_at, rows_by_act, norm_by_act, norm_by_dve):
        self.pr, self.slot_at = pr, slot_at
        self.norm_by_act, self.norm_by_dve = norm_by_act, norm_by_dve
        self.by = [1 if j % 2 and rows_by_act else 0 for j in range(NCH)]
        self.fw, self.fh, self.fh0 = mats
        self.turned, self.turned_read, self.high, self.made, self.kept = (
            pr.sem(f"{name}_{n}") for n in ("turned", "turned_read", "high", "made", "kept"))
        self.ready = [pr.sem(f"{name}_ready{c}") for c in range(NCH)]
        self.rows_read = [pr.sem(f"{name}_rows_read{e}") for e in range(2)]
        self.S = len(slot_at)
        self.G = NCH + self.S
        self.RW = 2 * 2 * 4 * self.S
        self.src = pr.sb(ctx, f"{name}_src", [P, PIX])
        self.th, self.tl = ([pr.sb(ctx, f"{name}_{n}{p}", [P, CH], F16) for p in range(4)] for n in ("th", "tl"))
        self.rows = pr.sb(ctx, f"{name}_rows", [P, N, 2, 4 * self.S])
        self.ch, self.cl = (pr.sb(ctx, f"{name}_{n}", [P, IB, 4 * self.S, C], F16) for n in ("ch", "cl"))

    def wait_rows(self, pe, q, j):
        for e in range(2):
            n = self.by[:j + 1].count(e)
            if n:
                pe.wait_ge(self.rows_read[e], self.by.count(e) * q + n)

    def products(self, pe):
        ps, S, G, RW = self.pr.psum, self.S, self.G, self.RW
        AHEAD = 3

        def product(to, h, l, m):
            pe.matmul(to, h, m[:, 0], start=True, stop=False)
            pe.matmul(to, h, m[:, 1], start=False, stop=False)
            return pe.matmul(to, l, m[:, 0], start=False, stop=True)

        pe.sem_inc(self.turned, START)
        self.pr.keep_warm(pe, 7)
        with pe.Fori(0, Q) as q:
            def turn(j):
                pe.wait_ge(self.ready[j], q + 1)
                if j >= 4:
                    pe.wait_ge(self.turned_read, G * q + j - 3)
                for k in range(4):
                    at = (4 * j + k) * P
                    m = pe.transpose(ps[j % 4][:, k * P:(k + 1) * P], self.src[:, at:at + P], self.pr.ident[:])
                m.then_inc(self.turned, 1)

            for j in range(AHEAD):
                turn(j)
            for j in range(NCH):
                if j + AHEAD < NCH:
                    turn(j + AHEAD)
                pe.wait_ge(self.turned_read, G * q + j + 1)
                if j < 4:
                    pe.wait_ge(self.kept, START + S * q + j - 3)
                else:
                    self.wait_rows(pe, q, j - 4)
                for k in range(4):
                    at = slice(k * P, (k + 1) * P)
                    m = product(ps[4 + j % 4][:, k * RW:(k + 1) * RW], self.th[j % 4][:, at], self.tl[j % 4][:, at],
                                self.fw)
                m.then_inc(self.made, 1)
            self.wait_rows(pe, q, NCH - 1)

            def turn_columns(s):
                if s >= 4:
                    pe.wait_ge(self.turned_read, G * q + NCH + s - 3)
                for k in range(4):
                    m = pe.transpose(ps[s % 4][:, k * P:(k + 1) * P],
                                     self.rows[:, :, :, self.slot_at[s][k]].rearrange("p h r -> p (h r)"),
                                     self.pr.ident[:])
                m.then_inc(self.turned, 1)

            for s in range(AHEAD):
                turn_columns(s)
            for s in range(S):
                if s + AHEAD < S:
                    turn_columns(s + AHEAD)
                pe.wait_ge(self.turned_read, G * q + NCH + s + 1)
                if s >= 4:
                    pe.wait_ge(self.kept, START + S * q + s - 3)
                width = self.fh.shape[-1]
                for b in range(IB):
                    at = slice(4 * s, 4 * s + 4)
                    m = product(ps[4 + s % 4][:, b * width:(b + 1) * width],
                                self.ch[:, b, at].rearrange("p s c -> p (s c)"),
                                self.cl[:, b, at].rearrange("p s c -> p (s c)"), self.fh)
                if s == 0 and self.fh0 is not None:
                    for b in range(IB):
                        m = product(ps[4][0:C, b * width:(b + 1) * width], self.ch[:, b, 0], self.cl[:, b, 0],
                                    self.fh0)
                m.then_inc(self.made, 1)

    def copy_rows(self, eng, copy, q, j):
        eng.wait_ge(self.made, self.G * q + j + 1)
        copy(self.rows[:, ROWS * j:ROWS * j + ROWS].rearrange("p h r k -> p (h r k)"),
             self.pr.psum[4 + j % 4][:, 0:4 * self.RW]).then_inc(self.rows_read[self.by[j]], 1)

    def high_parts(self, act, keep):
        pr, ps, S, G = self.pr, self.pr.psum, self.S, self.G
        act.sem_inc(self.kept, START)

        def group(q, more):
            def normalise_next(f):
                if more and f in self.norm_by_act:
                    c = self.norm_by_act[f]
                    pr.normalise(act, self.src, q + 1, c, self.ready[c])

            for j in range(NCH):
                act.wait_ge(self.turned, START + G * q + j + 1)
                if j >= 4:
                    act.wait_ge(self.made, G * q + j - 3)
                act.copy(self.th[j % 4][:], ps[j % 4][:]).then_inc(self.high, 1)
                normalise_next(j)
                if j > 1 and self.by[j - 2]:
                    self.copy_rows(act, act.copy, q, j - 2)
            for j in range(NCH - 2, NCH):
                if self.by[j]:
                    self.copy_rows(act, act.copy, q, j)

            def keep_filling(s):
                act.wait_ge(self.made, G * q + NCH + s + 1)
                keep(q, s).then_inc(self.kept, 1)

            for s in range(S):
                act.wait_ge(self.turned, START + G * q + NCH + s + 1)
                act.copy(self.ch[:, :, 4 * s:4 * s + 4].rearrange("p b s c -> p s b c"),
                         ps[s % 4][:].rearrange("p (s b c) -> p s b c", s=4, b=IB)).then_inc(self.high, 1)
                normalise_next(NCH + s)
                if s >= 3:
                    keep_filling(s - 3)
            for s in range(S - 3, S):
                keep_filling(s)

        for c in range(4, NCH):
            pr.normalise(act, self.src, 0, c, self.ready[c])
        with act.Fori(0, Q - 1) as q:
            group(q, True)
        group(Q - 1, False)

    def low_parts(self, dve):
        pr, ps, S, G = self.pr, self.pr.psum, self.S, self.G

        def normalise(q, c):
            at = slice(c * CH, (c + 1) * CH)
            dve.tensor_scalar(self.src[:, at], pr.X[:, q, at], pr.rstd[:, bass.ds(q, 1)], pr.shift[:, bass.ds(q, 1)],
                              ALU.mult, ALU.add).then_inc(self.ready[c], 1)

        def group(q, more):
            def normalise_next(f):
                if more and f in self.norm_by_dve:
                    normalise(q + 1, self.norm_by_dve[f])

            for j in range(NCH):
                dve.wait_ge(self.high, G * q + j + 1)
                dve.tensor_tensor(self.tl[j % 4][:], ps[j % 4][:], self.th[j % 4][:], ALU.subtract
                                  ).then_inc(self.turned_read, 1)
                normalise_next(j)
                if j and not self.by[j - 1]:
                    self.copy_rows(dve, dve.tensor_copy, q, j - 1)
            if not self.by[NCH - 1]:
                self.copy_rows(dve, dve.tensor_copy, q, NCH - 1)
            for s in range(S):
                dve.wait_ge(self.high, G * q + NCH + s + 1)
                at = slice(4 * s, 4 * s + 4)
                dve.tensor_tensor(self.cl[:, :, at].rearrange("p b s c -> p s b c"),
                                  ps[s % 4][:].rearrange("p (s b c) -> p s b c", s=4, b=IB),
                                  self.ch[:, :, at].rearrange("p b s c -> p s b c"), ALU.subtract
                                  ).then_inc(self.turned_read, 1)
                normalise_next(NCH + s)

        for c in range(4):
            normalise(0, c)
        with dve.Fori(0, Q - 1) as q:
            group(q, True)
        group(Q - 1, False)


def l0_forward_stage(pr, filt, mats, xb, wb, w_loaded, xb_loaded):
    nc, ps = pr.nc, pr.psum
    negated, moved = pr.sem("f0_negated"), pr.sem("f0_moved")
    S = KT // 4
    with ExitStack() as ctx:
        fwd = Forward(pr, ctx, "f0", mats, [[S * k + s for k in range(4)] for s in range(S)],
                      False, {1: 0, 3: 1, 5: 2, 7: 3, 9: 4, 11: 5}, {8: 6, 10: 7})
        xm = pr.sb(ctx, "f0_xm", [P, 2, S, KX, 2, IB])
        with nc.Block() as block:
            @block.sync
            def _(sp):
                sp.sem_inc(moved, START)
                for w in range(4):
                    for part, n in enumerate(("L0_conv_weights_r", "L0_conv_weights_i")):
                        to = (w % 2 * 2 + part) * C
                        sp.dma_start(wb[to:to + C, w // 2].rearrange("p o x y -> p (o x y)"),
                                     pr.ins[n][w].rearrange("i o x y -> i (o x y)")).then_inc(w_loaded, 16)
                with sp.Fori(0, Q - 1) as q:
                    sp.wait_ge(negated, S * q + S)
                    for part in range(2):
                        sp.dma_start(pr.xf[q, part].rearrange("c (s k) n -> s c (k n)", s=4),
                                     xm[:, part].rearrange("p s k r b -> p (s k r b)")).then_inc(moved, 16)
                    sp.wait_ge(moved, START + 32 * q + 32)
                    for w in range(4):
                        for part in range(2):
                            to = (w % 2 * 2 + part) * C
                            n = len(L0_BLOCKS[w])
                            sp.dma_start(xb[to:to + C, w // 2, q, :, 0:n].rearrange("c k x r b -> c k (x r b)"),
                                         pr.xf[q, part, :, :, L0_OFF[w] * 2 * IB:(L0_OFF[w] + n) * 2 * IB]
                                         ).then_inc(xb_loaded, 16)

            @block.tensor
            def _(pe):
                filt.spread_largest(pe)
                fwd.products(pe)

            def last_group(eng, copy, blocks):
                eng.wait_ge(negated, S * Q)
                for w in blocks:
                    n = len(L0_BLOCKS[w])
                    for part in range(2):
                        to = (w % 2 * 2 + part) * C
                        for k in range(4):
                            copy(xb[to:to + C, w // 2, Q - 1, S * k:S * k + S, 0:n].rearrange(
                                "c s x r b -> c s (x r b)"),
                                xm[k * C:(k + 1) * C, part, :, L0_OFF[w]:L0_OFF[w] + n].rearrange(
                                    "c s x r b -> c s (x r b)"))

            @block.scalar
            def _(act):
                def keep(q, s):
                    if s == 0:
                        act.wait_ge(moved, START + 32 * q)
                    made = ps[4 + s % 4][:, 0:IB * 2 * KX].rearrange("p (b k r) -> p k r b", b=IB, r=2)
                    act.copy(xm[:, 0, s], made)
                    return act.copy(xm[:, 1, s, :, 1, :], made[:, :, 0, :])

                fwd.high_parts(act, keep)
                last_group(act, act.copy, (0, 1))

            @block.vector
            def _(dve):
                filt.find_power(dve)
                fwd.low_parts(dve)
                last_group(dve, dve.tensor_copy, (2, 3))

            @block.gpsimd
            def _(pool):
                with pool.Fori(0, Q) as q:
                    for s in range(S):
                        pool.wait_ge(fwd.kept, START + S * q + s + 1)
                        pool.tensor_tensor(xm[:, 1, s, :, 0, :], pr.zero[:].unsqueeze(2).broadcast_to([P, KX, IB]),
                                           xm[:, 0, s, :, 1, :], ALU.subtract).then_inc(negated, 1)


def l0_mix_stage(pr, filt, xb, wb, w_loaded, xb_loaded, y):
    nc, ps = pr.nc, pr.psum
    mixed = pr.sem("m0_mixed")
    used = [len(b) for b in L0_BLOCKS]
    PAIR = 4 * K2
    seq = pr.sem("m0_seq")
    with ExitStack() as ctx:
        scaled = pr.sb(ctx, "c2_scaled", [P, C, KS * KS])
        parts = [pr.sb(ctx, f"c2_part{i}", [P, C, KS * KS], F16) for i in range(2)]
        with nc.Block() as block:
            @block.tensor
            def _(pe):
                pe.wait_ge(w_loaded, 16 * 8)
                pe.wait_ge(xb_loaded, 16 * 8 * (Q - 1))
                for t in range(KT // 4):
                    for n in range(PAIR):
                        for w in range(4):
                            m = PAIR * t + (n + PAIR // 2 * (w % 2)) % PAIR
                            kt, x = m // K2, m % K2
                            if x >= used[w]:
                                continue
                            at = slice(w % 2 * 2 * C, (w % 2 + 1) * 2 * C)
                            last = pe.matmul(ps[m // 16][w * C:(w + 1) * C, m % 16 * 2 * B:(m % 16 + 1) * 2 * B],
                                             wb[at, w // 2, :, x, kt],
                                             xb[at, w // 2, :, kt, x].rearrange("p q r b -> p r q b"),
                                             start=True, stop=True)
                    last.then_inc(mixed, 1)

            def copy_out(copy, t, bank):
                for kt in (2 * bank, 2 * bank + 1):
                    for w in range(4):
                        copy(y[kt % 4 * C:(kt % 4 + 1) * C, t, L0_OFF[w]:L0_OFF[w] + used[w]].rearrange(
                            "p x r b -> p (x r b)"),
                            ps[bank][w * C:(w + 1) * C, kt % 2 * CH // 2:kt % 2 * CH // 2 + used[w] * 2 * B])

            @block.vector
            def _(dve):
                filt.lay_out(dve, scaled, parts, seq)
                dve.wait_ge(pr.kf_stored, START + 32 * (C // IB))
                for t in range(KT // 4):
                    dve.wait_ge(mixed, t + 1)
                    copy_out(dve.tensor_copy, t, 2 * t)

            @block.scalar
            def _(act):
                act.wait_ge(pr.kf_stored, START + 32 * (C // IB))
                for t in range(KT // 4):
                    act.wait_ge(mixed, t + 1)
                    copy_out(act.copy, t, 2 * t + 1)

            @block.gpsimd
            def _(pool):
                pool.wait_ge(pr.kf_stored, START + 32 * (C // IB))
                pool.memset(y[:, :, KX:].rearrange("p s x r b -> p s (x r b)"), 0.0)


def inverse_stage(pr, name, y, slots, modes, mats, rows4, last):
    nc, ps = pr.nc, pr.psum
    K = P // 2 if 2 * modes <= P // 2 else P
    SG = slots // 4
    HG = N // rows4 // 4
    AHEAD = 3
    per = CH // (rows4 * N)
    staged, turned, turned_read = (pr.sem(f"{name}_{n}") for n in ("staged", "turned", "turned_read"))
    made, made_read, turned2, turned2_read = (pr.sem(f"{name}_{n}") for n in
                                              ("made", "made_read", "turned2", "turned2_read"))
    pixels, added, step, stored = (pr.sem(f"{name}_{n}") for n in ("pixels", "added", "step", "stored"))
    padded = pr.sem(f"{name}_padded")
    out_groups = pr.out.rearrange("(q b) c h w -> q (b c) (h w)", b=IB)
    with ExitStack() as ctx:
        yq = pr.sb(ctx, f"{name}_yq", [P, SG, modes, 2, IB])
        cols = pr.sb(ctx, f"{name}_cols", [P, slots, IB, C])
        rows = pr.sb(ctx, f"{name}_rows", [P, N, slots, 2])
        tt = [pr.sb(ctx, f"{name}_tt{p}", [P, CH]) for p in range(4)]
        mh, mh0, mw = mats
        with nc.Block() as block:
            @block.sync
            def _(sp):
                if last:
                    with sp.Fori(0, Q) as q:
                        for part in range(4):
                            sp.wait_ge(added, START + NCH * q + NCH // 4 * (part + 1))
                            at = slice(part * PIX // 4, (part + 1) * PIX // 4)
                            sp.dma_start(out_groups[q][:, at], pr.X[:, q, at]).then_inc(stored, 16)
                    sp.wait_ge(stored, 16 * 4 * Q)

            def stage(eng, q, s):
                eng.tensor_copy(yq[:, s].rearrange("p k r b -> p (k r) b"),
                                y[:, s, :, :, bass.ds(IB * q, IB)].rearrange("p k r b -> p (k r) b")
                                ).then_inc(staged, 1)

            @block.gpsimd
            def _(pool):
                if K < P:
                    pool.memset(cols[K:P], 0.0).then_inc(padded, 1)
                else:
                    pool.sem_inc(padded, 1)
                with pool.Fori(1, Q) as q:
                    pool.wait_ge(turned, START + SG * q)
                    for s in range(SG):
                        stage(pool, q, s)

            @block.tensor
            def _(pe):
                pe.sem_inc(turned, START)
                with pe.Fori(0, Q) as q:
                    def turn(s):
                        pe.wait_ge(staged, SG * q + s + 1)
                        if s >= 4:
                            pe.wait_ge(turned_read, SG * q + s - 3)
                        pe.sem_inc(pr.pace, 1)
                        for b in range(IB):
                            m = pe.transpose(ps[s % 4][0:K, b * P:(b + 1) * P],
                                             yq[:, s].rearrange("p k r b -> p (k r) b")[:, :, b], pr.ident[:])
                        m.then_inc(turned, 1)

                    for s in range(AHEAD):
                        turn(s)
                    pe.wait_ge(padded, 1)
                    for s in range(SG):
                        if s + AHEAD < SG:
                            turn(s + AHEAD)
                        pe.wait_ge(turned_read, SG * q + s + 1)
                        if s < 4:
                            pe.wait_ge(added, START + NCH * q + s - 3)
                        else:
                            pe.wait_ge(made_read, SG * q + s - 3)
                        for k in range(4):
                            m = pe.matmul(ps[4 + s % 4][:, k * P:(k + 1) * P],
                                          cols[:, 4 * s + k].rearrange("p b o -> p (b o)"),
                                          (mh0 if s == 0 and k == 0 else mh)[:], start=True, stop=True)
                        m.then_inc(made, 1)
                    pe.wait_ge(made_read, SG * q + SG)

                    def turn_rows(g):
                        if g >= 4:
                            pe.wait_ge(turned2_read, HG * q + g - 3)
                        for k in range(4):
                            h = (4 * g + k) * rows4
                            m = pe.transpose(ps[g % 4][:, k * P:(k + 1) * P],
                                             rows[:, h:h + rows4].rearrange("p h s r -> p (h s r)"), pr.ident[:])
                        m.then_inc(turned2, 1)

                    for g in range(AHEAD):
                        turn_rows(g)
                    for c in range(NCH):
                        g, first = c * per // 4, c * per % 4
                        if first == 0 and g + AHEAD < HG:
                            turn_rows(g + AHEAD)
                        if first == 0:
                            pe.wait_ge(turned2_read, HG * q + g + 1)
                        if c >= 4:
                            pe.wait_ge(added, START + NCH * q + c - 3)
                        for k in range(per):
                            n = rows4 * N
                            m = pe.matmul(ps[4 + c % 4][:, k * n:(k + 1) * n],
                                          tt[g % 4][:, (first + k) * P:(first + k + 1) * P], mw[:],
                                          start=True, stop=True)
                        m.then_inc(pixels, 1)

            @block.vector
            def _(dve):
                dve.sem_inc(added, START)
                for s in range(SG):
                    stage(dve, 0, s)
                with dve.Fori(0, Q) as q:
                    for c in range(NCH):
                        dve.wait_ge(pixels, NCH * q + c + 1)
                        x = pr.X[:, q, c * CH:(c + 1) * CH]
                        dve.tensor_tensor(x, x, ps[4 + c % 4][:], ALU.add).then_inc(added, 1)
                        if not last and c:
                            dve.wait_ge(added, START + NCH * q + c)
                            pr.chunk_stats(dve, q, c - 1, step)
                    if not last:
                        dve.wait_ge(added, START + NCH * q + NCH)
                        pr.chunk_stats(dve, q, NCH - 1, step)
                        pr.group_stats(dve, q, step)

            @block.scalar
            def _(act):
                with act.Fori(0, Q) as q:
                    def copy_columns(s):
                        act.wait_ge(turned, START + SG * q + s + 1)
                        act.copy(cols[0:K, 4 * s:4 * s + 4].rearrange("p s b o -> p b s o"),
                                 ps[s % 4][0:K, :].rearrange("p (b s o) -> p b s o", b=IB, s=4)
                                 ).then_inc(turned_read, 1)

                    for s in range(AHEAD):
                        copy_columns(s)
                    for s in range(SG):
                        if s + AHEAD < SG:
                            copy_columns(s + AHEAD)
                        act.wait_ge(made, SG * q + s + 1)
                        act.copy(rows[:, :, 4 * s:4 * s + 4, :].rearrange("p h s r -> p s h r"),
                                 ps[4 + s % 4][:].rearrange("p (s h r) -> p s h r", s=4, r=2)).then_inc(made_read, 1)
                    for g in range(HG):
                        act.wait_ge(turned2, HG * q + g + 1)
                        if g >= 4:
                            act.wait_ge(pixels, NCH * q + (g - 3) * 4 // per)
                        act.copy(tt[g % 4][:], ps[g % 4][:]).then_inc(turned2_read, 1)


def l1_edge_stage(pr, means, tables, edge, mm):
    nc, ps = pr.nc, pr.psum
    ready, window, meant = (pr.sem(f"e1_{n}") for n in ("ready", "window", "meant"))
    seq, root, picked, spread = (pr.sem(f"e1_{n}") for n in ("seq", "root", "picked", "spread"))
    zeroed, high = pr.sem("e1_zeroed"), pr.sem("e1_high")
    split = [pr.sem(f"e1_split{p}") for p in range(2)]
    HC = NCH // 2
    gained, mask, mats = (pr.sem(f"e1_{n}") for n in ("gained", "mask", "mats"))
    HALO = ROWS + 2
    with ExitStack() as ctx:
        src = pr.sb(ctx, "e1_src", [P, PIX])
        hi, lo16 = (pr.sb(ctx, f"e1_{n}", [P, Q, PIX], F16) for n in ("high_part", "low_part"))
        wide, pick, spread_m = means
        dft, same, band, high_mask = tables
        gain, mk, md = pr.sb(ctx, "e1_gain", [NB, 1]), pr.sb(ctx, "e1_mk", [P, 2]), pr.sb(ctx, "e1_md", [P, 2, P])
        wq = [pr.sb(ctx, f"e1_wq{p}", [P, 252], F16) for p in range(2)]
        m = pr.sb(ctx, "e1_m", [P, HALO, N + 2])
        d = pr.sb(ctx, "e1_d", [P, HALO, N])
        v = pr.sb(ctx, "e1_v", [P, HALO, N])
        g1, g2 = pr.sb(ctx, "e1_g1", [P, ROWS, N]), pr.sb(ctx, "e1_g2", [P, ROWS, N])
        es = pr.sb(ctx, "e1_es", [P, PS])
        eb = pr.sb(ctx, "e1_eb", [B, N])
        lo = pr.sb(ctx, "e1_lo", [B, 4])
        sq_eps = pr.sb(ctx, "e1_eps", [P, 1])
        nought = pr.sb(ctx, "e1_nought", [P, CH], F16)
        with nc.Block() as block:
            @block.sync
            def _(sp):
                sp.dma_start(gain[:], pr.ins["L1_conv_gain"].rearrange("a n -> n a")).then_inc(gained, 16)

            @block.scalar
            def _(act):
                with act.Fori(0, Q) as q:
                    for j in range(NCH):
                        act.wait_ge(split[j % 2], START + HC * (q - 1) + j // 2 + 1)
                        pr.normalise(act, src, q, j, ready)
                act.wait_ge(seq, 10)
                act.activation(g1[:], g2[:], ACT.Sqrt, bias=sq_eps[:, 0:1]).then_inc(root, 1)

            @block.tensor
            def _(pe):
                pr.keep_warm(pe, 16)
                pe.wait_ge(zeroed, 3)
                pe.matmul(ps[0][:], nought[:, 0:P], nought[:], start=True, stop=False, skip_group_check=True)
                pe.matmul(ps[1][:, 0:P], nought[:, 0:P], nought[:, 0:P], start=True, stop=False,
                          skip_group_check=True)
                with pe.Fori(0, Q // 2) as i:
                    for p in range(2):
                        q = 2 * i + p
                        pe.wait_ge(window, q + 1)
                        for s in range(NCH):
                            w = wq[p][:, 124 - B * s:124 - B * s + P]
                            pe.wait_ge(split[s % 2], START + HC * q + s // 2 + 1)
                            for part in (hi, lo16):
                                rows = part[:, q, :].rearrange("p (h w) -> p h w", w=N)
                                last = pe.matmul(ps[0][:], w, part[:, q, s * CH:(s + 1) * CH], start=False, stop=False,
                                                 skip_group_check=True)
                                if s > 0:
                                    pe.matmul(ps[1][:, 0:N], w, rows[:, ROWS * s - 1, :], start=False, stop=False,
                                              skip_group_check=True)
                                    above = wq[p][:, 124 - B * (s - 1):124 - B * (s - 1) + P]
                                    last = pe.matmul(ps[1][:, N:2 * N], above, rows[:, ROWS * s, :], start=False,
                                                     stop=False, skip_group_check=True)
                        last.then_inc(meant, 1)
                pe.wait_ge(gained, 16)
                pe.matmul(ps[4][:, 0:1], band[:], gain[:], start=True, stop=True).then_inc(mask, 1)
                pe.wait_ge(mats, 4)
                pe.matmul(ps[5][:, 0:2 * P], dft[:], md[:].rearrange("p t n -> p (t n)"), start=True,
                          stop=True).then_inc(mask, 1)
                pe.wait_ge(seq, 11)
                for s in range(PS):
                    last = pe.matmul(ps[2][0:B, s * PS:(s + 1) * PS], pick[:, B * s:B * s + B], es[:],
                                     start=True, stop=True)
                last.then_inc(picked, 1)
                pe.wait_ge(seq, 18)
                for q in range(Q):
                    last = pe.matmul(ps[3][:, q * N:(q + 1) * N], spread_m[:, q * P:(q + 1) * P], eb[:],
                                     start=True, stop=True)
                last.then_inc(spread, 1)

            def low_part(eng, q, j):
                at = slice(j * CH, (j + 1) * CH)
                eng.wait_ge(high, NCH * q + j + 1)
                eng.tensor_tensor(lo16[:, q, at], src[:, at], hi[:, q, at], ALU.subtract).then_inc(split[j % 2], 1)

            @block.gpsimd
            def _(pool):
                pool.sem_inc(split[1], START)
                with pool.Fori(0, Q) as q:
                    for j in range(1, NCH, 2):
                        low_part(pool, q, j)

            @block.vector
            def _(dve):
                count = [0]

                def then(ins):
                    count[0] += 1
                    ins.then_inc(seq, 1)
                    dve.wait_ge(seq, count[0])

                dve.memset(m[:], 0.0).then_inc(zeroed, 1)
                dve.memset(sq_eps[:], 1e-6).then_inc(zeroed, 1)
                dve.memset(nought[:], 0.0).then_inc(zeroed, 1)
                dve.sem_inc(split[0], START)
                dve.sem_inc(meant, START)
                with dve.Fori(0, Q // 2) as i:
                    for p in range(2):
                        q = 2 * i + p
                        dve.wait_ge(meant, START + q - 1)
                        dve.sem_inc(pr.pace, 1)
                        dve.tensor_copy(wq[p][:], wide[:, bass.ds(12 - IB * p - 2 * IB * i, 252)]).then_inc(window, 1)
                        for j in range(NCH):
                            at = slice(j * CH, (j + 1) * CH)
                            dve.wait_ge(ready, NCH * q + j + 1)
                            dve.tensor_copy(hi[:, q, at], src[:, at]).then_inc(high, 1)
                            if j % 2:
                                low_part(dve, q, j - 1)
                dve.wait_ge(meant, START + Q)
                dve.wait_ge(zeroed, 3)
                dve.tensor_copy(m[:, 1:1 + ROWS, 1:1 + N], ps[0][:].rearrange("p (h w) -> p h w", w=N))
                then(dve.tensor_copy(m[:, 0:HALO:HALO - 1, 1:1 + N],
                                     ps[1][:, 0:2 * N].rearrange("p (h w) -> p h w", w=N)))
                dve.scalar_tensor_tensor(v[:], m[:, :, 1:1 + N], 2.0, m[:, :, 0:N], ALU.mult, ALU.add)
                then(dve.tensor_tensor(d[:], m[:, :, 2:2 + N], m[:, :, 0:N], ALU.subtract))
                dve.wait_ge(mask, 1)
                dve.tensor_scalar(mk[:, 0:1], ps[4][:, 0:1], 0.0, None, ALU.max).then_inc(mats, 1)
                then(dve.tensor_tensor(v[:], v[:], m[:, :, 2:2 + N], ALU.add))
                dve.wait_ge(mats, 1)
                dve.tensor_tensor(mk[:, 1:2], mk[:, 0:1], high_mask[:], ALU.mult).then_inc(mats, 1)
                then(dve.scalar_tensor_tensor(g1[:], d[:, 1:1 + ROWS], 2.0, d[:, 0:ROWS], ALU.mult, ALU.add))
                then(dve.tensor_tensor(g1[:], g1[:], d[:, 2:2 + ROWS], ALU.add))
                dve.wait_ge(mats, 2)
                for t in range(2):
                    dve.tensor_scalar(md[:, t, :], dft[:], mk[:, t:t + 1], None, ALU.mult).then_inc(mats, 1)
                then(dve.tensor_tensor(g2[:], v[:, 2:2 + ROWS], v[:, 0:ROWS], ALU.subtract))
                then(dve.tensor_tensor(g2[:], g2[:], g2[:], ALU.mult))
                then(dve.tensor_tensor(g1[:], g1[:], g1[:], ALU.mult))
                then(dve.tensor_tensor(g2[:], g2[:], g1[:], ALU.add))
                then(dve.memset(lo[:], 0.0))
                dve.wait_ge(mask, 2)
                for t in range(2):
                    dve.tensor_tensor(mm[:, t, :], ps[5][:, t * P:(t + 1) * P], same[:], ALU.mult)
                dve.wait_ge(root, 1)
                then(dve.tensor_reduce(es[:], g1[:].rearrange("p y (c x) -> p c y x", x=PS), AX.XY, ALU.add))
                dve.wait_ge(picked, 1)
                then(dve.tensor_scalar(eb[:], ps[2][0:B, 0:N], 1.0 / (PS * PS), None, ALU.mult))
                then(dve.tensor_reduce(lo[:, 0:1], eb[:], AX.X, ALU.min))
                then(dve.tensor_scalar(eb[:], eb[:], lo[:, 0:1], None, ALU.subtract))
                then(dve.tensor_reduce(lo[:, 1:2], eb[:], AX.X, ALU.max))
                then(dve.tensor_scalar(lo[:, 2:3], lo[:, 1:2], 1e-6, None, ALU.add))
                then(dve.reciprocal(lo[:, 3:4], lo[:, 2:3]))
                then(dve.tensor_scalar(eb[:], eb[:], lo[:, 3:4], 0.5, ALU.mult, ALU.mult))
                dve.wait_ge(spread, 1)
                dve.tensor_copy(edge[:].rearrange("p q n -> p (q n)"), ps[3][:, 0:Q * N])


def l1_filter_stage(pr, mm, edge):
    nc, ps = pr.nc, pr.psum
    ready, turned = pr.sem("p1_ready"), pr.sem("p1_turned")
    turned_read, filtered, added, scaled = (pr.sem(f"p1_{n}") for n in ("turned_read", "filtered", "added", "scaled"))
    finished, step = pr.sem("p1_finished"), pr.sem("p1_step")
    with ExitStack() as ctx:
        src = pr.sb(ctx, "p1_src", [P, PIX])
        tt = [pr.sb(ctx, f"p1_tt{p}", [P, CH]) for p in range(2)]
        tmp = [pr.sb(ctx, f"p1_tmp{p}", [P, PS, PS * PS]) for p in range(2)]
        with nc.Block() as block:
            @block.tensor
            def _(pe):
                pe.sem_inc(turned, START)
                pr.keep_warm(pe, 6)
                with pe.Fori(0, Q) as q:
                    def turn(j):
                        pe.wait_ge(ready, NCH * q + j + 1)
                        if j >= 2:
                            pe.wait_ge(turned_read, NCH * q + j - 1)
                        for k in range(4):
                            m = pe.transpose(ps[j % 2][:, k * P:(k + 1) * P],
                                             src[:, (4 * j + k) * P:(4 * j + k + 1) * P], pr.ident[:])
                        m.then_inc(turned, 1)

                    turn(0)
                    for j in range(NCH):
                        if j + 1 < NCH:
                            turn(j + 1)
                        pe.wait_ge(turned_read, NCH * q + j + 1)
                        if j == 0:
                            pe.wait_ge(added, START + NCH * q)
                        if j >= 2:
                            pe.wait_ge(added, START + NCH * q + j - 1)
                        for t in range(2):
                            for k in range(4):
                                m = pe.matmul(ps[2 + 2 * (j % 2) + t][:, k * P:(k + 1) * P],
                                              tt[j % 2][:, k * P:(k + 1) * P], mm[:, t, :], start=True, stop=True)
                        m.then_inc(filtered, 1)

            @block.scalar
            def _(act):
                with act.Fori(0, Q) as q:
                    act.wait_ge(turned, START + NCH * q)
                    for j in range(3):
                        pr.normalise(act, src, q, j, ready, True)
                    for j in range(NCH):
                        act.wait_ge(turned, START + NCH * q + j + 1)
                        if j >= 2:
                            act.wait_ge(filtered, NCH * q + j - 1)
                        act.copy(tt[j % 2][:], ps[j % 2][:]).then_inc(turned_read, 1)
                        if j + 3 < NCH:
                            pr.normalise(act, src, q, j + 3, ready, True)

            @block.vector
            def _(dve):
                dve.sem_inc(added, START)
                with dve.Fori(0, Q) as q:
                    for j in range(NCH):
                        dve.wait_ge(filtered, NCH * q + j + 1)
                        if j >= 2:
                            dve.wait_ge(finished, NCH * q + j - 1)
                        dve.tensor_tensor(tmp[j % 2][:], ps[3 + 2 * (j % 2)][:].rearrange("p (a b) -> p a b", a=PS),
                                          edge[:, q, PS * j:PS * j + PS].unsqueeze(2).broadcast_to([P, PS, PS * PS]),
                                          ALU.mult).then_inc(scaled, 1)
                        x = pr.X[:, q, j * CH:(j + 1) * CH].rearrange("p (y a x) -> p a y x", y=PS, x=PS)
                        dve.tensor_tensor(x, x, ps[2 + 2 * (j % 2)][:].rearrange("p (a y x) -> p a y x", a=PS, x=PS),
                                          ALU.add).then_inc(added, 1)
                        if j >= 2:
                            pr.chunk_stats(dve, q, j - 2, step)
                    for j in (NCH - 2, NCH - 1):
                        dve.wait_ge(finished, NCH * q + j + 1)
                        pr.chunk_stats(dve, q, j, step)
                    pr.group_stats(dve, q, step)

            @block.gpsimd
            def _(pool):
                with pool.Fori(0, Q) as q:
                    for j in range(NCH):
                        pool.wait_ge(scaled, NCH * q + j + 1)
                        pool.wait_ge(added, START + NCH * q + j + 1)
                        x = pr.X[:, q, j * CH:(j + 1) * CH].rearrange("p (y a x) -> p a y x", y=PS, x=PS)
                        pool.tensor_tensor(x, x, tmp[j % 2][:].rearrange("p a (y x) -> p a y x", x=PS),
                                           ALU.add).then_inc(finished, 1)


class Filter5:

    def __init__(self, pr, ctx):
        self.pr = pr
        self.raw = pr.sb(ctx, "c2_raw", [P, C, KS * KS])
        self.high, self.low = (pr.sb(ctx, f"c2_{n}", [P, 3, 3, 4, C], F16) for n in ("w_high", "w_low"))
        self.largest = pr.sb(ctx, "c2_largest", [P, 1])
        self.top = pr.sb(ctx, "c2_top", [1, 1])
        self.ones = pr.sb(ctx, "c2_ones", [1, P])
        self.power = pr.sb(ctx, "c2_power", [P, 4])
        self.loaded, self.found, self.spread = (pr.sem(f"c2_{n}") for n in (
            "w_loaded", "w_found", "w_spread"))

    def load(self, sp):
        w = self.pr.ins["L2_conv_weight"].rearrange("o c y x -> c o (y x)")
        for i in range(4):
            sp.dma_start(self.raw[i * C:(i + 1) * C], w).then_inc(self.loaded, 16)

    def clear(self, dve):
        dve.memset(self.ones[:], 1.0)
        dve.memset(self.high[:], 0.0)
        dve.memset(self.low[:], 0.0)

    def find_largest(self, dve):
        dve.wait_ge(self.loaded, 64)
        dve.tensor_reduce(self.largest[:], self.raw[:].rearrange("p o y -> p (o y)"), AX.X, ALU.max,
                          apply_absolute_value=True)

    def spread_largest(self, pe):
        bank = self.pr.psum[7]
        pe.transpose(bank[0:1, 0:P], self.largest[:], self.pr.ident[:]).then_inc(self.spread, 1)
        pe.wait_ge(self.found, 1)
        pe.matmul(bank[:, P:P + 1], self.ones[:], self.top[:], start=True, stop=True).then_inc(self.spread, 1)
        pe.wait_ge(self.found, 2)

    def find_power(self, dve):
        bank, power = self.pr.psum[7], self.power
        dve.wait_ge(self.spread, 1)
        dve.tensor_reduce(self.top[:], bank[0:1, 0:P], AX.X, ALU.max).then_inc(self.found, 1)
        dve.wait_ge(self.spread, 2)
        dve.tensor_scalar(power[:, 0:1], bank[:, P:P + 1], 2.0 ** -100, 2.0 ** 100, ALU.max, ALU.min
                          ).then_inc(self.found, 1)
        dve.wait_ge(self.found, 2)
        dve.tensor_scalar(power[:, 1:2].bitcast(I32), power[:, 0:1].bitcast(I32), 0x7F800000, None,
                          ALU.bitwise_and).then_inc(self.found, 1)
        dve.wait_ge(self.found, 3)
        dve.tensor_scalar(power[:, 2:3], power[:, 1:2], 1.0 / (W_UP * X_UP), None, ALU.mult)
        dve.reciprocal(power[:, 3:4], power[:, 1:2])

    def lay_out(self, dve, scaled, parts, seq):
        flat = "p o y -> p (o y)"
        dve.tensor_scalar(scaled[:].rearrange(flat), self.raw[:].rearrange(flat), self.power[:, 3:4], W_UP,
                          ALU.mult, ALU.mult).then_inc(seq, 1)
        dve.wait_ge(seq, 1)
        dve.tensor_copy(parts[0][:].rearrange(flat), scaled[:].rearrange(flat)).then_inc(seq, 1)
        dve.wait_ge(seq, 2)
        dve.tensor_tensor(parts[1][:].rearrange(flat), scaled[:].rearrange(flat), parts[0][:].rearrange(flat),
                          ALU.subtract).then_inc(seq, 1)
        dve.wait_ge(seq, 3)

        def taps(d):
            k = [k for k in range(3) if 0 <= d + 2 * k < KS]
            return slice(k[0], k[-1] + 1), slice(d + 2 * k[0], d + 2 * k[-1] + 1, 2)

        for to, of in zip((self.high, self.low), parts):
            for ry, cx, oy, ox in np.ndindex(2, 2, 2, 2):
                at = slice((2 * ry + cx) * C, (2 * ry + cx + 1) * C)
                (ky, jy), (kx, jx) = taps(oy - ry), taps(ox - cx)
                dve.tensor_copy(to[at, ky, kx, 2 * oy + ox, :],
                                of[at].rearrange("c o (y x) -> c y x o", x=KS)[:, jy, jx, :])


def l2_stage(pr, filt):
    nc, ps = pr.nc, pr.psum
    ready, padded, high, low = ([pr.sem(f"c2_{n}{b}") for b in range(IB)] for n in ("ready", "padded", "high", "low"))
    conv, added, step, scales = (pr.sem(f"c2_{n}") for n in ("conv", "added", "step", "scales"))
    HALF = CH // HN
    TILES = IB * HN // HALF
    PADS = 9
    with ExitStack() as ctx:
        R = pr.sb(ctx, "c2_r", [P, IB, HP, HP])
        rh, rl = (pr.sb(ctx, f"c2_{n}", [P, Q, IB, HP, HP], F16) for n in ("rh", "rl"))
        nrm = pr.sb(ctx, "c2_nrm", [P, 2, Q])
        with nc.Block() as block:
            def parity(q, b, p):
                ry, cx = p // 2, p % 2
                return (R[p * C:(p + 1) * C, b, 1 - ry:1 - ry + HN, 1 - cx:1 - cx + HN],
                        pr.X[b * C:(b + 1) * C, q, :].rearrange("p (y r x s) -> p y r x s", r=2, x=HN, s=2)[
                            :, :, 1 - ry, :, 1 - cx])

            def pad(eng, copy, q, b):
                eng.wait_ge(ready[b], 4 * q + 4)
                for p in range(4):
                    at, ry = slice(p * C, (p + 1) * C), p // 2
                    I = R[at, b, 1 - ry:1 - ry + HN]
                    for to, of in ((slice(0, HP, HP - 1), slice(1, HP - 2, HP - 4)),) if p % 2 == 0 else (
                            (slice(HP - 2, HP - 1), slice(HP - 3, HP - 2)), (slice(HP - 1, HP), slice(1, 2))):
                        copy(I[:, :, to], I[:, :, of]).then_inc(padded[b], 1)
                eng.wait_ge(padded[b], PADS * q + 6)
                even, odd = R[0:2 * C, b], R[2 * C:P, b]
                copy(even[:, 0:HP:HP - 1, :], even[:, 1:HP - 2:HP - 4, :]).then_inc(padded[b], 1)
                copy(odd[:, HP - 2, :], odd[:, HP - 3, :]).then_inc(padded[b], 1)
                copy(odd[:, HP - 1, :], odd[:, 1, :]).then_inc(padded[b], 1)

            def low_part(eng, q, b):
                eng.wait_ge(high[b], q + 1)
                eng.tensor_tensor(rl[:, q, b].rearrange("p k w -> p (k w)"), R[:, b].rearrange("p k w -> p (k w)"),
                                  rh[:, q, b].rearrange("p k w -> p (k w)"), ALU.subtract).then_inc(low[b], 1)

            @block.scalar
            def _(act):
                act.wait_ge(scales, 1)

                def group(q, pads):
                    def normalise(b):
                        at = slice(b * C, (b + 1) * C)
                        act.wait_ge(low[b], START + q)
                        for p in range(4 if pads else 2):
                            to, of = parity(q, b, p)
                            act.activation(to, of, ACT.Identity, scale=nrm[at, 0, bass.ds(q, 1)],
                                           bias=nrm[at, 1, bass.ds(q, 1)]).then_inc(ready[b], 1)

                    normalise(0)
                    if pads:
                        normalise(1)
                    for b in range(IB):
                        if b == 1 and not pads:
                            normalise(1)
                        if 0 < b < IB - 1:
                            normalise(b + 1)
                        if pads:
                            pad(act, act.copy, q, b)
                        act.wait_ge(padded[b], PADS * q + PADS)
                        act.copy(rh[:, q, b].rearrange("p k w -> p (k w)"), R[:, b].rearrange("p k w -> p (k w)")
                                 ).then_inc(high[b], 1)

                group(0, False)
                with act.Fori(1, Q) as q:
                    group(q, True)

            @block.gpsimd
            def _(pool):
                for b in range(IB):
                    pool.sem_inc(low[b], START)
                with pool.Fori(1, Q) as q:
                    for b in range(IB):
                        low_part(pool, q, b)

            @block.tensor
            def _(pe):
                pr.keep_warm(pe, 26)
                with pe.Fori(0, Q) as q:
                    for n in range(TILES):
                        b, half = n % IB, n // IB
                        pe.wait_ge(low[b], START + q + 1)
                        pe.wait_ge(added, START + 32 * q + 4 * n - 28)
                        terms = [(ky, kx, w, d) for ky in range(3) for kx in range(3)
                                 for w, d in ((filt.high, rh), (filt.high, rl), (filt.low, rh))]
                        for i, (ky, kx, w, d) in enumerate(terms):
                            y, x = HALF * half + 2 - ky, 2 - kx
                            m = pe.matmul(ps[n][:], w[:, ky, kx].rearrange("p o c -> p (o c)"),
                                          d[:, q, b, y:y + HALF, x:x + HN], start=i == 0, stop=i == len(terms) - 1)
                        m.then_inc(conv, 1)

            @block.vector
            def _(dve):
                dve.sem_inc(added, START)
                dve.tensor_scalar(nrm[:, 0, :], pr.rstd[:], X_UP, None, ALU.mult)
                dve.tensor_scalar(nrm[:, 1, :], pr.shift[:], X_UP, None, ALU.mult).then_inc(scales, 1)
                dve.wait_ge(scales, 1)
                for b in range(IB):
                    at = slice(b * C, (b + 1) * C)
                    for p in range(2, 4):
                        to, of = parity(0, b, p)
                        dve.tensor_scalar(to, of, nrm[at, 0, 0:1], nrm[at, 1, 0:1], ALU.mult, ALU.add
                                          ).then_inc(ready[b], 1)
                    pad(dve, dve.tensor_copy, 0, b)
                    low_part(dve, 0, b)
                with dve.Fori(0, Q) as q:
                    for n in range(TILES):
                        b, half = n % IB, n // IB
                        if n == IB + 1:
                            dve.wait_ge(added, START + 32 * q + 16)
                            pr.chunk_stats(dve, q, 0, step)
                        if n > IB:
                            pr.chunk_stats(dve, q, n - IB, step)
                        dve.wait_ge(conv, TILES * q + n + 1)
                        at = slice(b * C, (b + 1) * C)
                        for oy, ox in np.ndindex(2, 2):
                            o = 2 * oy + ox
                            x = pr.X[at, q, :].rearrange("p (y r x s) -> p y r x s", r=2, x=HN, s=2)[
                                :, HALF * half:HALF * half + HALF, oy, :, ox]
                            dve.scalar_tensor_tensor(x, ps[n][o * C:(o + 1) * C, :].rearrange("p (y x) -> p y x", x=HN),
                                                     filt.power[at, 2:3], x, ALU.mult, ALU.add).then_inc(added, 1)
                    dve.wait_ge(added, START + 32 * q + 32)
                    for c in range(NCH // 2, NCH):
                        pr.chunk_stats(dve, q, c, step)
                    pr.group_stats(dve, q, step)


def l3_forward_stage(pr, mats, xm, kf0, loaded0):
    with ExitStack() as ctx:
        fwd = Forward(pr, ctx, "f3", mats, SLOT_AT, True, {2: 0, 4: 1, 6: 2, 8: 3}, {9: 4, 10: 5, 12: 6, 14: 7})
        with pr.nc.Block() as block:
            @block.sync
            def _(sp):
                load_kernel_spectra(sp, pr, kf0, 0, 0, loaded0)

            @block.tensor
            def _(pe):
                fwd.products(pe)

            @block.vector
            def _(dve):
                fwd.low_parts(dve)

            @block.scalar
            def _(act):
                fwd.high_parts(act, lambda q, s: act.copy(
                    xm[:, s, :, :, bass.ds(IB * q, IB)].rearrange("p k r b -> p b r k"),
                    pr.psum[4 + s % 4][:].rearrange("p (b r k) -> p b r k", b=IB, r=2)))


def load_kernel_spectra(sp, pr, to, i, pair, loaded):
    for s2 in range(2):
        for part in range(2):
            at = (2 * s2 + part) * C
            sp.dma_start(to[at:at + C].rearrange("c j o k -> c j (o k)"),
                         pr.kf[2 * i + s2, pair * 2 * C:(pair + 1) * 2 * C, part].rearrange(
                             "(j c) t n -> c j (t n)", j=2)).then_inc(loaded, 16)


def l3_mix_stage(pr, xm, kf0, loaded):
    nc, ps = pr.nc, pr.psum
    PAIRS = SLOT // 8
    staged, mixed, mixed_read, fix, zeroed = (pr.sem(f"m3_{n}") for n in
                                              ("staged", "mixed", "mixed_read", "fix", "zeroed"))
    H = N // 2
    with ExitStack() as ctx:
        kf = [kf0, pr.sb(ctx, "m3_kf1", [P, 2, C, N])]
        xp = [pr.sb(ctx, f"m3_xp{p}", [P, 2, H, 2, 2 * B]) for p in range(2)]
        with nc.Block() as block:
            @block.sync
            def _(sp):
                load_kernel_spectra(sp, pr, kf[1], 0, 1, loaded[1])
                with sp.Fori(1, PAIRS) as i:
                    for p in range(2):
                        sp.wait_ge(mixed, START + 4 * i + 2 * p - 2)
                        load_kernel_spectra(sp, pr, kf[p], i, p, loaded[p])

            def stage(dve, i, p, half, quadrants=(0, 1)):
                for j in quadrants:
                    for s2 in range(2):
                        of = xm[(2 * p + j) * C:(2 * p + j + 1) * C, 2 * i + s2, H * half:H * half + H]
                        re = xp[half][2 * s2 * C:(2 * s2 + 1) * C, j, :, s2]
                        im = xp[half][(2 * s2 + 1) * C:(2 * s2 + 2) * C, j, :, s2]
                        dve.tensor_copy(re, of.rearrange("p k r b -> p k (r b)"))
                        dve.tensor_copy(im[:, :, B:2 * B], of[:, :, 0, :])
                        last = dve.tensor_scalar(im[:, :, 0:B], of[:, :, 1, :], -1.0, None, ALU.mult)
                return last

            @block.vector
            def _(dve):
                for half in range(2):
                    if half == 1:
                        dve.memset(xp[1][0:2 * C, :, :, 1], 0.0)
                        dve.memset(xp[1][2 * C:P, :, :, 0], 0.0)
                    stage(dve, 0, 0, half, (0,)).then_inc(fix, 1)
                    dve.wait_ge(fix, 3 * half + 1)
                    dve.memset(xp[half][0:C, 0, 0, 0, B:2 * B], 0.0).then_inc(fix, 1)
                    dve.memset(xp[half][C:2 * C, 0, 0, 0, 0:B], 0.0).then_inc(fix, 1)
                    dve.tensor_copy(xp[half][C:2 * C, 0, 0, 0, B:2 * B], xm[0:C, 0, H * half, 1, :]).then_inc(staged, 1)
                    stage(dve, 0, 0, half, (1,)).then_inc(staged, 1)
                for half in range(2):
                    dve.wait_ge(mixed, START + half + 1)
                    stage(dve, 0, 1, half).then_inc(staged, 2)
                with dve.Fori(1, PAIRS) as i:
                    for p in range(2):
                        for half in range(2):
                            dve.wait_ge(mixed, START + 4 * i + 2 * p + half - 1)
                            stage(dve, i, p, half).then_inc(staged, 2)

            @block.gpsimd
            def _(pool):
                pool.memset(xp[0][0:2 * C, :, :, 1], 0.0).then_inc(zeroed, 1)
                pool.memset(xp[0][2 * C:P, :, :, 0], 0.0).then_inc(zeroed, 1)

            @block.tensor
            def _(pe):
                pe.sem_inc(mixed, START)
                pr.keep_warm(pe, 16)
                pe.wait_ge(zeroed, 2)
                with pe.Fori(0, PAIRS) as i:
                    for p in range(2):
                        pe.wait_ge(loaded[p], 64 * i + 64)
                        for half in range(2):
                            pe.wait_ge(mixed_read, START + 4 * i + 2 * p + half - 1)
                            for j in range(2):
                                pe.wait_ge(staged, 8 * i + 4 * p + 2 * half + j + 1)
                                pe.sem_inc(pr.pace, 1)
                                for m in range(H):
                                    at = (2 * p + j) * C
                                    last = pe.matmul(ps[4 * half + m // 8][at:at + C, m % 8 * N:(m % 8 + 1) * N],
                                                     kf[p][:, j, :, H * half + m],
                                                     xp[half][:, j, m].rearrange("p s n -> p (s n)"),
                                                     start=True, stop=True)
                            last.then_inc(mixed, 1)

            @block.scalar
            def _(act):
                act.sem_inc(mixed_read, START)
                with act.Fori(0, PAIRS) as i:
                    for p in range(2):
                        for half in range(2):
                            act.wait_ge(mixed, START + 4 * i + 2 * p + half + 1)
                            for m in range(4):
                                at = slice(p * 2 * C, (p + 1) * 2 * C)
                                k = H * half + 8 * m
                                c = act.copy(xm[at, bass.ds(2 * i, 2), k:k + 8].rearrange("p s k r b -> p k s (r b)"),
                                             ps[4 * half + m][at, :].rearrange("p (k s n) -> p k s n", s=2, n=2 * B))
                            c.then_inc(mixed_read, 1)


def matrices(pr, ctx, shapes, dt=F32):
    tiles = [pr.sb(ctx, f"c_{n}", shape, dt) for n, shape in shapes]
    return tiles, [(t, n) for t, (n, _) in zip(tiles, shapes)]


def four_layers(nc, ins, out, stop=None):
    with ExitStack() as ctx:
        pr = Program(nc, ctx, ins, out)
        with ExitStack() as first:
            filt = Filter5(pr, first)
            with ExitStack() as layer:
                fwd, fwd_loads = matrices(pr, layer, [("l0_fw", [P, 2, 4 * KT]), ("l0_fh", [P, 2, 2 * KX])], F16)
                inv, inv_loads = matrices(pr, layer, [("l0_ih", [P, P]), ("l0_iw", [P, 4 * N])])
                kernel_spectra_stage(pr, fwd_loads + inv_loads, filt)
                pr.stats_stage("n0")
                y = pr.sb(layer, "l0_y", [P, KT // 4, P // 4, 2, B])
                with ExitStack() as inner:
                    w_loaded, xb_loaded = pr.sem("l0_weights"), pr.sem("l0_xb_loaded")
                    xb = pr.sb(inner, "l0_xb", [P, 2, Q, KT, K2, 2, IB])
                    wb = pr.sb(inner, "l0_wb", [P, 2, C, K2, KT])
                    l0_forward_stage(pr, filt, (*fwd, None), xb, wb, w_loaded, xb_loaded)
                    l0_mix_stage(pr, filt, xb, wb, w_loaded, xb_loaded, y)
                inverse_stage(pr, "i0", y, KT, P // 4, (inv[0], inv[0], inv[1]), 4, False)
            if stop == 0: return dump(pr)
            with ExitStack() as layer:
                edge = pr.sb(layer, "edge", [P, Q, N])
                mm = pr.sb(layer, "mm", [P, 2, P])
                tables, table_loads = matrices(pr, layer, [("l1_dft", [P, P]), ("l1_same", [P, P]),
                                                           ("l1_band", [NB, P]), ("l1_high", [P, 1])])
                means, mean_loads = matrices(pr, layer, [("l1_mean", [P, 264]), ("l1_pick", [P, P]),
                                                         ("l1_spread", [B, Q * P])])
                pr.stats_stage("n1", mean_loads + table_loads)
                l1_edge_stage(pr, means, tables, edge, mm)
                l1_filter_stage(pr, mm, edge)
            if stop == 1: return dump(pr)
            pr.stats_stage("n2")
            l2_stage(pr, filt)
        if stop == 2: return dump(pr)
        with ExitStack() as layer:
            xm = pr.sb(layer, "xm", [P, SLOT // 4, N, 2, B])
            inv, inv_loads = matrices(pr, layer, [("l3_ih", [P, P]), ("l3_ih0", [P, P]), ("l3_iw", [P, P])])
            with ExitStack() as inner:
                kf0 = pr.sb(inner, "m3_kf0", [P, 2, C, N])
                loaded = [pr.sem(f"m3_load{p}") for p in range(2)]
                fwd, fwd_loads = matrices(pr, inner, [(n, [P, 2, P]) for n in ("l3_fw16", "l3_fh16", "l3_fh016")], F16)
                pr.stats_stage("n3", fwd_loads + inv_loads)
                l3_forward_stage(pr, fwd, xm, kf0, loaded[0])
                l3_mix_stage(pr, xm, kf0, loaded)
            inverse_stage(pr, "i3", xm, SLOT, N, inv, 2, True)


def dump(pr):
    s = pr.sem("dump")
    with pr.nc.Block() as block:
        @block.sync
        def _(sp):
            og = pr.out.rearrange("(q b) c h w -> q (b c) (h w)", b=IB)
            for q in range(Q):
                sp.dma_start(og[q], pr.X[:, q, :]).then_inc(s, 16)
            sp.wait_ge(s, 64)


_INS = ["x", "L0_conv_weights_r", "L0_conv_weights_i", "L1_conv_gain", "L2_conv_weight", "L3_conv_weights"]


def kernel(**inputs):
    import concourse.bacc as bacc
    from concourse.bass_utils import run_bass_kernel_spmd

    nc = bacc.Bacc("TRN2", target_bir_lowering=False, num_devices=1)
    arrays = {n: np.ascontiguousarray(inputs[n]) for n in _INS} | constants()
    ins = {n: nc.dram_tensor(f"in_{n}", a.shape, F16 if a.dtype == np.float16 else F32, kind="ExternalInput").ap()
           for n, a in arrays.items()}
    out = nc.dram_tensor("out_y", (B, C, N, N), F32, kind="ExternalOutput").ap()
    four_layers(nc, ins, out)
    r = run_bass_kernel_spmd(nc, [{f"in_{n}": a for n, a in arrays.items()}], core_ids=[0])
    return r.results[0]["out_y"]
```
